# Optimizing a Trainium2 kernel written in Bass

```python
import numpy as np
import jax
import jax.numpy as jnp

def _softmax(x, axis=-1):
    return jax.nn.softmax(x, axis=axis)

def _gelu(x):
    return jax.nn.gelu(x, approximate=True)

def _silu(x):
    return jax.nn.silu(x)

def _sigmoid(x):
    return jax.nn.sigmoid(x)

def _layernorm(x, axis=-1, eps=1e-05):
    m = jnp.mean(x, axis=axis, keepdims=True)
    v = jnp.var(x, axis=axis, keepdims=True)
    return (x - m) / jnp.sqrt(v + eps)

def _scatter_add(tgt, idx, src, axis=0):
    return tgt.at[idx].add(src)

def _segment_sum(src, seg, n):
    return jax.ops.segment_sum(src, seg, n)
kernel_name = 'mk_gnn_ffn_d1_gnn_r64_3801ab'

def setup_inputs(seed: int=0):
    np.random.seed(seed)
    _w = jnp.asarray

    def _rec_inputs():
        import jax
        import jax.numpy as jnp
        _gk = jax.random.key(seed)
        x = -0.0003713 + 1 * jax.random.normal(jax.random.fold_in(_gk, 1), (50000, 256), jnp.float32)
        _s = jax.random.randint(jax.random.fold_in(_gk, 2), (12500,), 0, 50000, jnp.int32)
        _d = jax.random.randint(jax.random.fold_in(_gk, 3), (12500,), 0, 50000, jnp.int32)
        _loop = jnp.arange(50000, dtype=jnp.int32)
        src = jnp.concatenate([_s, _d, _loop])
        dst = jnp.concatenate([_d, _s, _loop])
        _o = jnp.argsort(dst, stable=True)
        src = src[_o]
        dst = dst[_o]
        return (x, src, dst)
    x, src, dst = _rec_inputs()

    def _L0_gnn_setup():
        import jax, jax.numpy as jnp
        import numpy as np
        N = 50000
        E = 12500
        DIN = 256
        DH = 256
        DOUT = 256

        def _gcn_norm(row, col, n):
            ones = jnp.ones(row.shape[0], jnp.float32)
            deg = jax.ops.segment_sum(ones, row, num_segments=n)
            dinv = jnp.where(deg > 0, deg ** (-0.5), 0.0)
            val = dinv[row]
            cdeg = jax.ops.segment_sum(val, col, num_segments=n)
            cinv = jnp.where(cdeg > 0, cdeg ** (-0.5), 0.0)
            return val * cinv[col]

        def _gcn_conv(x, W, b, row, col, val, n):
            h = x @ W
            msg = val[:, None] * h[col]
            out = jax.ops.segment_sum(msg, row, num_segments=n)
            return out + b
        key = jax.random.key(seed)
        ks = jax.random.split(key, 8)
        x = jax.random.normal(ks[0], (N, DIN), dtype=jnp.float32)
        edge_index = jax.random.randint(ks[1], (2, E), 0, N, dtype=jnp.int32)

        def glorot(k, fan_in, fan_out):
            return jax.random.normal(k, (fan_in, fan_out), dtype=jnp.float32) * np.float32(1.0 / np.sqrt(fan_in))
        return {'x': x, 'W0': glorot(ks[2], DIN, DH), 'b0': jnp.zeros((DH,), jnp.float32), 'W1': glorot(ks[3], DH, DH), 'b1': jnp.zeros((DH,), jnp.float32), 'W2': glorot(ks[4], DH, DOUT), 'b2': jnp.zeros((DOUT,), jnp.float32), 'edge_index': edge_index}
    _L0_gnn_all = _L0_gnn_setup()
    _L0_gnn_in = {k: v for k, v in _L0_gnn_all.items() if k in ('W0', 'b0', 'W1', 'b1', 'W2', 'b2')}
    del _L0_gnn_all

    def _L0_ffn_setup():
        import jax, jax.numpy as jnp
        import numpy as np
        DIM = 256
        H = 8
        D = 64
        G = 64
        INNER = H * D
        SCALE = D ** (-0.5)
        key = jax.random.key(seed)
        ks = jax.random.split(key, 12)
        B, N = (4, 256)
        x = jax.random.normal(ks[0], (B, N, DIM), dtype=jnp.float32)
        s = lambda fan_in: 1.0 / np.sqrt(fan_in)
        W_fx = jax.random.normal(ks[1], (DIM, INNER), dtype=jnp.float32) * s(DIM)
        b_fx = jnp.zeros((INNER,), dtype=jnp.float32)
        W_x = jax.random.normal(ks[2], (DIM, INNER), dtype=jnp.float32) * s(DIM)
        b_x = jnp.zeros((INNER,), dtype=jnp.float32)
        A = jax.random.normal(ks[3], (G, D), dtype=jnp.float32)
        Q, _ = jnp.linalg.qr(A.T)
        W_slice = Q[:, :G].astype(jnp.float32)
        b_slice = jnp.zeros((G,), dtype=jnp.float32)
        W_q = jax.random.normal(ks[4], (D, D), dtype=jnp.float32) * s(D)
        W_k = jax.random.normal(ks[5], (D, D), dtype=jnp.float32) * s(D)
        W_v = jax.random.normal(ks[6], (D, D), dtype=jnp.float32) * s(D)
        W_out = jax.random.normal(ks[7], (INNER, DIM), dtype=jnp.float32) * s(INNER)
        b_out = jnp.zeros((DIM,), dtype=jnp.float32)
        temperature = jnp.ones((1, H, 1, 1), dtype=jnp.float32) * 0.5
        return {'x': x, 'W_fx': W_fx, 'b_fx': b_fx, 'W_x': W_x, 'b_x': b_x, 'W_slice': W_slice, 'b_slice': b_slice, 'W_q': W_q, 'W_k': W_k, 'W_v': W_v, 'W_out': W_out, 'b_out': b_out, 'temperature': temperature}
    _L0_ffn_all = _L0_ffn_setup()
    _L0_ffn_in = {k: v for k, v in _L0_ffn_all.items() if k in ('W_fx', 'b_fx', 'W_x', 'b_x', 'W_slice', 'b_slice', 'W_q', 'W_k', 'W_v', 'W_out', 'b_out', 'temperature')}
    del _L0_ffn_all
    return {'x': x, 'src': src, 'dst': dst, 'L0_gnn_W0': _L0_gnn_in['W0'], 'L0_gnn_b0': _L0_gnn_in['b0'], 'L0_gnn_W1': _L0_gnn_in['W1'], 'L0_gnn_b1': _L0_gnn_in['b1'], 'L0_gnn_W2': _L0_gnn_in['W2'], 'L0_gnn_b2': _L0_gnn_in['b2'], 'L0_ffn_W_fx': _L0_ffn_in['W_fx'], 'L0_ffn_b_fx': _L0_ffn_in['b_fx'], 'L0_ffn_W_x': _L0_ffn_in['W_x'], 'L0_ffn_b_x': _L0_ffn_in['b_x'], 'L0_ffn_W_slice': _L0_ffn_in['W_slice'], 'L0_ffn_b_slice': _L0_ffn_in['b_slice'], 'L0_ffn_W_q': _L0_ffn_in['W_q'], 'L0_ffn_W_k': _L0_ffn_in['W_k'], 'L0_ffn_W_v': _L0_ffn_in['W_v'], 'L0_ffn_W_out': _L0_ffn_in['W_out'], 'L0_ffn_b_out': _L0_ffn_in['b_out'], 'L0_ffn_temperature': _L0_ffn_in['temperature']}

def reference(x, src, dst, L0_gnn_W0, L0_gnn_b0, L0_gnn_W1, L0_gnn_b1, L0_gnn_W2, L0_gnn_b2, L0_ffn_W_fx, L0_ffn_b_fx, L0_ffn_W_x, L0_ffn_b_x, L0_ffn_W_slice, L0_ffn_b_slice, L0_ffn_W_q, L0_ffn_W_k, L0_ffn_W_v, L0_ffn_W_out, L0_ffn_b_out, L0_ffn_temperature):
    import jax
    import jax.numpy as jnp

    def _L0_gnn_ref(x, W0, b0, W1, b1, W2, b2, edge_index):
        import jax, jax.numpy as jnp
        import numpy as np
        N = 50000
        E = 12500
        DIN = 256
        DH = 256
        DOUT = 256

        def _gcn_norm(row, col, n):
            ones = jnp.ones(row.shape[0], jnp.float32)
            deg = jax.ops.segment_sum(ones, row, num_segments=n)
            dinv = jnp.where(deg > 0, deg ** (-0.5), 0.0)
            val = dinv[row]
            cdeg = jax.ops.segment_sum(val, col, num_segments=n)
            cinv = jnp.where(cdeg > 0, cdeg ** (-0.5), 0.0)
            return val * cinv[col]

        def _gcn_conv(x, W, b, row, col, val, n):
            h = x @ W
            msg = val[:, None] * h[col]
            out = jax.ops.segment_sum(msg, row, num_segments=n)
            return out + b
        row, col = (edge_index[0], edge_index[1])
        n = x.shape[0]
        for W, b in ((W0, b0), (W1, b1), (W2, b2)):
            val = _gcn_norm(row, col, n)
            x = jax.nn.relu(_gcn_conv(x, W, b, row, col, val, n))
        return x

    def _L0_ffn_ref(x, W_fx, b_fx, W_x, b_x, W_slice, b_slice, W_q, W_k, W_v, W_out, b_out, temperature):
        import jax, jax.numpy as jnp
        import numpy as np
        DIM = 256
        H = 8
        D = 64
        G = 64
        INNER = H * D
        SCALE = D ** (-0.5)
        B, N, _ = x.shape
        fx_mid = (x @ W_fx + b_fx).reshape(B, N, H, D).transpose(0, 2, 1, 3)
        x_mid = (x @ W_x + b_x).reshape(B, N, H, D).transpose(0, 2, 1, 3)
        temp = jnp.clip(temperature, 0.1, 5.0)
        slice_weights = jax.nn.softmax((x_mid @ W_slice + b_slice) / temp, axis=-1)
        slice_norm = slice_weights.sum(axis=2)
        slice_token = jnp.einsum('bhnc,bhng->bhgc', fx_mid, slice_weights)
        slice_token = slice_token / (slice_norm[..., None] + 1e-05)
        q = slice_token @ W_q
        k = slice_token @ W_k
        v = slice_token @ W_v
        attn = jax.nn.softmax(jnp.einsum('bhgc,bhkc->bhgk', q, k) * SCALE, axis=-1)
        out_slice = jnp.einsum('bhgk,bhkc->bhgc', attn, v)
        out_x = jnp.einsum('bhgc,bhng->bhnc', out_slice, slice_weights)
        out_x = out_x.transpose(0, 2, 1, 3).reshape(B, N, INNER)
        return out_x @ W_out + b_out
    edge_index = jnp.stack([src, dst])
    x = x + _L0_gnn_ref(_layernorm(x, axis=-1), L0_gnn_W0, L0_gnn_b0, L0_gnn_W1, L0_gnn_b1, L0_gnn_W2, L0_gnn_b2, edge_index)
    x = x + _L0_ffn_ref(_layernorm(x, axis=-1)[None], L0_ffn_W_fx, L0_ffn_b_fx, L0_ffn_W_x, L0_ffn_b_x, L0_ffn_W_slice, L0_ffn_b_slice, L0_ffn_W_q, L0_ffn_W_k, L0_ffn_W_v, L0_ffn_W_out, L0_ffn_b_out, L0_ffn_temperature)[0]
    return x

_drawn_inputs = setup_inputs


def setup_inputs(seed=0):
    import zlib

    import numpy as np

    out = dict(_drawn_inputs(seed))
    spreads = {'L0_gnn_b0': (0.0, 0.1),
     'L0_gnn_b1': (0.0, 0.1),
     'L0_gnn_b2': (0.0, 0.1),
     'L0_ffn_b_fx': (0.0, 0.1),
     'L0_ffn_b_x': (0.0, 0.8),
     'L0_ffn_b_slice': (0.0, 0.8),
     'L0_ffn_b_out': (0.0, 0.1),
     'L0_ffn_temperature': (0.5, 0.6)}
    factors = {'L0_ffn_W_x': 8.0, 'L0_ffn_W_slice': 8.0, 'L0_ffn_W_q': 8.0, 'L0_ffn_W_k': 8.0}
    for name, (base, spread) in spreads.items():
        noise = np.random.default_rng([zlib.crc32(name.encode()), seed]).standard_normal(out[name].shape)
        drawn = base * np.exp(spread * noise) if base else spread * noise
        out[name] = jnp.asarray(drawn.astype(out[name].dtype))
    for name, factor in factors.items():
        out[name] = (out[name] * factor).astype(out[name].dtype)
    return out
```

```python
import concourse.bass as bass
from concourse import mybir
from contextlib import ExitStack

P = 128
FP32 = mybir.dt.float32
FP16 = mybir.dt.float16
I32 = mybir.dt.int32
ALU = mybir.AluOpType
ACT = mybir.ActivationFunctionType
AX = mybir.AxisListType
BANK = 512
PAD = 1 << 16
EPS = 1e-5


class Turn:

    def __init__(self, g, at, unroll, end):
        self.g, self.at, self.unroll, self.end = g, at, unroll, end
        self.n = at if g is None else g * unroll + at

    def plus(self, d):
        return Turn(self.g, self.at + d, self.unroll, self.end)

    def slot(self, buffers):
        return self.at % buffers

    def uses(self, buffers):
        before = self.at // buffers
        return before if self.g is None else self.g * (self.unroll // buffers) + before

    def reused(self, buffers):
        return self.at >= buffers

    def later(self, d):
        return self.g is not None or self.at + d < self.end


BUFFERS = 4


def steps(eng, lo, hi, unroll, tail=0, end=None):
    end = hi if end is None else end
    for n in range(lo, min(BUFFERS, hi)):
        yield Turn(None, n, unroll, end)
    lo = min(max(lo, BUFFERS), hi)
    rounds = max(hi - lo - tail, 0) // unroll
    if rounds > 1:
        with eng.Fori(0, rounds) as g:
            for u in range(unroll):
                yield Turn(g, lo + u, unroll, end)
    else:
        rounds = 0
    for n in range(lo + rounds * unroll, hi):
        yield Turn(None, n, unroll, end)


class Chain:

    def __init__(self, eng, sem):
        self.eng, self.sem, self.base, self.count = eng, sem, 0, 0

    def at(self, base):
        self.base, self.count = base, 0

    def link(self, ins):
        self.mark(ins)
        self.wait()

    def mark(self, ins):
        self.count += 1
        ins.then_inc(self.sem, 1)

    def wait(self):
        self.eng.wait_ge(self.sem, self.base + self.count)


class Phase(ExitStack):

    count = 0

    def __init__(self, nc):
        super().__init__()
        self.nc, self.semaphores = nc, []
        Phase.count += 1
        self.number = Phase.count
        self.passed = nc.alloc_semaphore(f"passed_{self.number}")
        self.semaphores.append(self.passed)

    def __exit__(self, *error):
        done = super().__exit__(*error)
        if error[0] is None:
            self.nc.clear_and_free_semaphores(self.semaphores)
            self.nc.all_engine_barrier()
        return done


def wait_apart(eng, sem, value, passed):
    eng.wait_ge(sem, value)
    eng.sem_inc(passed, 1)


def spread(ap, shape_ap):
    return bass.AP(ap.tensor, ap.offset, [[0, P]] + list(shape_ap))


def gnn_ffn(nc, x, src, dst, gw, gb, W_fx, b_fx, W_x, b_x, W_slice, b_slice, W_q, W_k, W_v,
            W_out, b_out, temperature, out):
    Phase.count = 0
    N, D = x.shape
    E = src.shape[0]
    NT = -(-N // P)
    NP = NT * P
    LAST = N - (NT - 1) * P
    FC = D // P
    INNER = W_fx.shape[1]
    H = temperature.shape[1]
    C = INNER // H
    IC = INNER // P
    KE = -(-E // P)
    KE += -KE % 4
    EFULL, EREST = E // KE, E % KE
    LAYERS = len(gw)
    SCALE = float(C) ** -0.5
    assert D == 256 and C == 64 and INNER == 512 and NT <= 391 + 120 and NT > 12

    tables = [nc.dram_tensor(f"features_{l}", (NP, D), FP32).ap() for l in range(LAYERS)]
    node_sums = nc.dram_tensor("node_sums", (NP + P, D), FP32).ap()
    x2_dram = nc.dram_tensor("x2_rows", (NP, D), FP32).ap()
    w_dram = nc.dram_tensor("slice_weights", (NP, INNER), FP32).ap()
    dinv_dram = nc.dram_tensor("dinv_rows", (NP, 1), FP32).ap()
    cinv_dram = nc.dram_tensor("cinv_rows", (NP, 1), FP32).ap()

    def rows(ap, t, count=P):
        return ap[bass.ds(t.n * P, count), :]

    ctx = ExitStack()
    with ctx:
        def sb(name, shape, dt=FP32, c=ctx):
            return c.enter_context(nc.sbuf_tensor(name, shape, dt))

        def ps(name, shape, c=ctx):
            bank = c.enter_context(nc.psum_tensor(name, [P, BANK], FP32))
            if len(shape) == 3:
                return bank[:, :shape[1] * shape[2]].rearrange("p (a b) -> p a b", b=shape[2])
            return bank[:shape[0], :shape[1]]

        def sem(name, phase):
            handle = nc.alloc_semaphore(f"{name}_{phase.number}")
            phase.semaphores.append(handle)
            return handle

        ident = sb("ident", [P, P])
        W = max(NT, P)
        iota_i = sb("iota_i", [P, W], I32)
        iota = sb("iota", [P, W])
        iota_h = sb("iota_h", [P, W], FP16)
        before_h = sb("before_h", [P, P], FP16)
        not_before_h = sb("not_before_h", [P, P], FP16)
        ones_h = sb("ones_h", [P, P], FP16)
        zero_h = sb("zero_h", [P, P], FP16)
        ones = sb("ones", [P, P])
        earlier = sb("earlier", [P, P])
        minus_half = sb("minus_half", [P, NT])
        eps = sb("eps", [P, 1])
        lane = sb("lane", [P, 1])
        lane_i = sb("lane_i", [P, 1], I32)

        gw_sb = sb("gw_sb", [P, LAYERS, FC, D])
        gb_sb = sb("gb_sb", [P, LAYERS, D])
        wfx_sb = sb("wfx_sb", [P, FC, INNER])
        bfx_sb = sb("bfx_sb", [1, INNER])
        wx_sb = sb("wx_sb", [P, FC, INNER])
        bx_sb = sb("bx_sb", [C, H])
        wslice_sb = sb("wslice_sb", [C, C])
        bslice_sb = sb("bslice_sb", [P, C])
        wqkv_sb = sb("wqkv_sb", [C, 3, C])
        wout_sb = sb("wout_sb", [C, H, D])
        bout_sb = sb("bout_sb", [P, D])
        temp_sb = sb("temp_sb", [P, H])
        rtemp = sb("rtemp", [P, H])
        wlog = sb("wlog", [P, FC, INNER])
        blog = sb("blog", [P, INNER])
        wxT = sb("wxT", [C, FC, H, P])
        bxw = sb("bxw", [C, H, P])

        dinv = sb("dinv", [P, NT])
        cinv = sb("cinv", [P, NT])
        selfs = sb("selfs", [P, NT])
        own_coef = sb("own_coef", [P, NT])
        slot_row = sb("slot_row", [P, NT], I32)
        slot_node = sb("slot_node", [P, NT])
        slot_coef = sb("slot_coef", [P, NT])
        src_i = sb("src_i", [P, KE], I32)
        dst_i = sb("dst_i", [P, KE], I32)
        src_f = sb("src_f", [P, KE])
        dst_f = sb("dst_f", [P, KE])
        other = sb("other", [P, KE])
        overflow_i = sb("overflow_i", [P, 1], I32)
        token_sum = sb("token_sum", [P, IC, D])
        mix = sb("mix", [P, IC, D])
        weight_sum = sb("weight_sum", [P, INNER])

        with Phase(nc) as c:
            loaded = sem("weights_loaded", c)
            made = sem("constants_made", c)
            xT_done = sem("wx_transposed", c)
            xT_copied = sem("wx_transposes_copied", c)
            log_done = sem("slice_products", c)
            v_ch = sem("vector_chain_w", c)
            psT = [ps(f"psT{i}", [C, P], c=c) for i in range(2)]
            psW = ps("psW", [P, INNER], c=c)
            psB = ps("psB", [P, INNER], c=c)
            LOADS = 0
            with nc.Block() as block:
                pairs = []
                for l in range(LAYERS):
                    pairs.append((gw_sb[:, l, :, :], gw[l].rearrange("(f p) n -> p f n", p=P)))
                    pairs.append((gb_sb[:, l, :], spread(gb[l], [[1, D]])))
                pairs += [
                    (wfx_sb[:], W_fx.rearrange("(f p) n -> p f n", p=P)),
                    (bfx_sb[:], b_fx.rearrange("(a n) -> a n", a=1)),
                    (wx_sb[:], W_x.rearrange("(f p) n -> p f n", p=P)),
                    (wslice_sb[:], W_slice), (bslice_sb[:], spread(b_slice, [[1, C]])),
                    (wqkv_sb[:, 0, :], W_q), (wqkv_sb[:, 1, :], W_k), (wqkv_sb[:, 2, :], W_v),
                    (wout_sb[:], W_out.rearrange("(h c) n -> c h n", c=C)),
                    (bout_sb[:], spread(b_out, [[1, D]])),
                    (temp_sb[:], spread(temperature, [[1, H]])),
                ]
                LOADS = 16 * (len(pairs) + 1)

                @block.sync
                def _(sp):
                    for to, frm in pairs:
                        sp.dma_start(to, frm).then_inc(loaded, 16)
                    with nc.allow_non_contiguous_dma("one small vector, once"):
                        sp.dma_start(bx_sb[:], b_x.rearrange("(h c) -> c h", c=C)).then_inc(loaded, 16)
                    sp.wait_ge(loaded, LOADS)

                @block.gpsimd
                def _(pool):
                    ch = Chain(pool, made)
                    ch.mark(nc.gpsimd.iota(iota_i[:], pattern=[[1, W]], base=0, channel_multiplier=0))
                    ch.mark(nc.gpsimd.iota(lane_i[:], pattern=[[0, 1]], base=0, channel_multiplier=1))
                    for t, v in ((ident, 0.0), (ones_h, 1.0), (zero_h, 0.0), (ones, 1.0), (earlier, 1.0),
                                 (before_h, 1.0), (not_before_h, 1.0), (minus_half, -0.5), (eps, EPS)):
                        ch.mark(nc.gpsimd.memset(t[:], v))
                    ch.wait()
                    ch.mark(nc.gpsimd.tensor_copy(iota[:], iota_i[:]))
                    ch.mark(nc.gpsimd.tensor_copy(iota_h[:], iota_i[:]))
                    ch.mark(nc.gpsimd.tensor_copy(lane[:], lane_i[:]))
                    ch.mark(nc.gpsimd.affine_select(out=ident[:], in_=ident[:], compare_op=ALU.not_equal,
                                                    fill=1.0, base=0, pattern=[[-1, P]], channel_multiplier=1))
                    ch.mark(nc.gpsimd.affine_select(out=before_h[:], in_=before_h[:], compare_op=ALU.is_gt,
                                                    fill=0.0, base=0, pattern=[[1, P]], channel_multiplier=-1))
                    ch.mark(nc.gpsimd.affine_select(out=not_before_h[:], in_=not_before_h[:],
                                                    compare_op=ALU.is_ge, fill=0.0, base=0,
                                                    pattern=[[-1, P]], channel_multiplier=1))
                    ch.mark(nc.gpsimd.affine_select(out=earlier[:], in_=earlier[:], compare_op=ALU.is_gt,
                                                    fill=0.0, base=0, pattern=[[-1, P]], channel_multiplier=1))
                    ch.wait()

                MADE = 18

                @block.tensor
                def _(pe):
                    pe.wait_ge(loaded, LOADS)
                    pe.wait_ge(made, MADE)
                    n = 0
                    for f in range(FC):
                        for h in range(H):
                            if n >= 2:
                                pe.wait_ge(xT_copied, n)
                            nc.tensor.transpose(psT[n % 2][:], wx_sb[:, f, h * C:(h + 1) * C],
                                                ident[:]).then_inc(xT_done, 1)
                            n += 1
                    pe.wait_ge(xT_copied, FC * H + 1)
                    for h in range(H):
                        nc.tensor.matmul(psB[:, h * C:(h + 1) * C], bxw[:, h, :], wslice_sb[:],
                                         start=True, stop=True).then_inc(log_done, 1)
                    for f in range(FC):
                        if f:
                            pe.wait_ge(v_ch, 3 + f)
                        for h in range(H):
                            nc.tensor.matmul(psW[:, h * C:(h + 1) * C], wxT[:, f, h, :], wslice_sb[:],
                                             start=True, stop=True).then_inc(log_done, 1)

                @block.vector
                def _(dve):
                    dve.wait_ge(loaded, LOADS)
                    dve.wait_ge(made, MADE)
                    nc.vector.tensor_copy(bxw[:], bx_sb[:].unsqueeze(2).to_broadcast([C, H, P])).then_inc(xT_copied, 1)
                    n = 0
                    for f in range(FC):
                        for h in range(H):
                            dve.wait_ge(xT_done, n + 1)
                            nc.vector.tensor_copy(wxT[:, f, h, :], psT[n % 2][:]).then_inc(xT_copied, 1)
                            n += 1
                    ch = Chain(dve, v_ch)
                    ch.link(nc.vector.tensor_scalar(rtemp[:], temp_sb[:], 0.1, 5.0, ALU.max, ALU.min))
                    ch.link(nc.vector.reciprocal(rtemp[:], rtemp[:]))
                    scale = rtemp[:].unsqueeze(2).to_broadcast([P, H, C])

                    def heads(ap):
                        return ap.rearrange("p (h c) -> p h c", c=C)
                    dve.wait_ge(log_done, H)
                    ch.link(nc.vector.tensor_tensor(heads(blog[:]), heads(psB[:]),
                                                    bslice_sb[:].unsqueeze(1).to_broadcast([P, H, C]), ALU.add))
                    for f in range(FC):
                        dve.wait_ge(log_done, H + (f + 1) * H)
                        ch.link(nc.vector.tensor_tensor(heads(wlog[:, f, :]), heads(psW[:]), scale, ALU.mult))
                    ch.link(nc.vector.tensor_tensor(heads(blog[:]), heads(blog[:]), scale, ALU.mult))

        layer_norm_pass(nc, x, tables[0], NT, LAST, D, minus_half, eps, sb, sem)

        with Phase(nc) as c:
            slot_keys = [sb(f"slot_keys{i}", [P, NT], c=c) for i in range(2)]
            deg = sb("deg", [P, NT], c=c)
            src_tile = sb("src_tile", [P, KE], c=c)
            src_lane = sb("src_lane", [P, KE], c=c)
            self_lane = sb("self_lane", [P, KE], c=c)
            key1 = sb("key1", [P, KE], c=c)
            key2 = sb("key2", [P, KE], c=c)
            scratch_i = sb("scratch_i", [P, KE], I32, c)
            scratch_f = sb("scratch_f", [P, KE], c=c)
            tile_hot = sb("tile_hot", [P, 4, NT], FP16, c)
            lane_hot = sb("lane_hot", [P, 2, P], FP16, c)
            self_hot = sb("self_hot", [P, 2, P], FP16, c)
            before_o = sb("before_o", [P, 2, P], FP16, c)
            not_before_o = sb("not_before_o", [P, 2, P], FP16, c)
            all_o = sb("all_o", [P, 2, P], FP16, c)
            rank = sb("rank", [P, 2], c=c)
            picked = sb("picked", [P, 2, NT], c=c)
            rank_key1 = sb("rank_key1", [P, 2, P], FP16, c)
            rank_key2 = sb("rank_key2", [P, 2, P], FP16, c)
            counts = sb("counts", [P, NT], c=c)
            most = sb("most", [P, 1], c=c)
            over = sb("over", [P, 1], c=c)
            dec = [sb(f"dec{i}", [P, NT], I32, c) for i in range(3)]
            valid = sb("valid", [P, NT], c=c)
            fa = sb("fa", [P, NT], c=c)
            fb = sb("fb", [P, NT], c=c)
            ps_rank = [ps(f"ps_rank{i}", [P, NT], c=c) for i in range(2)]
            ps_deg = ps("ps_deg", [P, NT], c=c)
            ps_self = ps("ps_self", [P, NT], c=c)
            ps_key = [ps(f"ps_key{i}", [P, NT], c=c) for i in range(2)]

            cleared = sem("edges_cleared", c)
            edges_in = sem("edges_in", c)
            split = sem("edges_split", c)
            tile_hot_made = sem("tile_hot_made", c)
            lane_hot_made = sem("lane_hot_made", c)
            masks_made = sem("rank_masks_made", c)
            ranked = sem("prefix_in_psum", c)
            rank_read = sem("rank_read", c)
            keys_made = sem("rank_keys_made", c)
            counted = sem("column_counted", c)
            swept = sem("sweep_done", c)
            v_ch = sem("vector_chain_e", c)

            with nc.Block() as block:
                @block.gpsimd
                def _(pool):
                    nc.gpsimd.memset(src_i[:], PAD).then_inc(cleared, 1)
                    nc.gpsimd.memset(dst_i[:], PAD).then_inc(cleared, 1)

                @block.sync
                def _(sp):
                    sp.wait_ge(cleared, 2)
                    for to, frm in ((src_i, src), (dst_i, dst)):
                        sp.dma_start(to[0:EFULL, :], frm[0:EFULL * KE].rearrange("(p k) -> p k", k=KE)).then_inc(edges_in, 16)
                        if EREST:
                            sp.dma_start(to[EFULL:EFULL + 1, 0:EREST],
                                         frm[EFULL * KE:E].rearrange("(a k) -> a k", a=1)).then_inc(edges_in, 16)
                    sp.wait_ge(edges_in, 64 if EREST else 32)

                @block.scalar
                def _(act):
                    act.wait_ge(split, 1)
                    for t in steps(act, 0, KE, 2):
                        b = t.slot(2)
                        if t.reused(2):
                            act.wait_ge(counted, t.plus(-1).n)
                        for to, frm in ((before_o, before_h), (not_before_o, not_before_h), (all_o, ones_h)):
                            nc.scalar.activation(to[:, b, :], frm[:], ACT.Copy,
                                                 scale=other[:, bass.ds(t.n, 1)]).then_inc(masks_made, 1)

                @block.tensor
                def _(pe):
                    pe.wait_ge(split, 1)
                    for bank in (*ps_rank, ps_deg, ps_self, *ps_key):
                        nc.tensor.matmul(bank[:], zero_h[:], iota_h[:, :NT], start=True, stop=False,
                                         skip_group_check=True)

                    def add(bank, lhs, rhs):
                        return nc.tensor.matmul(bank[:], lhs, rhs, start=False, stop=False, skip_group_check=True)

                    def finish(t):
                        b = t.slot(2)
                        pe.wait_ge(rank_read, t.n + 1)
                        add(ps_rank[b], not_before_o[:, b, :], tile_hot[:, t.slot(4), :])
                        pe.wait_ge(keys_made, (t.n + 1) * 2)
                        add(ps_key[0], rank_key1[:, b, :], tile_hot[:, t.slot(4), :])
                        add(ps_key[1], rank_key2[:, b, :], tile_hot[:, t.slot(4), :]).then_inc(counted, 1)

                    for t in steps(pe, 0, KE, 4):
                        b, hot = t.slot(2), tile_hot[:, t.slot(4), :]
                        pe.wait_ge(tile_hot_made, t.n + 1)
                        pe.wait_ge(masks_made, (t.n + 1) * 3)
                        add(ps_rank[b], before_o[:, b, :], hot).then_inc(ranked, 1)
                        add(ps_rank[1 - b], all_o[:, b, :], hot)
                        pe.wait_ge(lane_hot_made, (t.n + 1) * 2)
                        add(ps_deg, lane_hot[:, b, :], hot)
                        add(ps_self, self_hot[:, b, :], hot)
                        finish(t)
                    for bank in (*ps_rank, ps_deg, ps_self, *ps_key):
                        last = nc.tensor.matmul(bank[:], zero_h[:], iota_h[:, :NT], start=False, stop=True,
                                                skip_group_check=True)
                    last.then_inc(swept, 1)

                @block.vector
                def _(dve):
                    ch = Chain(dve, v_ch)
                    dve.wait_ge(edges_in, 64 if EREST else 32)
                    V = nc.vector

                    def part(to, frm, op0, a, op1=None, b=None):
                        ch.link(V.tensor_scalar(scratch_i[:], frm[:], a, b, op0, *((op1,) if op1 else ())))
                        ch.link(V.tensor_copy(to[:], scratch_i[:]))
                    ch.link(V.tensor_copy(src_f[:], src_i[:]))
                    ch.link(V.tensor_copy(dst_f[:], dst_i[:]))
                    ch.link(V.tensor_tensor(other[:], src_f[:], dst_f[:], ALU.not_equal))
                    part(src_tile, src_i, ALU.logical_shift_right, 7)
                    part(src_lane, src_i, ALU.bitwise_and, P - 1)
                    ch.link(V.tensor_scalar(scratch_f[:], other[:], -1.0, 1.0, ALU.mult, ALU.add))
                    ch.link(V.scalar_tensor_tensor(self_lane[:], src_lane[:], 1.0, scratch_f[:], ALU.add, ALU.mult))
                    ch.link(V.tensor_scalar_add(self_lane[:], self_lane[:], -1.0))
                    part(key1, dst_i, ALU.logical_shift_right, 7)
                    part(key2, src_i, ALU.logical_shift_right, 5, ALU.bitwise_and, 3)
                    ch.link(V.scalar_tensor_tensor(key1[:], key1[:], 4.0, key2[:], ALU.mult, ALU.add))
                    ch.link(V.scalar_tensor_tensor(key1[:], key1[:], 1.0, other[:], ALU.add, ALU.mult))
                    part(key2, dst_i, ALU.bitwise_and, P - 1)
                    part(scratch_f, src_i, ALU.bitwise_and, 31)
                    ch.link(V.scalar_tensor_tensor(key2[:], key2[:], 32.0, scratch_f[:], ALU.mult, ALU.add))
                    ch.link(V.scalar_tensor_tensor(key2[:], key2[:], -2048.0, other[:], ALU.add, ALU.mult))
                    V.tensor_scalar_min(src_f[:], src_f[:], float(NP - 1)).then_inc(v_ch, 1)
                    V.tensor_scalar_min(dst_f[:], dst_f[:], float(NP - 1)).then_inc(v_ch, 1)
                    ch.count += 2
                    ch.wait()
                    ch.link(V.tensor_copy(src_i[:], src_f[:]))
                    V.tensor_copy(dst_i[:], dst_f[:]).then_inc(split, 1)
                    base = ch.count
                    for t in steps(dve, 0, KE, 4):
                        b = t.slot(2)
                        ch.at(base + t.n)
                        if t.reused(4):
                            dve.wait_ge(counted, t.plus(-3).n)
                        V.tensor_scalar(tile_hot[:, t.slot(4), :], iota_h[:, :NT], src_tile[:, bass.ds(t.n, 1)], None,
                                        ALU.is_equal).then_inc(tile_hot_made, 1)
                        if t.reused(2):
                            dve.wait_ge(counted, t.plus(-1).n)
                        for to, frm in ((lane_hot, src_lane), (self_hot, self_lane)):
                            V.tensor_scalar(to[:, b, :], iota_h[:, :P], frm[:, bass.ds(t.n, 1)], None,
                                            ALU.is_equal).then_inc(lane_hot_made, 1)
                        dve.wait_ge(tile_hot_made, t.n + 1)
                        dve.wait_ge(ranked, t.n + 1)
                        V.tensor_tensor_reduce(out=picked[:, b, :], in0=ps_rank[b][:], in1=tile_hot[:, t.slot(4), :],
                                               scale=1.0, scalar=0.0, op0=ALU.mult, op1=ALU.add,
                                               accum_out=rank[:, b:b + 1]).then_inc(rank_read, 1)
                        dve.wait_ge(rank_read, t.n + 1)
                        V.tensor_scalar(rank_key1[:, b, :], iota_h[:, :P], rank[:, b:b + 1],
                                        key1[:, bass.ds(t.n, 1)], ALU.is_equal, ALU.mult).then_inc(keys_made, 1)
                        V.tensor_scalar(rank_key2[:, b, :], iota_h[:, :P], rank[:, b:b + 1],
                                        key2[:, bass.ds(t.n, 1)], ALU.is_equal, ALU.mult).then_inc(keys_made, 1)

                    dve.wait_ge(swept, 1)
                    ch.at(base)
                    for to, bank in ((deg, ps_deg), (selfs, ps_self), (slot_keys[0], ps_key[0]),
                                     (slot_keys[1], ps_key[1]), (counts, ps_rank[0])):
                        ch.mark(V.tensor_copy(to[:], bank[:]))
                    ch.wait()
                    ch.link(V.tensor_reduce(most[:], counts[:], AX.X, ALU.max))
                    ch.link(V.tensor_scalar(over[:], most[:], float(P), None, ALU.is_gt))
                    ch.link(V.tensor_copy(overflow_i[:], over[:]))
                    ch.link(V.tensor_scalar(valid[:], slot_keys[0][:], 0.0, None, ALU.is_gt))
                    ch.link(V.tensor_scalar(fa[:], slot_keys[0][:], -1.0, 0.0, ALU.add, ALU.max))
                    ch.link(V.tensor_copy(dec[0][:], fa[:]))
                    ch.link(V.tensor_scalar(fb[:], slot_keys[1][:], 2048.0, None, ALU.add))
                    ch.link(V.tensor_copy(dec[1][:], fb[:]))
                    ch.link(V.tensor_scalar(dec[2][:], dec[0][:], 2, None, ALU.logical_shift_right))
                    ch.link(V.tensor_copy(fa[:], dec[2][:]))
                    ch.link(V.tensor_scalar(dec[2][:], dec[1][:], 5, None, ALU.logical_shift_right))
                    ch.link(V.tensor_copy(fb[:], dec[2][:]))
                    ch.link(V.scalar_tensor_tensor(fa[:], fa[:], float(P), fb[:], ALU.mult, ALU.add))
                    ch.link(V.scalar_tensor_tensor(fa[:], fa[:], -float(PAD * 8), valid[:], ALU.add, ALU.mult))
                    ch.link(V.tensor_scalar(fa[:], fa[:], float(PAD * 8), None, ALU.add))
                    ch.link(V.tensor_scalar(dec[0][:], dec[0][:], 3, None, ALU.bitwise_and))
                    ch.link(V.tensor_scalar(dec[1][:], dec[1][:], 31, None, ALU.bitwise_and))
                    ch.link(V.tensor_copy(slot_node[:], dec[0][:]))
                    ch.link(V.tensor_copy(fb[:], dec[1][:]))
                    ch.link(V.scalar_tensor_tensor(slot_node[:], slot_node[:], 32.0, fb[:], ALU.mult, ALU.add))
                    ch.link(V.scalar_tensor_tensor(slot_node[:], slot_node[:], 1.0, valid[:], ALU.add, ALU.mult))
                    ch.link(V.tensor_scalar_add(slot_node[:], slot_node[:], -1.0))
                    ch.link(V.tensor_scalar(fb[:], iota[:, :NT], float(P), lane[:], ALU.mult, ALU.add))
                    ch.link(V.tensor_tensor(fb[:], fb[:], fa[:], ALU.subtract))
                    ch.link(V.scalar_tensor_tensor(fa[:], fb[:], over[:], fa[:], ALU.mult, ALU.add))
                    ch.link(V.tensor_copy(slot_row[:], fa[:]))
                    ch.link(V.tensor_scalar(fb[:], slot_node[:], -1.0, lane[:], ALU.mult, ALU.add))
                    ch.link(V.scalar_tensor_tensor(slot_node[:], fb[:], over[:], slot_node[:], ALU.mult, ALU.add))
                    ch.link(V.tensor_scalar(fa[:], deg[:], 0.0, None, ALU.is_gt))
                    ch.link(V.tensor_scalar(fb[:], deg[:], 1.0, None, ALU.max))
                    ch.link(V.tensor_copy(deg[:], fa[:]))
                    ch.link(V.tensor_copy(dinv[:], fb[:]))
                    ch.link(V.tensor_copy(cinv[:], deg[:]))

        with Phase(nc) as c:
            dst_tile = sb("dst_tile", [P, KE], c=c)
            dst_lane = sb("dst_lane", [P, KE], c=c)
            scratch_i = sb("scratch_i2", [P, KE], I32, c)
            column = sb("column", [P, 4], I32, c)
            value = [sb(f"value{i}", [P, 1], c=c) for i in range(4)]
            hot_tile = sb("hot_tile32", [P, 2, NT], c=c)
            hot_lane = sb("hot_lane32", [P, 2, P], c=c)
            zero = sb("zero32", [P, P], c=c)
            raised = sb("raised", [P, NT], c=c)
            mask = sb("mask", [P, NT], c=c)
            by_tile = sb("by_tile", [P, -(-NT // P), P], c=c)
            ps_sum = ps("ps_sum", [P, NT], c=c)
            ps_t = ps("ps_t", [P, P], c=c)

            ready = sem("edges_ready", c)
            powered = sem("powered", c)
            masked = sem("masked", c)
            turned = sem("turned", c)
            copied = sem("turned_copied", c)
            written = sem("dinv_written", c)
            col_ready = sem("column_copied", c)
            got = [sem(f"value_in{i}", c) for i in range(4)]
            hots = sem("hot32_made", c)
            summed = sem("column_summed", c)
            cdone = sem("cdeg_done", c)
            v_ch = sem("vector_chain_c", c)
            CH = [(k, min(P, NT - k)) for k in range(0, NT, P)]

            with nc.Block() as block:
                @block.gpsimd
                def _(pool):
                    nc.gpsimd.tensor_tensor(raised[:], dinv[:], minus_half[:], ALU.pow).then_inc(powered, 1)
                    pool.wait_ge(written, 16 * len(CH))
                    for t in steps(pool, 0, KE, 4):
                        b = t.slot(4)
                        if t.reused(4):
                            wait_apart(pool, hots, t.plus(-3).n * 2, c.passed)
                        nc.gpsimd.tensor_copy(column[:, b:b + 1], src_i[:, bass.ds(t.n, 1)]).then_inc(col_ready, 1)
                        wait_apart(pool, col_ready, t.n + 1, c.passed)
                        nc.gpsimd.indirect_dma_start(
                            out=value[b][:], out_offset=None, in_=dinv_dram[:, :],
                            in_offset=bass.IndirectOffsetOnAxis(ap=column[:, b:b + 1], axis=0)).then_inc(got[b], 16)
                    pool.wait_ge(cdone, 1)
                    nc.gpsimd.tensor_tensor(raised[:], cinv[:], minus_half[:], ALU.pow).then_inc(powered, 1)

                @block.tensor
                def _(pe):
                    def turn(frm, base):
                        for k, (at, w) in enumerate(CH):
                            if base + k:
                                pe.wait_ge(copied, base + k)
                            nc.tensor.transpose(ps_t[0:w, :], frm[:, at:at + w], ident[:]).then_inc(turned, 1)
                    pe.wait_ge(masked, 1)
                    turn(dinv, 0)
                    pe.wait_ge(ready, 1)
                    nc.tensor.matmul(ps_sum[:], zero[:], iota[:, :NT], start=True, stop=False, skip_group_check=True)
                    for t in steps(pe, 0, KE, 2):
                        b = t.slot(2)
                        pe.wait_ge(hots, (t.n + 1) * 2)
                        nc.tensor.matmul(ps_sum[:], hot_lane[:, b, :], hot_tile[:, b, :], start=False, stop=False,
                                         skip_group_check=True).then_inc(summed, 1)
                    nc.tensor.matmul(ps_sum[:], zero[:], iota[:, :NT], start=False, stop=True,
                                     skip_group_check=True).then_inc(summed, 1)
                    pe.wait_ge(masked, 2)
                    turn(cinv, len(CH))

                @block.vector
                def _(dve):
                    V = nc.vector
                    ch = Chain(dve, v_ch)
                    dve.wait_ge(powered, 1)
                    V.tensor_tensor(dinv[:], raised[:], cinv[:], ALU.mult).then_inc(masked, 1)
                    for k, (at, w) in enumerate(CH):
                        dve.wait_ge(turned, k + 1)
                        V.tensor_copy(by_tile[0:w, k, :], ps_t[0:w, :]).then_inc(copied, 1)
                    ch.link(V.memset(zero[:], 0.0))
                    ch.link(V.tensor_scalar(scratch_i[:], dst_i[:], 7, None, ALU.logical_shift_right))
                    ch.link(V.tensor_copy(dst_tile[:], scratch_i[:]))
                    ch.link(V.tensor_scalar(scratch_i[:], dst_i[:], P - 1, None, ALU.bitwise_and))
                    V.tensor_copy(dst_lane[:], scratch_i[:]).then_inc(ready, 1)
                    dve.wait_ge(ready, 1)
                    for t in steps(dve, 0, KE, 4):
                        b = t.slot(2)
                        if t.reused(2):
                            dve.wait_ge(summed, t.plus(-1).n)
                        V.tensor_scalar(hot_tile[:, b, :], iota[:, :NT], dst_tile[:, bass.ds(t.n, 1)], None,
                                        ALU.is_equal).then_inc(hots, 1)
                        dve.wait_ge(got[t.slot(4)], t.uses(4) * 16 + 16)
                        V.tensor_scalar(hot_lane[:, b, :], iota[:, :P], dst_lane[:, bass.ds(t.n, 1)],
                                        value[t.slot(4)][:], ALU.is_equal, ALU.mult).then_inc(hots, 1)
                    dve.wait_ge(summed, KE + 1)
                    ch.link(V.tensor_scalar(mask[:], ps_sum[:], 0.0, None, ALU.is_gt))
                    V.tensor_scalar(cinv[:], ps_sum[:], 1e-30, None, ALU.max).then_inc(cdone, 1)
                    dve.wait_ge(powered, 2)
                    V.tensor_tensor(cinv[:], raised[:], mask[:], ALU.mult).then_inc(masked, 1)
                    dve.wait_ge(masked, 2)
                    ch.link(V.tensor_tensor(own_coef[:], cinv[:], selfs[:], ALU.mult))
                    dve.wait_ge(written, 16 * len(CH))
                    for k, (at, w) in enumerate(CH):
                        dve.wait_ge(turned, len(CH) + k + 1)
                        V.tensor_copy(by_tile[0:w, k, :], ps_t[0:w, :]).then_inc(copied, 1)

                @block.sync
                def _(sp):
                    view = dinv_dram.rearrange("(t p) a -> t (p a)", p=P)
                    for k, (at, w) in enumerate(CH):
                        sp.wait_ge(copied, k + 1)
                        sp.dma_start(view[at:at + w, :], by_tile[0:w, k, :]).then_inc(written, 16)
                    view = cinv_dram.rearrange("(t p) a -> t (p a)", p=P)
                    for k, (at, w) in enumerate(CH):
                        sp.wait_ge(copied, len(CH) + k + 1)
                        sp.dma_start(view[at:at + w, :], by_tile[0:w, k, :]).then_inc(written, 16)
                    sp.wait_ge(written, 16 * 2 * len(CH))

        for l in range(LAYERS):
            general_pass(nc, l, tables[l], dict(
                KE=KE, NP=NP, D=D, node_sums=node_sums, src_i=src_i, dst_i=dst_i, src_f=src_f,
                other=other, ident=ident, earlier=earlier, lane=lane, cinv_dram=cinv_dram,
                overflow_i=overflow_i), sb, ps, sem)
            layer(nc, l, l == LAYERS - 1, dict(
                NT=NT, D=D, FC=FC, H=H, C=C, IC=IC, INNER=INNER, LAST=LAST, N=N, table=tables[l],
                after=tables[l + 1] if l + 1 < LAYERS else None, x=x, x2_dram=x2_dram, w_dram=w_dram,
                cinv_dram=cinv_dram, ident=ident, iota=iota, minus_half=minus_half, eps=eps, slot_row=slot_row,
                slot_node=slot_node, slot_coef=slot_coef, own_coef=own_coef, dinv=dinv,
                w=gw_sb[:, l, :, :], b=gb_sb[:, l, :], wlog=wlog, blog=blog, token_sum=token_sum,
                weight_sum=weight_sum, node_sums=node_sums, overflow_i=overflow_i), sb, ps, sem)

        slices(nc, dict(D=D, FC=FC, H=H, C=C, IC=IC, INNER=INNER, SCALE=SCALE, ident=ident, ones=ones,
                        token_sum=token_sum, weight_sum=weight_sum, mix=mix, wfx_sb=wfx_sb, bfx_sb=bfx_sb,
                        wqkv_sb=wqkv_sb, wout_sb=wout_sb), sb, ps, sem)

        spread_back(nc, dict(NT=NT, D=D, IC=IC, INNER=INNER, LAST=LAST, N=N, x2_dram=x2_dram, w_dram=w_dram,
                             out=out, ident=ident, mix=mix, bout_sb=bout_sb), sb, ps, sem)


def flagged(eng, overflow_i):
    return eng.value_load(overflow_i[0:1, 0:1], min_val=0, max_val=1)


def tile_rows(ap, t, count=P):
    return ap[bass.ds(t.n * P, count), :]


def layer_norm_pass(nc, x, to, NT, LAST, D, minus_half, eps, sb, sem):
    B = 4
    with Phase(nc) as c:
        xin = sb("ln_x", [P, B, D], c=c)
        y = sb("ln_y", [P, B, D], c=c)
        stats = sb("ln_stats", [P, B, 6], c=c)
        mv = sb("ln_mv", [P, B, 2], c=c)
        ve = sb("ln_ve", [P, B, 1], c=c)
        rstd = sb("ln_rstd", [P, B, 1], c=c)
        cleared = sem("ln_cleared", c)
        x_in = [sem(f"ln_x_in{i}", c) for i in range(B)]
        y_out = [sem(f"ln_y_out{i}", c) for i in range(B)]
        stats_done = sem("ln_stats_done", c)
        var_done = sem("ln_var_done", c)
        eps_added = sem("ln_eps_added", c)
        rstd_done = sem("ln_rstd_done", c)
        y_done = sem("ln_y_done", c)
        with nc.Block() as block:
            @block.sync
            def _(sp):
                sp.wait_ge(cleared, 1)
                for t in steps(sp, 0, NT, B, tail=1):
                    b = t.slot(B)
                    if t.reused(B):
                        sp.wait_ge(y_done, t.plus(1 - B).n)
                    n = P if t.later(1) else LAST
                    sp.dma_start(xin[0:n, b, :], tile_rows(x, t, n)).then_inc(x_in[b], 16)

            @block.gpsimd
            def _(pool):
                nc.gpsimd.memset(xin[:], 0.0).then_inc(cleared, 1)
                for t in steps(pool, 0, NT, B):
                    b = t.slot(B)
                    pool.wait_ge(var_done, t.n + 1)
                    nc.gpsimd.tensor_tensor(ve[:, b, :], mv[:, b, 1:2], eps[:], ALU.add).then_inc(eps_added, 1)
                    pool.wait_ge(eps_added, t.n + 1)
                    nc.gpsimd.tensor_tensor(rstd[:, b, :], ve[:, b, :], minus_half[:, 0:1],
                                            ALU.pow).then_inc(rstd_done, 1)

            @block.vector
            def _(dve):
                def normalise(t):
                    b = t.slot(B)
                    dve.wait_ge(rstd_done, t.n + 1)
                    if t.reused(B):
                        dve.wait_ge(y_out[b], t.uses(B) * 16)
                    nc.vector.tensor_scalar(y[:, b, :], xin[:, b, :], mv[:, b, 0:1], rstd[:, b, :],
                                            ALU.subtract, ALU.mult).then_inc(y_done, 1)

                def statistics(t):
                    b = t.slot(B)
                    dve.wait_ge(x_in[b], t.uses(B) * 16 + 16)
                    nc.vector.bn_stats(stats[:, b, :], xin[:, b, :]).then_inc(stats_done, 1)

                def aggregate(t):
                    b = t.slot(B)
                    wait_apart(dve, stats_done, t.n + 1, c.passed)
                    nc.vector.bn_aggr(mv[:, b, :], stats[:, b, :]).then_inc(var_done, 1)
                statistics(Turn(None, 0, B, NT))
                aggregate(Turn(None, 0, B, NT))
                for t in steps(dve, 0, NT - 1, B):
                    statistics(t.plus(1))
                    normalise(t)
                    aggregate(t.plus(1))
                normalise(Turn(None, NT - 1, B, NT))

            @block.scalar
            def _(act):
                for t in steps(act, 0, NT, B):
                    b = t.slot(B)
                    act.wait_ge(y_done, t.n + 1)
                    act.dma_start(tile_rows(to, t), y[:, b, :]).then_inc(y_out[b], 16)
                for b in range(B):
                    act.wait_ge(y_out[b], 16 * (-(-(NT - b) // B)))


def general_pass(nc, l, table, k, sb, ps, sem):
    KE, NP, D, node_sums = k["KE"], k["NP"], k["D"], k["node_sums"]
    src_i, dst_i, src_f, other, ident = k["src_i"], k["dst_i"], k["src_f"], k["other"], k["ident"]
    with Phase(nc) as c:
        zero = sb(f"g_zero{l}", [P, D], c=c)
        col = sb(f"g_col{l}", [P, 3], I32, c)
        row_f = sb(f"g_row_f{l}", [P, 2], c=c)
        coef = sb(f"g_coef{l}", [P, 1], c=c)
        feat = sb(f"g_feat{l}", [P, D], c=c)
        have = sb(f"g_have{l}", [P, D], c=c)
        new = sb(f"g_new{l}", [P, D], c=c)
        wide = sb(f"g_wide{l}", [P, P], c=c)
        same = sb(f"g_same{l}", [P, P], c=c)
        dups = sb(f"g_dups{l}", [P, P], c=c)
        dup = sb(f"g_dup{l}", [P, 1], c=c)
        srow = sb(f"g_srow{l}", [P, 1], c=c)
        ps_wide = ps(f"g_ps_wide{l}", [P, P], c=c)
        ps_comb = ps(f"g_ps_comb{l}", [P, D], c=c)
        zeroed = sem(f"g_zeroed{l}", c)
        clear = sem(f"g_clear{l}", c)
        index = sem(f"g_index{l}", c)
        in_feat = sem(f"g_in_feat{l}", c)
        in_have = sem(f"g_in_have{l}", c)
        in_coef = sem(f"g_in_coef{l}", c)
        scattered = sem(f"g_scattered{l}", c)
        wide_made = sem(f"g_wide_made{l}", c)
        turned = sem(f"g_turned{l}", c)
        scaled = sem(f"g_scaled{l}", c)
        combined = sem(f"g_combined{l}", c)
        v_ch = sem(f"g_chain{l}", c)
        row_made = sem(f"g_row_made{l}", c)
        sums_made = sem(f"g_sums_made{l}", c)

        with nc.Block() as block:
            @block.sync
            def _(sp):
                with sp.If(flagged(sp, k["overflow_i"]) > 0):
                    sp.wait_ge(zeroed, 1)
                    with sp.Fori(0, NP // P + 1) as i:
                        sp.dma_start(node_sums[bass.ds(i * P, P), :], zero[:]).then_inc(clear, 16)
                    sp.wait_ge(clear, (NP // P + 1) * 16)

            @block.gpsimd
            def _(pool):
                with pool.If(flagged(pool, k["overflow_i"]) > 0):
                    pool.wait_ge(clear, (NP // P + 1) * 16)
                    with pool.Fori(0, KE) as n:
                        wait_apart(pool, row_made, n * 2 + 1, c.passed)
                        nc.gpsimd.tensor_copy(col[:, 0:1], dst_i[:, bass.ds(n, 1)]).then_inc(index, 1)
                        nc.gpsimd.tensor_copy(col[:, 1:2], row_f[:, 0:1]).then_inc(index, 1)
                        wait_apart(pool, index, n * 3 + 2, c.passed)
                        for to, frm, i, s in ((feat, table, 0, in_feat), (coef, k["cinv_dram"], 0, in_coef),
                                              (have, node_sums, 1, in_have)):
                            nc.gpsimd.indirect_dma_start(
                                out=to[:], out_offset=None, in_=frm[:, :],
                                in_offset=bass.IndirectOffsetOnAxis(ap=col[:, i:i + 1], axis=0)).then_inc(s, 16)
                        wait_apart(pool, row_made, n * 2 + 2, c.passed)
                        nc.gpsimd.tensor_copy(col[:, 2:3], row_f[:, 1:2]).then_inc(index, 1)
                        wait_apart(pool, index, n * 3 + 3, c.passed)
                        wait_apart(pool, sums_made, n + 1, c.passed)
                        nc.gpsimd.indirect_dma_start(
                            out=node_sums[:, :], out_offset=bass.IndirectOffsetOnAxis(ap=col[:, 2:3], axis=0),
                            in_=new[:], in_offset=None).then_inc(scattered, 16)
                        pool.wait_ge(scattered, n * 16 + 16)

            @block.vector
            def _(dve):
                V = nc.vector
                with dve.If(flagged(dve, k["overflow_i"]) > 0):
                    V.memset(zero[:], 0.0).then_inc(zeroed, 1)
                    with dve.Fori(0, KE) as n:
                        ch = Chain(dve, v_ch)
                        ch.at(n * 7)
                        V.tensor_copy(row_f[:, 0:1], src_f[:, bass.ds(n, 1)]).then_inc(row_made, 1)
                        ch.link(V.tensor_copy(srow[:], src_f[:, bass.ds(n, 1)]))
                        V.tensor_copy(wide[:], srow[:].to_broadcast([P, P])).then_inc(wide_made, 1)
                        dve.wait_ge(turned, n + 1)
                        ch.link(V.tensor_scalar(same[:], ps_wide[:], srow[:], None, ALU.is_equal))
                        ch.link(V.tensor_tensor_reduce(out=dups[:], in0=same[:], in1=k["earlier"][:], scale=1.0,
                                                       scalar=0.0, op0=ALU.mult, op1=ALU.add, accum_out=dup[:]))
                        ch.link(V.tensor_scalar(dup[:], dup[:], 0.0, None, ALU.is_gt))
                        dve.wait_ge(row_made, n * 2 + 1)
                        ch.link(V.tensor_scalar(row_f[:, 1:2], row_f[:, 0:1], -1.0, float(NP), ALU.mult, ALU.add))
                        ch.link(V.tensor_scalar(row_f[:, 1:2], row_f[:, 1:2], k["lane"][:], None, ALU.add))
                        ch.link(V.tensor_tensor(row_f[:, 1:2], row_f[:, 1:2], dup[:], ALU.mult))
                        V.tensor_tensor(row_f[:, 1:2], row_f[:, 1:2], row_f[:, 0:1], ALU.add).then_inc(row_made, 1)
                        dve.wait_ge(in_feat, n * 16 + 16)
                        dve.wait_ge(in_coef, n * 16 + 16)
                        V.tensor_scalar(feat[:], feat[:], coef[:], other[:, bass.ds(n, 1)], ALU.mult,
                                        ALU.mult).then_inc(scaled, 1)
                        dve.wait_ge(in_have, n * 16 + 16)
                        dve.wait_ge(combined, n + 1)
                        V.tensor_tensor(new[:], ps_comb[:], have[:], ALU.add).then_inc(sums_made, 1)
                        dve.wait_ge(scattered, n * 16 + 16)

            @block.tensor
            def _(pe):
                with pe.If(flagged(pe, k["overflow_i"]) > 0):
                    with pe.Fori(0, KE) as n:
                        pe.wait_ge(wide_made, n + 1)
                        nc.tensor.transpose(ps_wide[:], wide[:], ident[:]).then_inc(turned, 1)
                        pe.wait_ge(scaled, n + 1)
                        nc.tensor.matmul(ps_comb[:], same[:], feat[:], start=True, stop=True).then_inc(combined, 1)


def layer(nc, l, fused, k, sb, ps, sem):
    NT, D, FC, H, C, IC, INNER, LAST = (k[n] for n in ("NT", "D", "FC", "H", "C", "IC", "INNER", "LAST"))
    ident, iota, dinv = k["ident"], k["iota"], k["dinv"]
    with Phase(nc) as c:
        G = 3
        own = sb(f"own{l}", [P, 3, D], c=c)
        others = [sb(f"others{l}_{i}", [P, D], c=c) for i in range(G)]
        row = sb(f"row{l}", [P, G], I32, c)
        coef = [sb(f"coef{l}_{i}", [P, 1], c=c) for i in range(G)]
        pick = sb(f"pick{l}", [P, 2, P], c=c)
        diag = sb(f"diag{l}", [P, 2, P], c=c)
        sumT = sb(f"sumT{l}", [P, 2, D], c=c)
        z = sb(f"z{l}", [P, 2, D], c=c)
        y = sb(f"y{l}", [P, 3, D], c=c)
        ps_sum = [ps(f"ps_sum{l}_{i}", [P, D], c=c) for i in range(2)]
        outs = [ps(f"ps_out{l}_{i}", [P, D], c=c)[:] for i in range(2)]

        cleared = sem("cleared", c)
        own_in = [sem(f"own_in{i}", c) for i in range(3)]
        others_in = [sem(f"others_in{i}", c) for i in range(G)]
        coef_in = [sem(f"coef_in{i}", c) for i in range(G)]
        row_made = sem("row_made", c)
        coef_kept = sem("coef_kept", c)
        picks = sem("picks_made", c)
        diags = sem("diags_made", c)
        sums = sem("sums_done", c)
        sums_copied = sem("sums_copied", c)
        outs_done = sem("outs_done", c)
        z_done = sem("z_done", c)
        y_done = sem("y_done", c)
        y_out = [sem(f"y_out{i}", c) for i in range(3)]
        if fused:
            xres = sb("xres", [P, 3, D], c=c)
            xn = sb("xn", [P, 3, D], c=c)
            stats = sb("stats", [P, 2, 6], c=c)
            mv = sb("mv", [P, 2, 2], c=c)
            ve = sb("ve", [P, 2, 1], c=c)
            rstd = sb("rstd", [P, 2, 1], c=c)
            xnT = sb("xnT", [P, 2, D], c=c)
            lg = sb("lg", [P, 2, INNER], c=c)
            nmx = sb("nmx", [P, 2, H], c=c)
            ex = sb("ex", [P, 2, INNER], c=c)
            tot = sb("tot", [P, 2, H], c=c)
            rtot = sb("rtot", [P, 2, H], c=c)
            w = sb("w", [P, 3, INNER], c=c)
            ps_T = ps("ps_T", [P, D], c=c)
            ps_log = ps("ps_log", [P, INNER], c=c)
            ps_tok = [ps(f"ps_tok{i}", [P, 2, D], c=c) for i in range(IC // 2)]
            x_in = [sem(f"x_in{i}", c) for i in range(3)]
            stats_done = sem("stats_done", c)
            var_done = sem("var_done", c)
            eps_added = sem("eps_added", c)
            rstd_done = sem("rstd_done", c)
            xn_done = sem("xn_done", c)
            turned = sem("xn_turned", c)
            turned_copied = sem("turned_copied", c)
            logits_done = sem("logits_done", c)
            biased = sem("biased", c)
            max_done = sem("max_done", c)
            exp_done = sem("exp_done", c)
            recip_done = sem("recip_done", c)
            w_done = sem("w_done", c)
            w_out = [sem(f"w_out{i}", c) for i in range(3)]
            tokens_done = sem("tokens_done", c)
            wsum_done = sem("wsum_done", c)
        U = 6

        with nc.Block() as block:
            @block.sync
            def _(sp):
                sp.wait_ge(cleared, G + 1)
                for t in steps(sp, 0, NT, U, tail=1):
                    b = t.slot(3)
                    if t.reused(3):
                        sp.wait_ge(sums, t.plus(-2).n)
                    sp.dma_start(own[:, b, :], tile_rows(k["table"], t)).then_inc(own_in[b], 16)
                    if fused:
                        if t.reused(3):
                            sp.wait_ge(y_done, t.plus(-2).n)
                        n = P if t.later(1) else LAST
                        sp.dma_start(xres[0:n, b, :], tile_rows(k["x"], t, n)).then_inc(x_in[b], 16)

            @block.gpsimd
            def _(pool):
                over = flagged(pool, k["overflow_i"])
                for i in range(G):
                    nc.gpsimd.memset(others[i][:], 0.0).then_inc(cleared, 1)
                    if l == 0:
                        nc.gpsimd.memset(coef[i][:], 0.0).then_inc(coef_kept, 1)
                if fused:
                    nc.gpsimd.memset(xres[:], 0.0).then_inc(cleared, 1)
                    nc.gpsimd.memset(k["weight_sum"][:], 0.0).then_inc(wsum_done, 1)
                else:
                    nc.gpsimd.memset(y[:], 0.0).then_inc(cleared, 1)
                pool.wait_ge(cleared, G + 1)

                def gather(t, source, general):
                    b = t.slot(G)
                    if t.reused(G):
                        wait_apart(pool, sums, t.plus(1 - G).n, c.passed)
                    nc.gpsimd.tensor_copy(row[:, b:b + 1], k["slot_row"][:, bass.ds(t.n, 1)]).then_inc(row_made, 1)
                    wait_apart(pool, row_made, t.n + 1, c.passed)
                    at = bass.IndirectOffsetOnAxis(ap=row[:, b:b + 1], axis=0)
                    nc.gpsimd.indirect_dma_start(out=others[b][:], out_offset=None, in_=source[0:NT * P, :], in_offset=at,
                                                 bounds_check=NT * P - 1, oob_is_err=False).then_inc(others_in[b], 16)
                    if l == 0 and not general:
                        wait_apart(pool, coef_kept, t.n + 1, c.passed)
                        nc.gpsimd.indirect_dma_start(out=coef[b][:], out_offset=None, in_=k["cinv_dram"][:, :],
                                                     in_offset=at, bounds_check=k["cinv_dram"].shape[0] - 1,
                                                     oob_is_err=False).then_inc(coef_in[b], 16)

                def keep_coefs(t, general):
                    g = t.slot(G)
                    if l == 0 and not general:
                        wait_apart(pool, coef_in[g], t.uses(G) * 16 + 16, c.passed)
                        nc.gpsimd.tensor_copy(k["slot_coef"][:, bass.ds(t.n, 1)], coef[g][:]).then_inc(coef_kept, 1)

                def deviation(t):
                    b = t.slot(2)
                    pool.wait_ge(var_done, t.n + 1)
                    nc.gpsimd.tensor_tensor(ve[:, b, :], mv[:, b, 1:2], k["eps"][:], ALU.add).then_inc(eps_added, 1)
                    pool.wait_ge(eps_added, t.n + 1)
                    nc.gpsimd.tensor_tensor(rstd[:, b, :], ve[:, b, :], k["minus_half"][:, 0:1],
                                            ALU.pow).then_inc(rstd_done, 1)

                def weights(t, n=P):
                    pool.wait_ge(w_done, t.n + 1)
                    pool.wait_ge(wsum_done, t.n + 1)
                    ws = k["weight_sum"]
                    nc.gpsimd.tensor_tensor(ws[0:n, :], ws[0:n, :], w[0:n, t.slot(3), :], ALU.add).then_inc(wsum_done, 1)

                S = lambda n: Turn(None, n, U, NT)

                def program(source, general):
                    gather(S(0), source, general)
                    gather(S(1), source, general)
                    gather(S(2), source, general)
                    keep_coefs(S(0), general)
                    keep_coefs(S(1), general)
                    if fused:
                        deviation(S(0))
                        deviation(S(1))
                    for t in steps(pool, 0, NT - 2, U, tail=1, end=NT):
                        keep_coefs(t.plus(2), general)
                        if t.later(3):
                            gather(t.plus(3), source, general)
                        if fused:
                            weights(t)
                            deviation(t.plus(2))
                    if fused:
                        weights(S(NT - 2))
                        weights(S(NT - 1), LAST)

                with pool.If(over > 0):
                    if l == 0:
                        nc.gpsimd.memset(k["slot_coef"][:], 1.0).then_inc(coef_kept, NT)
                        pool.wait_ge(coef_kept, G + NT)
                    program(k["node_sums"], True)
                with pool.If(over < 1):
                    program(k["table"], False)

            @block.tensor
            def _(pe):
                def aggregate(t):
                    b, o, g = t.slot(2), t.slot(3), t.slot(G)
                    pe.wait_ge(own_in[o], t.uses(3) * 16 + 16)
                    pe.wait_ge(others_in[g], t.uses(G) * 16 + 16)
                    pe.wait_ge(picks, t.n + 1)
                    pe.wait_ge(diags, t.n + 1)
                    if t.reused(2):
                        pe.wait_ge(sums_copied, t.plus(-1).n)
                    for f in range(FC):
                        part = slice(f * P, (f + 1) * P)
                        nc.tensor.matmul(ps_sum[b][:, part], own[:, o, part], diag[:, b, :], start=True, stop=False)
                        last = nc.tensor.matmul(ps_sum[b][:, part], others[g][:, part], pick[:, b, :],
                                                start=False, stop=True)
                    last.then_inc(sums, 1)

                def project(t):
                    b = t.slot(2)
                    pe.wait_ge(sums_copied, t.n + 1)
                    if t.reused(2):
                        pe.wait_ge(z_done, t.plus(-1).n)
                    for f in range(FC):
                        last = nc.tensor.matmul(outs[b], sumT[:, b, f * P:(f + 1) * P], k["w"][:, f, :],
                                                start=(f == 0), stop=(f == FC - 1))
                    last.then_inc(outs_done, 1)

                def turn(t):
                    pe.wait_ge(xn_done, t.n + 1)
                    pe.wait_ge(turned_copied, t.n)
                    for f in range(FC):
                        last = nc.tensor.transpose(ps_T[:, f * P:(f + 1) * P], xn[:, t.slot(3), f * P:(f + 1) * P], ident[:])
                    last.then_inc(turned, 1)

                def logits(t):
                    pe.wait_ge(turned_copied, t.n + 1)
                    pe.wait_ge(biased, t.n)
                    for f in range(FC):
                        last = nc.tensor.matmul(ps_log[:], xnT[:, t.slot(2), f * P:(f + 1) * P], k["wlog"][:, f, :],
                                                start=(f == 0), stop=(f == FC - 1))
                    last.then_inc(logits_done, 1)

                def tokens(t, n=P, first=False, final=False):
                    pe.wait_ge(w_done, t.n + 1)
                    for i in range(IC):
                        last = nc.tensor.matmul(ps_tok[i // 2][:, i % 2, :], w[0:n, t.slot(3), i * P:(i + 1) * P],
                                                xn[0:n, t.slot(3), :], start=first and i % 2 == 0,
                                                stop=final and i % 2 == 1, skip_group_check=True)
                    last.then_inc(tokens_done, 1)

                S = lambda n: Turn(None, n, U, NT)
                if not fused:
                    aggregate(S(0))
                    for t in steps(pe, 0, NT - 1, U):
                        aggregate(t.plus(1))
                        project(t)
                    project(S(NT - 1))
                else:
                    aggregate(S(0))
                    project(S(0))
                    aggregate(S(1))
                    turn(S(0))
                    project(S(1))
                    logits(S(0))
                    aggregate(S(2))
                    turn(S(1))
                    project(S(2))
                    logits(S(1))
                    tokens(S(0), first=True)
                    for t in steps(pe, 1, NT - 2, U, end=NT):
                        aggregate(t.plus(2))
                        turn(t.plus(1))
                        project(t.plus(2))
                        logits(t.plus(1))
                        tokens(t)
                    turn(S(NT - 1))
                    logits(S(NT - 1))
                    tokens(S(NT - 2))
                    tokens(S(NT - 1), LAST, final=True)

            @block.vector
            def _(dve):
                V = nc.vector

                def pick_others(t):
                    b = t.slot(2)
                    if l == 0:
                        dve.wait_ge(coef_kept, t.n + 1 + G)
                    if t.reused(2):
                        dve.wait_ge(sums, t.plus(-1).n)
                    V.tensor_scalar(pick[:, b, :], iota[:, :P], k["slot_node"][:, bass.ds(t.n, 1)],
                                    k["slot_coef"][:, bass.ds(t.n, 1)], ALU.is_equal, ALU.mult).then_inc(picks, 1)

                def scaled(t):
                    b = t.slot(2)
                    dve.wait_ge(outs_done, t.n + 1)
                    if t.reused(2) and not fused:
                        dve.wait_ge(y_done, t.plus(-1).n)
                    V.scalar_tensor_tensor(z[:, b, :], outs[b], dinv[:, bass.ds(t.n, 1)], k["b"], ALU.mult,
                                           ALU.add).then_inc(z_done, 1)

                def heads(ap):
                    return ap.rearrange("p (h c) -> p h c", c=C)

                def norm(t):
                    scaled(t)
                    b, q = t.slot(2), t.slot(3)
                    dve.wait_ge(z_done, t.n + 1)
                    dve.wait_ge(x_in[q], t.uses(3) * 16 + 16)
                    if t.reused(3):
                        dve.wait_ge(y_out[q], t.uses(3) * 16)
                    V.scalar_tensor_tensor(y[:, q, :], z[:, b, :], 0.0, xres[:, q, :], ALU.max,
                                           ALU.add).then_inc(y_done, 1)
                    dve.wait_ge(y_done, t.n + 1)
                    V.bn_stats(stats[:, b, :], y[:, q, :]).then_inc(stats_done, 1)
                    wait_apart(dve, stats_done, t.n + 1, c.passed)
                    V.bn_aggr(mv[:, b, :], stats[:, b, :]).then_inc(var_done, 1)
                    dve.wait_ge(rstd_done, t.n + 1)
                    if t.reused(3):
                        dve.wait_ge(tokens_done, t.plus(-2).n)
                    V.tensor_scalar(xn[:, q, :], y[:, q, :], mv[:, b, 0:1], rstd[:, b, :], ALU.subtract,
                                    ALU.mult).then_inc(xn_done, 1)

                def softmax(t):
                    b, q = t.slot(2), t.slot(3)
                    dve.wait_ge(logits_done, t.n + 1)
                    V.tensor_tensor(lg[:, b, :], ps_log[:], k["blog"][:], ALU.add).then_inc(biased, 1)
                    dve.wait_ge(biased, t.n + 1)
                    V.tensor_reduce(nmx[:, b, :], heads(lg[:, b, :]), AX.X, ALU.max, negate=True).then_inc(max_done, 1)
                    dve.wait_ge(exp_done, (t.n + 1) * H)
                    V.reciprocal(rtot[:, b, :], tot[:, b, :]).then_inc(recip_done, 1)
                    dve.wait_ge(recip_done, t.n + 1)
                    if t.reused(3):
                        dve.wait_ge(w_out[q], t.uses(3) * 16)
                        dve.wait_ge(wsum_done, t.plus(-2).n + 1)
                        dve.wait_ge(tokens_done, t.plus(-2).n)
                    V.tensor_tensor(heads(w[:, q, :]), heads(ex[:, b, :]),
                                    rtot[:, b, :].unsqueeze(2).to_broadcast([P, H, C]), ALU.mult).then_inc(w_done, 1)

                S = lambda n: Turn(None, n, U, NT)
                if not fused:
                    pick_others(S(0))
                    for t in steps(dve, 0, NT - 1, U):
                        pick_others(t.plus(1))
                        scaled(t)
                    scaled(S(NT - 1))
                else:
                    pick_others(S(0))
                    pick_others(S(1))
                    norm(S(0))
                    norm(S(1))
                    for t in steps(dve, 0, NT - 2, U, end=NT):
                        pick_others(t.plus(2))
                        softmax(t)
                        norm(t.plus(2))
                    softmax(S(NT - 2))
                    softmax(S(NT - 1))
                    dve.wait_ge(tokens_done, NT)
                    for i in range(IC // 2):
                        last = V.tensor_copy(k["token_sum"][:, 2 * i:2 * i + 2, :], ps_tok[i][:])
                    last.then_inc(z_done, 1)
                    dve.wait_ge(z_done, NT + 1)

            @block.scalar
            def _(act):
                def diagonal(t):
                    if t.reused(2):
                        act.wait_ge(sums, t.plus(-1).n)
                    nc.scalar.activation(diag[:, t.slot(2), :], ident[:], ACT.Copy,
                                         scale=k["own_coef"][:, bass.ds(t.n, 1)]).then_inc(diags, 1)

                def copy_sums(t):
                    b = t.slot(2)
                    act.wait_ge(sums, t.n + 1)
                    if t.reused(2):
                        act.wait_ge(outs_done, t.plus(-1).n)
                    nc.scalar.activation(sumT[:, b, :], ps_sum[b][:], ACT.Copy).then_inc(sums_copied, 1)

                def relu(t):
                    b, q = t.slot(2), t.slot(3)
                    act.wait_ge(z_done, t.n + 1)
                    if t.reused(3):
                        act.wait_ge(y_out[q], t.uses(3) * 16)
                    nc.scalar.activation(y[:, q, :], z[:, b, :], ACT.Relu).then_inc(y_done, 1)
                    act.wait_ge(y_done, t.n + 1)
                    act.dma_start(tile_rows(k["after"], t), y[:, q, :]).then_inc(y_out[q], 16)

                def store_x2(t):
                    q = t.slot(3)
                    act.wait_ge(y_done, t.n + 1)
                    act.dma_start(tile_rows(k["x2_dram"], t), y[:, q, :]).then_inc(y_out[q], 16)

                def copy_turned(t):
                    b = t.slot(2)
                    act.wait_ge(turned, t.n + 1)
                    if t.reused(2):
                        act.wait_ge(logits_done, t.plus(-1).n)
                    nc.scalar.activation(xnT[:, b, :], ps_T[:], ACT.Copy).then_inc(turned_copied, 1)

                def exponentials(t):
                    b = t.slot(2)
                    act.wait_ge(max_done, t.n + 1)
                    if t.reused(2):
                        act.wait_ge(w_done, t.plus(-1).n)
                    for h in range(H):
                        part = slice(h * C, (h + 1) * C)
                        nc.scalar.activation(ex[:, b, part], lg[:, b, part], ACT.Exp, bias=nmx[:, b, h:h + 1],
                                             accum_out=tot[:, b, h:h + 1]).then_inc(exp_done, 1)

                def store_w(t):
                    q = t.slot(3)
                    act.wait_ge(w_done, t.n + 1)
                    act.dma_start(tile_rows(k["w_dram"], t), w[:, q, :]).then_inc(w_out[q], 16)

                S = lambda n: Turn(None, n, U, NT)
                if not fused:
                    act.wait_ge(cleared, G + 1)
                    diagonal(S(0))
                    copy_sums(S(0))
                    for t in steps(act, 0, NT - 1, U):
                        diagonal(t.plus(1))
                        copy_sums(t.plus(1))
                        relu(t)
                    relu(S(NT - 1))
                else:
                    diagonal(S(0))
                    diagonal(S(1))
                    copy_sums(S(0))
                    store_x2(S(0))
                    copy_sums(S(1))
                    copy_turned(S(0))
                    store_x2(S(1))
                    for t in steps(act, 0, NT - 2, U, end=NT):
                        diagonal(t.plus(2))
                        exponentials(t)
                        copy_sums(t.plus(2))
                        copy_turned(t.plus(1))
                        store_w(t)
                        store_x2(t.plus(2))
                    exponentials(S(NT - 2))
                    copy_turned(S(NT - 1))
                    store_w(S(NT - 2))
                    exponentials(S(NT - 1))
                    store_w(S(NT - 1))
                    for b in range(3):
                        act.wait_ge(w_out[b], 16 * (-(-(NT - b) // 3)))
                for b in range(3):
                    act.wait_ge(y_out[b], 16 * (-(-(NT - b) // 3)))


def slices(nc, k, sb, ps, sem):
    D, FC, H, C, IC, INNER = (k[n] for n in ("D", "FC", "H", "C", "IC", "INNER"))
    ident, ones, token_sum = k["ident"], k["ones"], k["token_sum"]
    with Phase(nc) as c:
        norm = sb("s_norm", [P, IC], c=c)
        rnorm = sb("s_rnorm", [P, IC], c=c)
        norm_row = sb("s_norm_row", [1, INNER], c=c)
        ratio_row = sb("s_ratio_row", [1, INNER], c=c)
        sumsT = sb("s_sumsT", [P, FC, INNER], c=c)
        tokT = sb("s_tokT", [C, INNER], c=c)
        qT = sb("s_qT", [C, INNER], c=c)
        kT = sb("s_kT", [C, INNER], c=c)
        v = sb("s_v", [C, INNER], c=c)
        score = sb("s_score", [C, INNER], c=c)
        big = sb("s_big", [C, H], c=c)
        total = sb("s_total", [C, H], c=c)
        attnT = sb("s_attnT", [C, INNER], c=c)
        oT = sb("s_oT", [C, INNER], c=c)
        pa = ps("s_pa", [P, INNER], c=c)
        pb = ps("s_pb", [P, INNER], c=c)
        pc = ps("s_pc", [P, INNER], c=c)
        pe_done = sem("s_pe", c)
        v_done = sem("s_v_done", c)
        a_done = sem("s_a_done", c)

        def head(ap, h):
            return ap[:, h * C:(h + 1) * C]
        with nc.Block() as block:
            @block.tensor
            def _(pe):
                T = nc.tensor
                for i in range(IC):
                    last = T.matmul(pa[:, i:i + 1], k["weight_sum"][:, i * P:(i + 1) * P], ones[:, 0:1],
                                    start=True, stop=True)
                last.then_inc(pe_done, 1)
                T.matmul(pb[0:1, :], ones[:, 0:1], k["weight_sum"][:], start=True, stop=True).then_inc(pe_done, 1)
                pe.wait_ge(v_done, 7)
                for f in range(FC):
                    if f:
                        pe.wait_ge(v_done, 7 + f)
                    for i in range(IC):
                        last = T.transpose(pc[:, i * P:(i + 1) * P], token_sum[:, i, f * P:(f + 1) * P], ident[:])
                    last.then_inc(pe_done, 1)
                pe.wait_ge(v_done, 7 + FC)
                for h in range(H):
                    part = slice(h * C, (h + 1) * C)
                    for f in range(FC):
                        T.matmul(pa[0:C, part], k["wfx_sb"][:, f, part], sumsT[:, f, part], start=(f == 0), stop=False)
                    last = T.matmul(pa[0:C, part], k["bfx_sb"][:, part], ratio_row[:, part], start=False, stop=True)
                last.then_inc(pe_done, 1)
                pe.wait_ge(v_done, 8 + FC)
                T.matmul(pb[0:C, :], k["wqkv_sb"][:, 0, :], tokT[:], start=True, stop=True).then_inc(pe_done, 1)
                T.matmul(pc[0:C, :], k["wqkv_sb"][:, 1, :], tokT[:], start=True, stop=True).then_inc(pe_done, 1)
                for h in range(H):
                    last = T.matmul(head(pa[0:C, :], h), head(tokT, h), k["wqkv_sb"][:, 2, :], start=True, stop=True)
                last.then_inc(pe_done, 1)
                pe.wait_ge(v_done, 11 + FC)
                for h in range(H):
                    last = T.matmul(head(pb[0:C, :], h), head(qT, h), head(kT, h), start=True, stop=True)
                last.then_inc(pe_done, 1)
                pe.wait_ge(v_done, 16 + FC)
                for h in range(H):
                    last = T.transpose(head(pc[0:C, :], h), head(score, h), ident[0:C, 0:C])
                last.then_inc(pe_done, 1)
                pe.wait_ge(v_done, 17 + FC)
                for h in range(H):
                    last = T.matmul(head(pa[0:C, :], h), head(v, h), head(attnT, h), start=True, stop=True)
                last.then_inc(pe_done, 1)
                pe.wait_ge(v_done, 18 + FC)
                for i in range(IC):
                    if i:
                        pe.wait_ge(v_done, 18 + FC + i)
                    for j in range(2):
                        h = 2 * i + j
                        last = T.matmul(pb[j * C:(j + 1) * C, 0:D], head(oT, h), k["wout_sb"][:, h, :],
                                        start=True, stop=True)
                    last.then_inc(pe_done, 1)

            @block.vector
            def _(dve):
                V = nc.vector
                ch = Chain(dve, v_done)
                dve.wait_ge(pe_done, 2)
                ch.mark(V.tensor_copy(norm_row[:], pb[0:1, :]))
                ch.link(V.tensor_scalar(norm[:], pa[:, 0:IC], EPS, None, ALU.add))
                ch.mark(V.reciprocal(rnorm[:], norm[:]))
                ch.link(V.tensor_scalar(ratio_row[:], norm_row[:], EPS, None, ALU.add))
                ch.link(V.reciprocal(ratio_row[:], ratio_row[:]))
                ch.link(V.tensor_tensor(ratio_row[:], ratio_row[:], norm_row[:], ALU.mult))
                ch.link(V.tensor_tensor(token_sum[:], token_sum[:], rnorm[:].unsqueeze(2).to_broadcast([P, IC, D]), ALU.mult))
                for f in range(FC):
                    dve.wait_ge(pe_done, 3 + f)
                    ch.link(V.tensor_copy(sumsT[:, f, :], pc[:]))
                dve.wait_ge(pe_done, 3 + FC)
                ch.link(V.tensor_copy(tokT[:], pa[0:C, :]))
                dve.wait_ge(pe_done, 6 + FC)
                ch.mark(V.tensor_copy(qT[:], pb[0:C, :]))
                ch.mark(V.tensor_copy(kT[:], pc[0:C, :]))
                ch.link(V.tensor_copy(v[:], pa[0:C, :]))
                dve.wait_ge(pe_done, 7 + FC)

                def heads(ap):
                    return ap.rearrange("p (h c) -> p h c", c=C)

                def wide(ap):
                    return ap[:].unsqueeze(2).to_broadcast([C, H, C])
                ch.link(V.tensor_reduce(big[:], heads(pb[0:C, :]), AX.X, ALU.max))
                ch.link(V.tensor_tensor(heads(score[:]), heads(pb[0:C, :]), wide(big), ALU.subtract))
                dve.wait_ge(a_done, 1)
                ch.link(V.tensor_reduce(total[:], heads(score[:]), AX.X, ALU.add))
                ch.link(V.reciprocal(total[:], total[:]))
                ch.link(V.tensor_tensor(heads(score[:]), heads(score[:]), wide(total), ALU.mult))
                dve.wait_ge(pe_done, 8 + FC)
                ch.link(V.tensor_copy(attnT[:], pc[0:C, :]))
                dve.wait_ge(pe_done, 9 + FC)
                ch.link(V.tensor_copy(oT[:], pa[0:C, :]))
                for i in range(IC):
                    dve.wait_ge(pe_done, 10 + FC + i)
                    ch.link(V.tensor_copy(k["mix"][:, i, :], pb[:, 0:D]))

            @block.scalar
            def _(act):
                act.wait_ge(v_done, 13 + FC)
                nc.scalar.activation(score[:], score[:], ACT.Exp, scale=k["SCALE"]).then_inc(a_done, 1)


def spread_back(nc, k, sb, ps, sem):
    NT, D, IC, INNER, LAST = (k[n] for n in ("NT", "D", "IC", "INNER", "LAST"))
    with Phase(nc) as c:
        w = sb("o_w", [P, 4, INNER], c=c)
        x2 = sb("o_x2", [P, 4, D], c=c)
        wT = sb("o_wT", [P, 2, INNER], c=c)
        xb = sb("o_xb", [P, 2, D], c=c)
        o = sb("o_o", [P, 4, D], c=c)
        ps_T = [ps(f"o_psT{i}", [P, INNER], c=c) for i in range(2)]
        ps_o = [ps(f"o_ps{i}", [P, D], c=c) for i in range(2)]
        w_in = [sem(f"o_w_in{i}", c) for i in range(4)]
        x_in = [sem(f"o_x_in{i}", c) for i in range(4)]
        o_out = [sem(f"o_out{i}", c) for i in range(4)]
        turned = sem("o_turned", c)
        copied = sem("o_copied", c)
        mixed = sem("o_mixed", c)
        biased = sem("o_biased", c)
        o_done = sem("o_done", c)
        U = 4
        with nc.Block() as block:
            @block.sync
            def _(sp):
                for t in steps(sp, 0, NT, U):
                    b = t.slot(4)
                    if t.reused(4):
                        sp.wait_ge(turned, t.plus(-3).n)
                        sp.wait_ge(biased, t.plus(-3).n)
                    sp.dma_start(w[:, b, :], tile_rows(k["w_dram"], t)).then_inc(w_in[b], 16)
                    sp.dma_start(x2[:, b, :], tile_rows(k["x2_dram"], t)).then_inc(x_in[b], 16)

            @block.tensor
            def _(pe):
                def turn(t):
                    b = t.slot(2)
                    pe.wait_ge(w_in[t.slot(4)], t.uses(4) * 16 + 16)
                    if t.reused(2):
                        pe.wait_ge(copied, t.plus(-1).n)
                    for i in range(IC):
                        part = slice(i * P, (i + 1) * P)
                        last = nc.tensor.transpose(ps_T[b][:, part], w[:, t.slot(4), part], k["ident"][:])
                    last.then_inc(turned, 1)

                def mixing(t):
                    b = t.slot(2)
                    pe.wait_ge(copied, t.n + 1)
                    if t.reused(2):
                        pe.wait_ge(o_done, t.plus(-1).n)
                    for i in range(IC):
                        last = nc.tensor.matmul(ps_o[b][:], wT[:, b, i * P:(i + 1) * P], k["mix"][:, i, :],
                                                start=(i == 0), stop=(i == IC - 1))
                    last.then_inc(mixed, 1)
                turn(Turn(None, 0, U, NT))
                for t in steps(pe, 0, NT - 1, U):
                    turn(t.plus(1))
                    mixing(t)
                mixing(Turn(None, NT - 1, U, NT))

            @block.scalar
            def _(act):
                def copy(t):
                    b = t.slot(2)
                    act.wait_ge(turned, t.n + 1)
                    if t.reused(2):
                        act.wait_ge(mixed, t.plus(-1).n)
                    nc.scalar.activation(wT[:, b, :], ps_T[b][:], ACT.Copy).then_inc(copied, 1)

                def store(t, n=P):
                    b = t.slot(4)
                    act.wait_ge(o_done, t.n + 1)
                    act.dma_start(tile_rows(k["out"], t, n), o[0:n, b, :]).then_inc(o_out[b], 16)
                copy(Turn(None, 0, U, NT))
                for t in steps(act, 0, NT - 1, U):
                    copy(t.plus(1))
                    store(t)
                store(Turn(None, NT - 1, U, NT), LAST)
                for b in range(4):
                    act.wait_ge(o_out[b], 16 * (-(-(NT - b) // 4)))

            @block.vector
            def _(dve):
                def bias(t):
                    dve.wait_ge(x_in[t.slot(4)], t.uses(4) * 16 + 16)
                    if t.reused(2):
                        dve.wait_ge(o_done, t.plus(-1).n)
                    nc.vector.tensor_tensor(xb[:, t.slot(2), :], x2[:, t.slot(4), :], k["bout_sb"][:],
                                            ALU.add).then_inc(biased, 1)

                def add(t):
                    dve.wait_ge(mixed, t.n + 1)
                    dve.wait_ge(biased, t.n + 1)
                    if t.reused(4):
                        dve.wait_ge(o_out[t.slot(4)], t.uses(4) * 16)
                    nc.vector.tensor_tensor(o[:, t.slot(4), :], ps_o[t.slot(2)][:], xb[:, t.slot(2), :],
                                            ALU.add).then_inc(o_done, 1)
                for t in steps(dve, 0, NT, U):
                    bias(t)
                    add(t)


_INS = ["x", "src", "dst", "L0_gnn_W0", "L0_gnn_b0", "L0_gnn_W1", "L0_gnn_b1", "L0_gnn_W2", "L0_gnn_b2",
        "L0_ffn_W_fx", "L0_ffn_b_fx", "L0_ffn_W_x", "L0_ffn_b_x", "L0_ffn_W_slice", "L0_ffn_b_slice",
        "L0_ffn_W_q", "L0_ffn_W_k", "L0_ffn_W_v", "L0_ffn_W_out", "L0_ffn_b_out", "L0_ffn_temperature"]


def _program(nc, shapes):
    a = {n: nc.dram_tensor(f"in_{n}", s, d, kind="ExternalInput").ap() for n, (s, d) in shapes.items()}
    out = nc.dram_tensor("out_0", shapes["x"][0], FP32, kind="ExternalOutput").ap()
    f = lambda n: a["L0_ffn_" + n]
    gnn_ffn(nc, a["x"], a["src"], a["dst"], [a[f"L0_gnn_W{l}"] for l in range(3)],
            [a[f"L0_gnn_b{l}"] for l in range(3)], f("W_fx"), f("b_fx"), f("W_x"), f("b_x"), f("W_slice"),
            f("b_slice"), f("W_q"), f("W_k"), f("W_v"), f("W_out"), f("b_out"), f("temperature"), out)


def kernel(**inputs):
    import numpy as _np
    import concourse.bacc as _bacc
    from concourse import mybir as _mybir
    from concourse.bass_utils import run_bass_kernel_spmd as _run

    nc = _bacc.Bacc("TRN2", target_bir_lowering=False, num_devices=1)
    arrays = {n: _np.ascontiguousarray(inputs[n]) for n in _INS}
    _program(nc, {n: (v.shape, _mybir.dt.from_np(v.dtype)) for n, v in arrays.items()})
    r = _run(nc, [{f"in_{n}": v for n, v in arrays.items()}], core_ids=[0])
    return r.results[0]["out_0"]
```

```python
import concourse.bass as bass
from concourse import mybir
from contextlib import ExitStack

P = 128
FP32 = mybir.dt.float32
FP16 = mybir.dt.float16
I32 = mybir.dt.int32
ALU = mybir.AluOpType
ACT = mybir.ActivationFunctionType
AX = mybir.AxisListType
BANK = 512
PAD = 1 << 16
EPS = 1e-5


class Turn:

    def __init__(self, g, at, unroll, end):
        self.g, self.at, self.unroll, self.end = g, at, unroll, end
        self.n = at if g is None else g * unroll + at

    def plus(self, d):
        return Turn(self.g, self.at + d, self.unroll, self.end)

    def slot(self, buffers):
        return self.at % buffers

    def uses(self, buffers):
        before = self.at // buffers
        return before if self.g is None else self.g * (self.unroll // buffers) + before

    def reused(self, buffers):
        return self.at >= buffers

    def exists(self):
        return self.g is not None or 0 <= self.at < self.end

    def rows(self, last):
        return last if self.g is None and self.at == self.end - 1 else P


BUFFERS = 4


def steps(eng, lo, hi, unroll, end=None, behind=0, ahead=0):
    end = hi if end is None else end
    first = min(max(lo, BUFFERS + behind), hi)
    rounds = max(min(hi, end - 1 - ahead) - first, 0) // unroll
    rounds = rounds if rounds > 1 else 0
    for n in range(lo, first):
        yield Turn(None, n, unroll, end)
    if rounds:
        with eng.Fori(0, rounds) as g:
            for u in range(unroll):
                yield Turn(g, first + u, unroll, end)
    for n in range(first + rounds * unroll, hi):
        yield Turn(None, n, unroll, end)


def at(t, d, op):
    if t.plus(d).exists():
        op(t.plus(d))


class Chain:

    def __init__(self, eng, sem):
        self.eng, self.sem, self.base, self.count = eng, sem, 0, 0

    def at(self, base):
        self.base, self.count = base, 0

    def link(self, ins):
        self.mark(ins)
        self.wait()

    def mark(self, ins):
        self.count += 1
        ins.then_inc(self.sem, 1)

    def wait(self):
        self.eng.wait_ge(self.sem, self.base + self.count)


class Phase(ExitStack):

    count = 0

    def __init__(self, nc):
        super().__init__()
        self.nc, self.semaphores = nc, []
        Phase.count += 1
        self.number = Phase.count
        self.passed = nc.alloc_semaphore(f"passed_{self.number}")
        self.semaphores.append(self.passed)

    def __exit__(self, *error):
        done = super().__exit__(*error)
        if error[0] is None:
            self.nc.clear_and_free_semaphores(self.semaphores)
            self.nc.all_engine_barrier()
        return done


def wait_apart(eng, sem, value, passed):
    eng.wait_ge(sem, value)
    eng.sem_inc(passed, 1)


def spread(ap, shape_ap):
    return bass.AP(ap.tensor, ap.offset, [[0, P]] + list(shape_ap))


def gnn_ffn(nc, x, src, dst, gw, gb, W_fx, b_fx, W_x, b_x, W_slice, b_slice, W_q, W_k, W_v,
            W_out, b_out, temperature, out):
    Phase.count = 0
    N, D = x.shape
    E = src.shape[0]
    NT = -(-N // P)
    NP = NT * P
    LAST = N - (NT - 1) * P
    FC = D // P
    INNER = W_fx.shape[1]
    H = temperature.shape[1]
    C = INNER // H
    IC = INNER // P
    KE = -(-E // P)
    KE += -KE % 4
    EFULL, EREST = E // KE, E % KE
    LAYERS = len(gw)
    SCALE = float(C) ** -0.5
    assert D == 256 and C == 64 and INNER == 512 and NT <= 391 + 120 and NT > 12

    tables = [nc.dram_tensor(f"features_{l}", (NP, D), FP32).ap() for l in range(LAYERS)]
    node_sums = nc.dram_tensor("node_sums", (NP + P, D), FP32).ap()
    x2_dram = nc.dram_tensor("x2_rows", (NP, D), FP32).ap()
    w_dram = nc.dram_tensor("slice_weights", (NP, INNER), FP32).ap()
    dinv_dram = nc.dram_tensor("dinv_rows", (NP, 1), FP32).ap()

    def rows(ap, t, count=P):
        return ap[bass.ds(t.n * P, count), :]

    ctx = ExitStack()
    with ctx:
        def sb(name, shape, dt=FP32, c=ctx):
            name = f"{name}_{c.number}" if c is not ctx else name
            return c.enter_context(nc.sbuf_tensor(name, shape, dt))

        def ps(name, shape, c):
            bank = c.enter_context(nc.psum_tensor(f"{name}_{c.number}", [P, BANK], FP32))
            if len(shape) == 3:
                return bank[:, :shape[1] * shape[2]].rearrange("p (a b) -> p a b", b=shape[2])
            return bank[:shape[0], :shape[1]]

        def sem(name, phase):
            handle = nc.alloc_semaphore(f"{name}_{phase.number}")
            phase.semaphores.append(handle)
            return handle

        ident = sb("ident", [P, P])
        W = max(NT, P)
        iota_i = sb("iota_i", [P, W], I32)
        iota = sb("iota", [P, W])
        iota_h = sb("iota_h", [P, W], FP16)
        before_h = sb("before_h", [P, P], FP16)
        not_before_h = sb("not_before_h", [P, P], FP16)
        ones_h = sb("ones_h", [P, P], FP16)
        zero_h = sb("zero_h", [P, P], FP16)
        ones = sb("ones", [P, P])
        earlier = sb("earlier", [P, P])
        minus_half = sb("minus_half", [P, NT])
        eps = sb("eps", [P, 1])
        lane = sb("lane", [P, 1])
        lane_i = sb("lane_i", [P, 1], I32)

        gw_sb = sb("gw_sb", [P, LAYERS, FC, D])
        gb_sb = sb("gb_sb", [P, LAYERS, D])
        wfx_sb = sb("wfx_sb", [P, FC, INNER])
        bfx_sb = sb("bfx_sb", [1, INNER])
        wx_sb = sb("wx_sb", [P, FC, INNER])
        bx_sb = sb("bx_sb", [C, H])
        wslice_sb = sb("wslice_sb", [C, C])
        bslice_sb = sb("bslice_sb", [P, C])
        wqkv_sb = sb("wqkv_sb", [C, 3, C])
        wout_sb = sb("wout_sb", [C, H, D])
        bout_sb = sb("bout_sb", [P, D])
        temp_sb = sb("temp_sb", [P, H])
        rtemp = sb("rtemp", [P, H])
        wlog = sb("wlog", [P, FC, INNER])
        blog = sb("blog", [P, INNER])
        wxT = sb("wxT", [C, FC, H, P])
        bxw = sb("bxw", [C, H, P])

        dinv = sb("dinv", [P, NT])
        cinv = sb("cinv", [P, NT])
        selfs = sb("selfs", [P, NT])
        slot_row = sb("slot_row", [P, NT], I32)
        slot_node = sb("slot_node", [P, NT])
        slot_tile = sb("slot_tile", [P, NT])
        slot_lane = sb("slot_lane", [P, NT])
        src_i = sb("src_i", [P, KE], I32)
        dst_i = sb("dst_i", [P, KE], I32)
        src_f = sb("src_f", [P, KE])
        dst_f = sb("dst_f", [P, KE])
        other = sb("other", [P, KE])
        overflow_i = sb("overflow_i", [P, 1], I32)
        token_sum = sb("token_sum", [P, IC, D])
        mix = sb("mix", [P, IC, D])
        weight_sum = sb("weight_sum", [P, INNER])

        with Phase(nc) as c:
            loaded = sem("weights_loaded", c)
            made = sem("constants_made", c)
            xT_done = sem("wx_transposed", c)
            xT_copied = sem("wx_transposes_copied", c)
            log_done = sem("slice_products", c)
            v_ch = sem("vector_chain_w", c)
            psT = [ps(f"psT{i}", [C, P], c=c) for i in range(2)]
            psW = ps("psW", [P, INNER], c=c)
            psB = ps("psB", [P, INNER], c=c)
            LOADS = 0
            with nc.Block() as block:
                pairs = []
                for l in range(LAYERS):
                    pairs.append((gw_sb[:, l, :, :], gw[l].rearrange("(f p) n -> p f n", p=P)))
                    pairs.append((gb_sb[:, l, :], spread(gb[l], [[1, D]])))
                pairs += [
                    (wfx_sb[:], W_fx.rearrange("(f p) n -> p f n", p=P)),
                    (bfx_sb[:], b_fx.rearrange("(a n) -> a n", a=1)),
                    (wx_sb[:], W_x.rearrange("(f p) n -> p f n", p=P)),
                    (wslice_sb[:], W_slice), (bslice_sb[:], spread(b_slice, [[1, C]])),
                    (wqkv_sb[:, 0, :], W_q), (wqkv_sb[:, 1, :], W_k), (wqkv_sb[:, 2, :], W_v),
                    (wout_sb[:], W_out.rearrange("(h c) n -> c h n", c=C)),
                    (bout_sb[:], spread(b_out, [[1, D]])),
                    (temp_sb[:], spread(temperature, [[1, H]])),
                ]
                LOADS = 16 * (len(pairs) + 1)

                @block.sync
                def _(sp):
                    for to, frm in pairs:
                        sp.dma_start(to, frm).then_inc(loaded, 16)
                    with nc.allow_non_contiguous_dma("one small vector, once"):
                        sp.dma_start(bx_sb[:], b_x.rearrange("(h c) -> c h", c=C)).then_inc(loaded, 16)
                    sp.wait_ge(loaded, LOADS)

                @block.gpsimd
                def _(pool):
                    ch = Chain(pool, made)
                    ch.mark(nc.gpsimd.iota(iota_i[:], pattern=[[1, W]], base=0, channel_multiplier=0))
                    ch.mark(nc.gpsimd.iota(lane_i[:], pattern=[[0, 1]], base=0, channel_multiplier=1))
                    for t, v in ((ident, 0.0), (ones_h, 1.0), (zero_h, 0.0), (ones, 1.0), (earlier, 1.0),
                                 (before_h, 1.0), (not_before_h, 1.0), (minus_half, -0.5), (eps, EPS)):
                        ch.mark(nc.gpsimd.memset(t[:], v))
                    ch.wait()
                    ch.mark(nc.gpsimd.tensor_copy(iota[:], iota_i[:]))
                    ch.mark(nc.gpsimd.tensor_copy(iota_h[:], iota_i[:]))
                    ch.mark(nc.gpsimd.tensor_copy(lane[:], lane_i[:]))
                    ch.mark(nc.gpsimd.affine_select(out=ident[:], in_=ident[:], compare_op=ALU.not_equal,
                                                    fill=1.0, base=0, pattern=[[-1, P]], channel_multiplier=1))
                    ch.mark(nc.gpsimd.affine_select(out=before_h[:], in_=before_h[:], compare_op=ALU.is_gt,
                                                    fill=0.0, base=0, pattern=[[1, P]], channel_multiplier=-1))
                    ch.mark(nc.gpsimd.affine_select(out=not_before_h[:], in_=not_before_h[:],
                                                    compare_op=ALU.is_ge, fill=0.0, base=0,
                                                    pattern=[[-1, P]], channel_multiplier=1))
                    ch.mark(nc.gpsimd.affine_select(out=earlier[:], in_=earlier[:], compare_op=ALU.is_gt,
                                                    fill=0.0, base=0, pattern=[[-1, P]], channel_multiplier=1))
                    ch.wait()

                MADE = 18

                @block.tensor
                def _(pe):
                    pe.wait_ge(loaded, LOADS)
                    pe.wait_ge(made, MADE)
                    n = 0
                    for f in range(FC):
                        for h in range(H):
                            if n >= 2:
                                pe.wait_ge(xT_copied, n)
                            nc.tensor.transpose(psT[n % 2][:], wx_sb[:, f, h * C:(h + 1) * C],
                                                ident[:]).then_inc(xT_done, 1)
                            n += 1
                    pe.wait_ge(xT_copied, FC * H + 1)
                    for h in range(H):
                        nc.tensor.matmul(psB[:, h * C:(h + 1) * C], bxw[:, h, :], wslice_sb[:],
                                         start=True, stop=True).then_inc(log_done, 1)
                    for f in range(FC):
                        if f:
                            pe.wait_ge(v_ch, 3 + f)
                        for h in range(H):
                            nc.tensor.matmul(psW[:, h * C:(h + 1) * C], wxT[:, f, h, :], wslice_sb[:],
                                             start=True, stop=True).then_inc(log_done, 1)

                @block.vector
                def _(dve):
                    dve.wait_ge(loaded, LOADS)
                    dve.wait_ge(made, MADE)
                    nc.vector.tensor_copy(bxw[:], bx_sb[:].unsqueeze(2).to_broadcast([C, H, P])).then_inc(xT_copied, 1)
                    n = 0
                    for f in range(FC):
                        for h in range(H):
                            dve.wait_ge(xT_done, n + 1)
                            nc.vector.tensor_copy(wxT[:, f, h, :], psT[n % 2][:]).then_inc(xT_copied, 1)
                            n += 1
                    ch = Chain(dve, v_ch)
                    ch.link(nc.vector.tensor_scalar(rtemp[:], temp_sb[:], 0.1, 5.0, ALU.max, ALU.min))
                    ch.link(nc.vector.reciprocal(rtemp[:], rtemp[:]))
                    scale = rtemp[:].unsqueeze(2).to_broadcast([P, H, C])

                    def heads(ap):
                        return ap.rearrange("p (h c) -> p h c", c=C)
                    dve.wait_ge(log_done, H)
                    ch.link(nc.vector.tensor_tensor(heads(blog[:]), heads(psB[:]),
                                                    bslice_sb[:].unsqueeze(1).to_broadcast([P, H, C]), ALU.add))
                    for f in range(FC):
                        dve.wait_ge(log_done, H + (f + 1) * H)
                        ch.link(nc.vector.tensor_tensor(heads(wlog[:, f, :]), heads(psW[:]), scale, ALU.mult))
                    ch.link(nc.vector.tensor_tensor(heads(blog[:]), heads(blog[:]), scale, ALU.mult))

        with Phase(nc) as c:
            slot_keys = [sb(f"slot_keys{i}", [P, NT], c=c) for i in range(2)]
            deg = sb("deg", [P, NT], c=c)
            src_tile = sb("src_tile", [P, KE], c=c)
            src_lane = sb("src_lane", [P, KE], c=c)
            own_edge = sb("own_edge", [P, KE], c=c)
            key1 = sb("key1", [P, KE], c=c)
            key2 = sb("key2", [P, KE], c=c)
            scratch_i = sb("scratch_i", [P, KE], I32, c)
            scratch_f = sb("scratch_f", [P, KE], c=c)
            tile_hot = sb("tile_hot", [P, 4, NT], FP16, c)
            lane_hot = sb("lane_hot", [P, 4, P], FP16, c)
            self_hot = sb("self_hot", [P, 4, P], FP16, c)
            before_o = sb("before_o", [P, 4, P], FP16, c)
            not_before_o = sb("not_before_o", [P, 4, P], FP16, c)
            all_o = sb("all_o", [P, 4, P], FP16, c)
            lane_col = sb("lane_col", [P, 4], c=c)
            rank = sb("rank", [P, 2], c=c)
            picked = sb("picked", [P, 2, NT], c=c)
            rank_key1 = sb("rank_key1", [P, 2, P], FP16, c)
            rank_key2 = sb("rank_key2", [P, 2, P], FP16, c)
            counts = sb("counts", [P, NT], c=c)
            most = sb("most", [P, 1], c=c)
            over = sb("over", [P, 1], c=c)
            dec = [sb(f"dec{i}", [P, NT], I32, c) for i in range(3)]
            valid = sb("valid", [P, NT], c=c)
            fa = sb("fa", [P, NT], c=c)
            fb = sb("fb", [P, NT], c=c)
            ps_rank = [ps(f"ps_rank{i}", [P, NT], c=c) for i in range(2)]
            ps_deg = ps("ps_deg", [P, NT], c=c)
            ps_self = ps("ps_self", [P, NT], c=c)
            ps_key = [ps(f"ps_key{i}", [P, NT], c=c) for i in range(2)]

            cleared = sem("edges_cleared", c)
            edges_in = sem("edges_in", c)
            split = sem("edges_split", c)
            tile_hot_made = sem("tile_hot_made", c)
            lane_hot_made = sem("lane_hot_made", c)
            lane_col_made = sem("lane_col_made", c)
            self_hot_made = sem("self_hot_made", c)
            masks_made = sem("rank_masks_made", c)
            ranked = sem("prefix_in_psum", c)
            rank_read = sem("rank_read", c)
            keys_made = sem("rank_keys_made", c)
            counted = sem("column_counted", c)
            swept = sem("sweep_done", c)
            v_ch = sem("vector_chain_e", c)

            with nc.Block() as block:
                @block.gpsimd
                def _(pool):
                    nc.gpsimd.memset(src_i[:], PAD).then_inc(cleared, 1)
                    nc.gpsimd.memset(dst_i[:], PAD).then_inc(cleared, 1)
                    pool.wait_ge(split, 1)
                    for t in steps(pool, 0, KE, 4):
                        b = t.slot(4)
                        if t.reused(4):
                            wait_apart(pool, counted, t.plus(-3).n, c.passed)
                        nc.gpsimd.tensor_copy(lane_col[:, b:b + 1], src_lane[:, bass.ds(t.n, 1)]).then_inc(lane_col_made, 1)
                        wait_apart(pool, lane_col_made, t.n + 1, c.passed)
                        nc.gpsimd.tensor_scalar(lane_hot[:, b, :], iota[:, :P], lane_col[:, b:b + 1], None,
                                                ALU.is_equal).then_inc(lane_hot_made, 1)

                @block.sync
                def _(sp):
                    sp.wait_ge(cleared, 2)
                    for to, frm in ((src_i, src), (dst_i, dst)):
                        sp.dma_start(to[0:EFULL, :], frm[0:EFULL * KE].rearrange("(p k) -> p k", k=KE)).then_inc(edges_in, 16)
                        if EREST:
                            sp.dma_start(to[EFULL:EFULL + 1, 0:EREST],
                                         frm[EFULL * KE:E].rearrange("(a k) -> a k", a=1)).then_inc(edges_in, 16)
                    sp.wait_ge(edges_in, 64 if EREST else 32)

                @block.scalar
                def _(act):
                    act.wait_ge(split, 1)
                    for t in steps(act, 0, KE, 4):
                        b = t.slot(4)
                        if t.reused(4):
                            act.wait_ge(counted, t.plus(-3).n)
                        for to, frm in ((before_o, before_h), (not_before_o, not_before_h), (all_o, ones_h)):
                            nc.scalar.activation(to[:, b, :], frm[:], ACT.Copy,
                                                 scale=other[:, bass.ds(t.n, 1)]).then_inc(masks_made, 1)
                        act.wait_ge(lane_hot_made, t.n + 1)
                        nc.scalar.activation(self_hot[:, b, :], lane_hot[:, b, :], ACT.Copy,
                                             scale=own_edge[:, bass.ds(t.n, 1)]).then_inc(self_hot_made, 1)

                @block.tensor
                def _(pe):
                    pe.wait_ge(split, 1)
                    for bank in (*ps_rank, ps_deg, ps_self, *ps_key):
                        nc.tensor.matmul(bank[:], zero_h[:], iota_h[:, :NT], start=True, stop=False,
                                         skip_group_check=True)

                    def add(bank, lhs, rhs):
                        return nc.tensor.matmul(bank[:], lhs, rhs, start=False, stop=False, skip_group_check=True)

                    def count(t):
                        q, hot = t.slot(4), tile_hot[:, t.slot(4), :]
                        pe.wait_ge(tile_hot_made, t.n + 1)
                        pe.wait_ge(masks_made, (t.n + 1) * 3)
                        add(ps_rank[t.slot(2)], before_o[:, q, :], hot).then_inc(ranked, 1)
                        pe.wait_ge(lane_hot_made, t.n + 1)
                        add(ps_deg, lane_hot[:, q, :], hot)
                        pe.wait_ge(self_hot_made, t.n + 1)
                        add(ps_self, self_hot[:, q, :], hot)

                    def finish(t):
                        b, q = t.slot(2), t.slot(4)
                        pe.wait_ge(rank_read, t.n + 1)
                        add(ps_rank[b], not_before_o[:, q, :], tile_hot[:, q, :])
                        if t.plus(1).exists():
                            q1 = t.plus(1).slot(4)
                            add(ps_rank[b], all_o[:, q1, :], tile_hot[:, q1, :])
                        pe.wait_ge(keys_made, (t.n + 1) * 2)
                        add(ps_key[0], rank_key1[:, b, :], tile_hot[:, q, :])
                        add(ps_key[1], rank_key2[:, b, :], tile_hot[:, q, :]).then_inc(counted, 1)

                    for t in steps(pe, 0, KE + 1, 4, end=KE, behind=1):
                        at(t, 0, count)
                        if t.g is None and t.at == 0:
                            add(ps_rank[1], all_o[:, 0, :], tile_hot[:, 0, :])
                        at(t, -1, finish)
                    for bank in (*ps_rank, ps_deg, ps_self, *ps_key):
                        last = nc.tensor.matmul(bank[:], zero_h[:], iota_h[:, :NT], start=False, stop=True,
                                                skip_group_check=True)
                    last.then_inc(swept, 1)

                @block.vector
                def _(dve):
                    ch = Chain(dve, v_ch)
                    dve.wait_ge(edges_in, 64 if EREST else 32)
                    V = nc.vector

                    def part(to, frm, op0, a, op1=None, b=None):
                        ch.link(V.tensor_scalar(scratch_i[:], frm[:], a, b, op0, *((op1,) if op1 else ())))
                        ch.link(V.tensor_copy(to[:], scratch_i[:]))
                    ch.link(V.tensor_copy(src_f[:], src_i[:]))
                    ch.link(V.tensor_copy(dst_f[:], dst_i[:]))
                    ch.link(V.tensor_tensor(other[:], src_f[:], dst_f[:], ALU.not_equal))
                    part(src_tile, src_i, ALU.logical_shift_right, 7)
                    part(src_lane, src_i, ALU.bitwise_and, P - 1)
                    ch.link(V.tensor_scalar(own_edge[:], other[:], -1.0, 1.0, ALU.mult, ALU.add))
                    part(key1, dst_i, ALU.logical_shift_right, 7)
                    part(key2, src_i, ALU.logical_shift_right, 5, ALU.bitwise_and, 3)
                    ch.link(V.scalar_tensor_tensor(key1[:], key1[:], 4.0, key2[:], ALU.mult, ALU.add))
                    ch.link(V.scalar_tensor_tensor(key1[:], key1[:], 1.0, other[:], ALU.add, ALU.mult))
                    part(key2, dst_i, ALU.bitwise_and, P - 1)
                    part(scratch_f, src_i, ALU.bitwise_and, 31)
                    ch.link(V.scalar_tensor_tensor(key2[:], key2[:], 32.0, scratch_f[:], ALU.mult, ALU.add))
                    ch.link(V.scalar_tensor_tensor(key2[:], key2[:], -2048.0, other[:], ALU.add, ALU.mult))
                    V.tensor_scalar_min(src_f[:], src_f[:], float(NP - 1)).then_inc(v_ch, 1)
                    V.tensor_scalar_min(dst_f[:], dst_f[:], float(NP - 1)).then_inc(v_ch, 1)
                    ch.count += 2
                    ch.wait()
                    ch.link(V.tensor_copy(src_i[:], src_f[:]))
                    V.tensor_copy(dst_i[:], dst_f[:]).then_inc(split, 1)
                    base = ch.count

                    def hots(t):
                        q = t.slot(4)
                        if t.reused(4):
                            dve.wait_ge(counted, t.plus(-3).n)
                        V.tensor_scalar(tile_hot[:, q, :], iota_h[:, :NT], src_tile[:, bass.ds(t.n, 1)], None,
                                        ALU.is_equal).then_inc(tile_hot_made, 1)

                    def ranks(t):
                        b = t.slot(2)
                        dve.wait_ge(tile_hot_made, t.n + 1)
                        dve.wait_ge(ranked, t.n + 1)
                        V.tensor_tensor_reduce(out=picked[:, b, :], in0=ps_rank[b][:], in1=tile_hot[:, t.slot(4), :],
                                               scale=1.0, scalar=0.0, op0=ALU.mult, op1=ALU.add,
                                               accum_out=rank[:, b:b + 1]).then_inc(rank_read, 1)

                    def slot_keys_of(t):
                        b = t.slot(2)
                        dve.wait_ge(rank_read, t.n + 1)
                        if t.reused(2):
                            dve.wait_ge(counted, t.plus(-1).n)
                        V.tensor_scalar(rank_key1[:, b, :], iota_h[:, :P], rank[:, b:b + 1],
                                        key1[:, bass.ds(t.n, 1)], ALU.is_equal, ALU.mult).then_inc(keys_made, 1)
                        V.tensor_scalar(rank_key2[:, b, :], iota_h[:, :P], rank[:, b:b + 1],
                                        key2[:, bass.ds(t.n, 1)], ALU.is_equal, ALU.mult).then_inc(keys_made, 1)

                    for t in steps(dve, -2, KE, 4, end=KE, ahead=2):
                        at(t, 0, ranks)
                        at(t, 2, hots)
                        at(t, 0, slot_keys_of)
                    dve.wait_ge(swept, 1)
                    ch.at(base)
                    for to, bank in ((deg, ps_deg), (selfs, ps_self), (slot_keys[0], ps_key[0]),
                                     (slot_keys[1], ps_key[1]), (counts, ps_rank[0])):
                        ch.mark(V.tensor_copy(to[:], bank[:]))
                    ch.wait()
                    ch.link(V.tensor_reduce(most[:], counts[:], AX.X, ALU.max))
                    ch.link(V.tensor_scalar(over[:], most[:], float(P), None, ALU.is_gt))
                    ch.link(V.tensor_copy(overflow_i[:], over[:]))
                    ch.link(V.tensor_scalar(valid[:], slot_keys[0][:], 0.0, None, ALU.is_gt))
                    ch.link(V.tensor_scalar(fa[:], slot_keys[0][:], -1.0, 0.0, ALU.add, ALU.max))
                    ch.link(V.tensor_copy(dec[0][:], fa[:]))
                    ch.link(V.tensor_scalar(fb[:], slot_keys[1][:], 2048.0, None, ALU.add))
                    ch.link(V.tensor_copy(dec[1][:], fb[:]))
                    ch.link(V.tensor_scalar(dec[2][:], dec[0][:], 2, None, ALU.logical_shift_right))
                    ch.link(V.tensor_copy(slot_tile[:], dec[2][:]))
                    ch.link(V.tensor_scalar(dec[2][:], dec[1][:], 5, None, ALU.logical_shift_right))
                    ch.link(V.tensor_copy(slot_lane[:], dec[2][:]))
                    ch.link(V.scalar_tensor_tensor(fa[:], slot_tile[:], float(P), slot_lane[:], ALU.mult,
                                                   ALU.add))
                    ch.link(V.scalar_tensor_tensor(fa[:], fa[:], -float(PAD * 8), valid[:], ALU.add, ALU.mult))
                    ch.link(V.tensor_scalar(fa[:], fa[:], float(PAD * 8), None, ALU.add))
                    ch.link(V.tensor_scalar(dec[0][:], dec[0][:], 3, None, ALU.bitwise_and))
                    ch.link(V.tensor_scalar(dec[1][:], dec[1][:], 31, None, ALU.bitwise_and))
                    ch.link(V.tensor_copy(slot_node[:], dec[0][:]))
                    ch.link(V.tensor_copy(fb[:], dec[1][:]))
                    ch.link(V.scalar_tensor_tensor(slot_node[:], slot_node[:], 32.0, fb[:], ALU.mult, ALU.add))
                    ch.link(V.scalar_tensor_tensor(slot_node[:], slot_node[:], 1.0, valid[:], ALU.add, ALU.mult))
                    ch.link(V.tensor_scalar_add(slot_node[:], slot_node[:], -1.0))
                    ch.link(V.tensor_scalar(fb[:], iota[:, :NT], float(P), lane[:], ALU.mult, ALU.add))
                    ch.link(V.tensor_tensor(fb[:], fb[:], fa[:], ALU.subtract))
                    ch.link(V.scalar_tensor_tensor(fa[:], fb[:], over[:], fa[:], ALU.mult, ALU.add))
                    ch.link(V.tensor_copy(slot_row[:], fa[:]))
                    ch.link(V.tensor_scalar(fb[:], slot_node[:], -1.0, lane[:], ALU.mult, ALU.add))
                    ch.link(V.scalar_tensor_tensor(slot_node[:], fb[:], over[:], slot_node[:], ALU.mult, ALU.add))
                    ch.link(V.tensor_scalar(fa[:], deg[:], 0.0, None, ALU.is_gt))
                    ch.link(V.tensor_scalar(fb[:], deg[:], 1.0, None, ALU.max))
                    ch.link(V.tensor_copy(deg[:], fa[:]))
                    ch.link(V.tensor_copy(dinv[:], fb[:]))
                    ch.link(V.tensor_copy(cinv[:], deg[:]))

        with Phase(nc) as c:
            G = 4
            NG = -(-NT // G)
            dst_tile = sb("dst_tile", [P, KE], c=c)
            dst_lane = sb("dst_lane", [P, KE], c=c)
            scratch_i = sb("scratch_i2", [P, KE], I32, c)
            column = sb("column", [P, 4], I32, c)
            value = [sb(f"value{i}", [P, 1], c=c) for i in range(4)]
            hot_tile = sb("hot_tile32", [P, 2, NT], c=c)
            hot_lane = sb("hot_lane32", [P, 2, P], c=c)
            zero = sb("zero32", [P, P], c=c)
            root = sb("root", [P, NT], c=c)
            raised = sb("raised", [P, NT], c=c)
            scratch = sb("scratch32", [P, NT], c=c)
            mask = sb("mask", [P, NT], c=c)
            by_tile = sb("by_tile", [P, -(-NT // P), P], c=c)
            near = sb("near", [P, 4, G * P], c=c)
            picked = sb("picked_dinv", [P, 2, G, P], c=c)
            slot_value = sb("slot_value", [P, 2, G], c=c)
            ps_sum = ps("ps_sum", [P, NT], c=c)
            ps_t = ps("ps_t", [P, P], c=c)

            ready = sem("edges_ready", c)
            rooted = sem("rooted", c)
            masked = sem("masked", c)
            turned = sem("turned", c)
            copied = sem("turned_copied", c)
            written = sem("dinv_written", c)
            col_ready = sem("column_copied", c)
            got = [sem(f"value_in{i}", c) for i in range(4)]
            hots = sem("hot32_made", c)
            summed = sem("column_summed", c)
            cdone = sem("cdeg_done", c)
            near_in = [sem(f"near_in{i}", c) for i in range(4)]
            value_made = sem("value_made", c)
            closed = sem("sums_closed", c)
            maskd = sem("sums_masked", c)
            sums = sb("sums", [P, NT], c=c)
            v_ch = sem("vector_chain_c", c)
            CH = [(k, min(P, NT - k)) for k in range(0, NT, P)]

            def tiles(g):
                return G if g.g is not None or g.at < NG - 1 else NT - (NG - 1) * G

            with nc.Block() as block:
                @block.gpsimd
                def _(pool):
                    pool.wait_ge(written, 16 * len(CH))
                    with pool.If(flagged(pool, overflow_i) > 0):
                        for t in steps(pool, 0, KE, 4):
                            b = t.slot(4)
                            if t.reused(4):
                                wait_apart(pool, hots, t.plus(-3).n * 2, c.passed)
                            nc.gpsimd.tensor_copy(column[:, b:b + 1], src_i[:, bass.ds(t.n, 1)]).then_inc(col_ready, 1)
                            wait_apart(pool, col_ready, t.n + 1, c.passed)
                            nc.gpsimd.indirect_dma_start(
                                out=value[b][:], out_offset=None, in_=dinv_dram[:, :],
                                in_offset=bass.IndirectOffsetOnAxis(ap=column[:, b:b + 1], axis=0)).then_inc(got[b], 16)

                @block.scalar
                def _(act):
                    nc.scalar.activation(root[:], dinv[:], ACT.Sqrt).then_inc(rooted, 1)
                    act.wait_ge(maskd, 2)
                    nc.scalar.activation(root[:], cinv[:], ACT.Sqrt).then_inc(rooted, 1)

                @block.tensor
                def _(pe):
                    def turn(frm, base):
                        for k, (lo, w) in enumerate(CH):
                            if base + k:
                                pe.wait_ge(copied, base + k)
                            nc.tensor.transpose(ps_t[0:w, :], frm[:, lo:lo + w], ident[:]).then_inc(turned, 1)
                    pe.wait_ge(masked, 1)
                    turn(dinv, 0)
                    pe.wait_ge(ready, 1)
                    nc.tensor.matmul(ps_sum[:], zero[:], iota[:, :NT], start=True, stop=False, skip_group_check=True)

                    def add_columns(columns):
                        for t in steps(pe, 0, columns, 2):
                            b = t.slot(2)
                            pe.wait_ge(hots, (t.n + 1) * 2)
                            nc.tensor.matmul(ps_sum[:], hot_lane[:, b, :], hot_tile[:, b, :], start=False, stop=False,
                                             skip_group_check=True).then_inc(summed, 1)
                    over = flagged(pe, overflow_i)
                    with pe.If(over > 0):
                        add_columns(KE)
                    with pe.If(over < 1):
                        add_columns(NT)
                    nc.tensor.matmul(ps_sum[:], zero[:], iota[:, :NT], start=False, stop=True,
                                     skip_group_check=True).then_inc(closed, 1)

                @block.vector
                def _(dve):
                    V = nc.vector
                    ch = Chain(dve, v_ch)

                    def inverse_root(of):
                        ch.link(V.reciprocal(raised[:], root[:]))
                        ch.link(V.tensor_tensor(scratch[:], raised[:], raised[:], ALU.mult))
                        ch.link(V.tensor_tensor(scratch[:], scratch[:], of[:], ALU.mult))
                        ch.link(V.tensor_scalar(scratch[:], scratch[:], -0.5, 1.5, ALU.mult, ALU.add))
                        ch.link(V.tensor_tensor(raised[:], raised[:], scratch[:], ALU.mult))
                    dve.wait_ge(rooted, 1)
                    inverse_root(dinv)
                    V.tensor_tensor(dinv[:], raised[:], cinv[:], ALU.mult).then_inc(masked, 1)
                    for k, (lo, w) in enumerate(CH):
                        dve.wait_ge(turned, k + 1)
                        V.tensor_copy(by_tile[0:w, k, :], ps_t[0:w, :]).then_inc(copied, 1)
                    ch.link(V.memset(zero[:], 0.0))
                    ch.link(V.tensor_scalar(scratch_i[:], dst_i[:], 7, None, ALU.logical_shift_right))
                    ch.link(V.tensor_copy(dst_tile[:], scratch_i[:]))
                    ch.link(V.tensor_scalar(scratch_i[:], dst_i[:], P - 1, None, ALU.bitwise_and))
                    V.tensor_copy(dst_lane[:], scratch_i[:]).then_inc(ready, 1)
                    dve.wait_ge(ready, 1)

                    def hot_matrices(n, b, reused, tile, lane, values):
                        if reused:
                            dve.wait_ge(summed, n - 1)
                        V.tensor_scalar(hot_tile[:, b, :], iota[:, :NT], tile[:, bass.ds(n, 1)], None,
                                        ALU.is_equal).then_inc(hots, 1)
                        V.tensor_scalar(hot_lane[:, b, :], iota[:, :P], lane[:, bass.ds(n, 1)],
                                        values, ALU.is_equal, ALU.mult).then_inc(hots, 1)

                    def slot_dinv(g):
                        b, q = g.slot(2), g.slot(4)
                        dve.wait_ge(near_in[q], g.uses(4) * 16 + 16)
                        if g.reused(2):
                            dve.wait_ge(hots, g.plus(-1).n * (2 * G))
                        for j in range(tiles(g)):
                            last = V.scalar_tensor_tensor(
                                out=picked[:, b, j, :], in0=iota[:, :P], scalar=slot_node[:, bass.ds(g.n * G + j, 1)],
                                in1=near[:, q, j * P:(j + 1) * P], op0=ALU.is_equal, op1=ALU.mult,
                                accum_out=slot_value[:, b, j:j + 1])
                        last.then_inc(value_made, 1)

                    over, linked = flagged(dve, overflow_i), ch.count
                    with dve.If(over > 0):
                        for t in steps(dve, 0, KE, 4):
                            dve.wait_ge(got[t.slot(4)], t.uses(4) * 16 + 16)
                            hot_matrices(t.n, t.slot(2), t.reused(2), dst_tile, dst_lane, value[t.slot(4)][:])
                        dve.wait_ge(closed, 1)
                        ch.link(V.tensor_copy(sums[:], ps_sum[:]))
                    with dve.If(over < 1):
                        ch.at(linked)
                        for g in steps(dve, -1, NG, 4, end=NG, ahead=1):
                            at(g, 1, slot_dinv)
                            if g.exists():
                                dve.wait_ge(value_made, g.n + 1)
                                for j in range(tiles(g)):
                                    hot_matrices(g.n * G + j, j % 2, g.reused(1) or j >= 2, slot_tile, slot_lane,
                                                 slot_value[:, g.slot(2), j:j + 1])
                        ch.link(V.tensor_tensor(sums[:], selfs[:], dinv[:], ALU.mult))
                        dve.wait_ge(closed, 1)
                        V.tensor_tensor(sums[:], sums[:], ps_sum[:], ALU.add).then_inc(cdone, 1)
                        dve.wait_ge(cdone, 1)
                    ends = ch.count + ch.base
                    V.tensor_scalar(mask[:], sums[:], 0.0, None, ALU.is_gt).then_inc(maskd, 1)
                    V.tensor_scalar(cinv[:], sums[:], 1e-30, None, ALU.max).then_inc(maskd, 1)
                    dve.wait_ge(rooted, 2)
                    ch.at(ends)
                    inverse_root(cinv)
                    V.tensor_tensor(cinv[:], raised[:], mask[:], ALU.mult).then_inc(masked, 1)
                    dve.wait_ge(masked, 2)

                @block.sync
                def _(sp):
                    view = dinv_dram.rearrange("(t p) a -> t (p a)", p=P)
                    for k, (lo, w) in enumerate(CH):
                        sp.wait_ge(copied, k + 1)
                        sp.dma_start(view[lo:lo + w, :], by_tile[0:w, k, :]).then_inc(written, 16)
                    sp.wait_ge(written, 16 * len(CH))
                    with sp.If(flagged(sp, overflow_i) < 1):
                        flat = dinv_dram.rearrange("n a -> (n a)")
                        for g in steps(sp, 0, NG, 4):
                            q, size = g.slot(4), tiles(g) * P
                            if g.reused(4):
                                sp.wait_ge(value_made, g.plus(-3).n)
                            sp.dma_start(near[:, q, 0:size],
                                         flat[bass.ds(g.n * (G * P), size)].partition_broadcast(P)).then_inc(near_in[q], 16)

        layer_norm_pass(nc, x, tables[0], NT, LAST, D, minus_half, eps, cinv, sb, sem)

        for l in range(LAYERS):
            general_pass(nc, l, tables[l], dict(
                KE=KE, NP=NP, D=D, node_sums=node_sums, src_i=src_i, dst_i=dst_i, src_f=src_f,
                other=other, ident=ident, earlier=earlier, lane=lane,
                overflow_i=overflow_i), sb, ps, sem)
            layer(nc, l, l == LAYERS - 1, dict(
                NT=NT, D=D, FC=FC, H=H, C=C, IC=IC, INNER=INNER, LAST=LAST, N=N, table=tables[l],
                after=tables[l + 1] if l + 1 < LAYERS else None, x=x, x2_dram=x2_dram, w_dram=w_dram,
                ident=ident, iota=iota, minus_half=minus_half, eps=eps, slot_row=slot_row,
                slot_node=slot_node, selfs=selfs, dinv=dinv, cinv=cinv,
                w=gw_sb[:, l, :, :], b=gb_sb[:, l, :], wlog=wlog, blog=blog, token_sum=token_sum,
                weight_sum=weight_sum, node_sums=node_sums, overflow_i=overflow_i), sb, ps, sem)

        slices(nc, dict(D=D, FC=FC, H=H, C=C, IC=IC, INNER=INNER, SCALE=SCALE, ident=ident, ones=ones,
                        token_sum=token_sum, weight_sum=weight_sum, mix=mix, wfx_sb=wfx_sb, bfx_sb=bfx_sb,
                        wqkv_sb=wqkv_sb, wout_sb=wout_sb), sb, ps, sem)

        spread_back(nc, dict(NT=NT, D=D, IC=IC, INNER=INNER, LAST=LAST, N=N, x2_dram=x2_dram, w_dram=w_dram,
                             out=out, ident=ident, mix=mix, bout_sb=bout_sb), sb, ps, sem)


def flagged(eng, overflow_i):
    return eng.value_load(overflow_i[0:1, 0:1], min_val=0, max_val=1)


def tile_rows(ap, t, count=P):
    return ap[bass.ds(t.n * P, count), :]


def layer_norm_pass(nc, x, to, NT, LAST, D, minus_half, eps, cinv, sb, sem):
    B, T = 4, 4
    NG = -(-NT // T)
    with Phase(nc) as c:
        xin = sb("ln_x", [P, B, T, D], c=c)
        y = sb("ln_y", [P, B, T, D], c=c)
        stats = sb("ln_stats", [P, B, T, 6], c=c)
        mv = sb("ln_mv", [P, B, T, 2], c=c)
        scale = sb("ln_scale", [P, B, T], c=c)
        eps_t = sb("ln_eps", [P, T], c=c)
        cleared = sem("ln_cleared", c)
        x_in = [sem(f"ln_x_in{i}", c) for i in range(B)]
        y_out = [sem(f"ln_y_out{i}", c) for i in range(B)]
        stats_done = sem("ln_stats_done", c)
        var_done = sem("ln_var_done", c)
        pool_step = sem("ln_pool_step", c)
        scale_done = sem("ln_scale_done", c)
        y_done = sem("ln_y_done", c)

        def group(ap, t):
            return ap[bass.ds(t.n * (T * P), T * P), :].rearrange("(j p) n -> p j n", p=P)

        def tiles(t):
            return T if t.g is not None or t.at < NG - 1 else NT - (NG - 1) * T
        with nc.Block() as block:
            @block.sync
            def _(sp):
                sp.wait_ge(cleared, 1)
                for t in steps(sp, 0, NG, B, ahead=0):
                    b = t.slot(B)
                    if t.reused(B):
                        sp.wait_ge(y_done, t.plus(1 - B).n)
                    if t.g is not None or t.at < NG - 1:
                        sp.dma_start(xin[:, b, :, :], group(x, t)).then_inc(x_in[b], 16)
                    else:
                        for j in range(tiles(t)):
                            n, r0 = (P if t.at * T + j < NT - 1 else LAST), (t.at * T + j) * P
                            sp.dma_start(xin[0:n, b, j, :], x[r0:r0 + n, :]).then_inc(x_in[b], 16)

            @block.gpsimd
            def _(pool):
                nc.gpsimd.memset(xin[:], 0.0).then_inc(cleared, 1)
                nc.gpsimd.memset(eps_t[:], EPS).then_inc(cleared, 1)
                pool.wait_ge(cleared, 2)
                for t in steps(pool, 0, NG, B):
                    b, k = t.slot(B), tiles(t)
                    pool.wait_ge(var_done, t.n + 1)
                    s, m = scale[:, b, 0:k], mv[:, b, 0:k, :]
                    nc.gpsimd.tensor_tensor(s, m[:, :, 1], eps_t[:, 0:k], ALU.add).then_inc(pool_step, 1)
                    pool.wait_ge(pool_step, t.n * 2 + 1)
                    nc.gpsimd.tensor_tensor(s, s, minus_half[:, 0:k], ALU.pow).then_inc(pool_step, 1)
                    pool.wait_ge(pool_step, t.n * 2 + 2)
                    nc.gpsimd.tensor_tensor(s, s, cinv[:, bass.ds(t.n * T, k)], ALU.mult).then_inc(scale_done, 1)

            @block.vector
            def _(dve):
                def statistics(t):
                    b = t.slot(B)
                    dve.wait_ge(x_in[b], t.uses(B) * 16 + 16 * (1 if tiles(t) == T or t.g is not None else tiles(t)))
                    for j in range(tiles(t)):
                        last = nc.vector.bn_stats(stats[:, b, j, :], xin[:, b, j, :])
                    last.then_inc(stats_done, 1)

                def aggregate(t):
                    b = t.slot(B)
                    wait_apart(dve, stats_done, t.n + 1, c.passed)
                    for j in range(tiles(t)):
                        last = nc.vector.bn_aggr(mv[:, b, j, :], stats[:, b, j, :])
                    last.then_inc(var_done, 1)

                def normalise(t):
                    b = t.slot(B)
                    dve.wait_ge(scale_done, t.n + 1)
                    if t.reused(B):
                        dve.wait_ge(y_out[b], t.uses(B) * 16)
                    for j in range(tiles(t)):
                        last = nc.vector.tensor_scalar(y[:, b, j, :], xin[:, b, j, :], mv[:, b, j, 0:1],
                                                       scale[:, b, j:j + 1], ALU.subtract, ALU.mult)
                    last.then_inc(y_done, 1)
                for t in steps(dve, -1, NG + 1, B, end=NG, behind=1, ahead=1):
                    at(t, 1, statistics)
                    at(t, 1, aggregate)
                    at(t, 0, normalise)

            @block.scalar
            def _(act):
                for t in steps(act, 0, NG, B):
                    b = t.slot(B)
                    act.wait_ge(y_done, t.n + 1)
                    if t.g is not None or t.at < NG - 1:
                        act.dma_start(group(to, t), y[:, b, :, :]).then_inc(y_out[b], 16)
                    else:
                        r0, k = t.at * T * P, tiles(t)
                        act.dma_start(to[r0:r0 + k * P, :].rearrange("(j p) n -> p j n", p=P),
                                      y[:, b, 0:k, :]).then_inc(y_out[b], 16)
                for b in range(B):
                    act.wait_ge(y_out[b], 16 * (-(-(NG - b) // B)))


def general_pass(nc, l, table, k, sb, ps, sem):
    KE, NP, D, node_sums = k["KE"], k["NP"], k["D"], k["node_sums"]
    src_i, dst_i, src_f, other, ident = k["src_i"], k["dst_i"], k["src_f"], k["other"], k["ident"]
    with Phase(nc) as c:
        zero = sb(f"g_zero{l}", [P, D], c=c)
        col = sb(f"g_col{l}", [P, 3], I32, c)
        row_f = sb(f"g_row_f{l}", [P, 2], c=c)
        feat = sb(f"g_feat{l}", [P, D], c=c)
        have = sb(f"g_have{l}", [P, D], c=c)
        new = sb(f"g_new{l}", [P, D], c=c)
        wide = sb(f"g_wide{l}", [P, P], c=c)
        same = sb(f"g_same{l}", [P, P], c=c)
        dups = sb(f"g_dups{l}", [P, P], c=c)
        dup = sb(f"g_dup{l}", [P, 1], c=c)
        srow = sb(f"g_srow{l}", [P, 1], c=c)
        ps_wide = ps(f"g_ps_wide{l}", [P, P], c=c)
        ps_comb = ps(f"g_ps_comb{l}", [P, D], c=c)
        zeroed = sem(f"g_zeroed{l}", c)
        clear = sem(f"g_clear{l}", c)
        index = sem(f"g_index{l}", c)
        in_feat = sem(f"g_in_feat{l}", c)
        in_have = sem(f"g_in_have{l}", c)
        scattered = sem(f"g_scattered{l}", c)
        wide_made = sem(f"g_wide_made{l}", c)
        turned = sem(f"g_turned{l}", c)
        scaled = sem(f"g_scaled{l}", c)
        combined = sem(f"g_combined{l}", c)
        v_ch = sem(f"g_chain{l}", c)
        row_made = sem(f"g_row_made{l}", c)
        sums_made = sem(f"g_sums_made{l}", c)

        with nc.Block() as block:
            @block.sync
            def _(sp):
                with sp.If(flagged(sp, k["overflow_i"]) > 0):
                    sp.wait_ge(zeroed, 1)
                    with sp.Fori(0, NP // P + 1) as i:
                        sp.dma_start(node_sums[bass.ds(i * P, P), :], zero[:]).then_inc(clear, 16)
                    sp.wait_ge(clear, (NP // P + 1) * 16)

            @block.gpsimd
            def _(pool):
                with pool.If(flagged(pool, k["overflow_i"]) > 0):
                    pool.wait_ge(clear, (NP // P + 1) * 16)
                    with pool.Fori(0, KE) as n:
                        wait_apart(pool, row_made, n * 2 + 1, c.passed)
                        nc.gpsimd.tensor_copy(col[:, 0:1], dst_i[:, bass.ds(n, 1)]).then_inc(index, 1)
                        nc.gpsimd.tensor_copy(col[:, 1:2], row_f[:, 0:1]).then_inc(index, 1)
                        wait_apart(pool, index, n * 3 + 2, c.passed)
                        for to, frm, i, s in ((feat, table, 0, in_feat), (have, node_sums, 1, in_have)):
                            nc.gpsimd.indirect_dma_start(
                                out=to[:], out_offset=None, in_=frm[:, :],
                                in_offset=bass.IndirectOffsetOnAxis(ap=col[:, i:i + 1], axis=0)).then_inc(s, 16)
                        wait_apart(pool, row_made, n * 2 + 2, c.passed)
                        nc.gpsimd.tensor_copy(col[:, 2:3], row_f[:, 1:2]).then_inc(index, 1)
                        wait_apart(pool, index, n * 3 + 3, c.passed)
                        wait_apart(pool, sums_made, n + 1, c.passed)
                        nc.gpsimd.indirect_dma_start(
                            out=node_sums[:, :], out_offset=bass.IndirectOffsetOnAxis(ap=col[:, 2:3], axis=0),
                            in_=new[:], in_offset=None).then_inc(scattered, 16)
                        pool.wait_ge(scattered, n * 16 + 16)

            @block.vector
            def _(dve):
                V = nc.vector
                with dve.If(flagged(dve, k["overflow_i"]) > 0):
                    V.memset(zero[:], 0.0).then_inc(zeroed, 1)
                    with dve.Fori(0, KE) as n:
                        ch = Chain(dve, v_ch)
                        ch.at(n * 7)
                        V.tensor_copy(row_f[:, 0:1], src_f[:, bass.ds(n, 1)]).then_inc(row_made, 1)
                        ch.link(V.tensor_copy(srow[:], src_f[:, bass.ds(n, 1)]))
                        V.tensor_copy(wide[:], srow[:].to_broadcast([P, P])).then_inc(wide_made, 1)
                        dve.wait_ge(turned, n + 1)
                        ch.link(V.tensor_scalar(same[:], ps_wide[:], srow[:], None, ALU.is_equal))
                        ch.link(V.tensor_tensor_reduce(out=dups[:], in0=same[:], in1=k["earlier"][:], scale=1.0,
                                                       scalar=0.0, op0=ALU.mult, op1=ALU.add, accum_out=dup[:]))
                        ch.link(V.tensor_scalar(dup[:], dup[:], 0.0, None, ALU.is_gt))
                        dve.wait_ge(row_made, n * 2 + 1)
                        ch.link(V.tensor_scalar(row_f[:, 1:2], row_f[:, 0:1], -1.0, float(NP), ALU.mult, ALU.add))
                        ch.link(V.tensor_scalar(row_f[:, 1:2], row_f[:, 1:2], k["lane"][:], None, ALU.add))
                        ch.link(V.tensor_tensor(row_f[:, 1:2], row_f[:, 1:2], dup[:], ALU.mult))
                        V.tensor_tensor(row_f[:, 1:2], row_f[:, 1:2], row_f[:, 0:1], ALU.add).then_inc(row_made, 1)
                        dve.wait_ge(in_feat, n * 16 + 16)
                        V.tensor_scalar(feat[:], feat[:], other[:, bass.ds(n, 1)], None, ALU.mult).then_inc(scaled, 1)
                        dve.wait_ge(in_have, n * 16 + 16)
                        dve.wait_ge(combined, n + 1)
                        V.tensor_tensor(new[:], ps_comb[:], have[:], ALU.add).then_inc(sums_made, 1)
                        dve.wait_ge(scattered, n * 16 + 16)

            @block.tensor
            def _(pe):
                with pe.If(flagged(pe, k["overflow_i"]) > 0):
                    with pe.Fori(0, KE) as n:
                        pe.wait_ge(wide_made, n + 1)
                        nc.tensor.transpose(ps_wide[:], wide[:], ident[:]).then_inc(turned, 1)
                        pe.wait_ge(scaled, n + 1)
                        nc.tensor.matmul(ps_comb[:], same[:], feat[:], start=True, stop=True).then_inc(combined, 1)


def layer(nc, l, fused, k, sb, ps, sem):
    NT, D, FC, H, C, IC, INNER, LAST = (k[n] for n in ("NT", "D", "FC", "H", "C", "IC", "INNER", "LAST"))
    ident, iota, dinv = k["ident"], k["iota"], k["dinv"]
    B = BUFFERS
    with Phase(nc) as c:
        own = sb("own", [P, B, D], c=c)
        scaled_own = sb("scaled_own", [P, B, D], c=c)
        others = [sb(f"others{i}", [P, D], c=c) for i in range(B)]
        row = sb("row", [P, B], I32, c)
        pick = sb("pick", [P, B, P], c=c)
        sumT = sb("sumT", [P, 2, D], c=c)
        z = sb("z", [P, 2, D], c=c)
        y = sb("y", [P, B, D], c=c)
        ps_sum = [ps(f"ps_sum{l}_{i}", [P, D], c=c) for i in range(2)]
        ps_out = [ps(f"ps_out{l}_{i}", [P, D], c=c) for i in range(2)]

        cleared = sem("cleared", c)
        own_in = [sem(f"own_in{i}", c) for i in range(B)]
        others_in = [sem(f"others_in{i}", c) for i in range(B)]
        row_made = sem("row_made", c)
        own_scaled = sem("own_scaled", c)
        picks = sem("picks_made", c)
        sums = sem("sums_done", c)
        sums_copied = sem("sums_copied", c)
        outs_done = sem("outs_done", c)
        z_done = sem("z_done", c)
        y_done = sem("y_done", c)
        y_out = [sem(f"y_out{i}", c) for i in range(B)]
        if fused:
            xres = sb("xres", [P, B, D], c=c)
            xn = sb("xn", [P, B, D], c=c)
            stats = sb("stats", [P, 2, 6], c=c)
            mv = sb("mv", [P, 2, 2], c=c)
            ve = sb("ve", [P, 2, 1], c=c)
            rstd = sb("rstd", [P, 2, 1], c=c)
            xnT = sb("xnT", [P, 2, D], c=c)
            lg = sb("lg", [P, 2, INNER], c=c)
            nmx = sb("nmx", [P, 2, H], c=c)
            ex = sb("ex", [P, 2, INNER], c=c)
            tot = sb("tot", [P, 2, H], c=c)
            rtot = sb("rtot", [P, 2, H], c=c)
            w = sb("w", [P, B, INNER], c=c)
            ps_T = ps("ps_T", [P, D], c=c)
            ps_log = ps("ps_log", [P, INNER], c=c)
            ps_tok = [ps(f"ps_tok{i}", [P, 2, D], c=c) for i in range(IC // 2)]
            x_in = [sem(f"x_in{i}", c) for i in range(B)]
            stats_done = sem("stats_done", c)
            var_done = sem("var_done", c)
            eps_added = sem("eps_added", c)
            rstd_done = sem("rstd_done", c)
            xn_done = sem("xn_done", c)
            turned = sem("xn_turned", c)
            turned_copied = sem("xn_turned_copied", c)
            logits_done = sem("logits_done", c)
            biased = sem("biased", c)
            max_done = sem("max_done", c)
            exp_done = sem("exp_done", c)
            recip_done = sem("recip_done", c)
            w_done = sem("w_done", c)
            w_out = [sem(f"w_out{i}", c) for i in range(B)]
            tokens_done = sem("tokens_done", c)
            wsum_done = sem("wsum_done", c)
            saved = sem("tokens_saved", c)
        LOADS = B

        def scale_own(eng, make, t):
            b = t.slot(B)
            eng.wait_ge(own_in[b], t.uses(B) * 16 + 16)
            if t.reused(B):
                eng.wait_ge(sums, t.plus(1 - B).n)
            make(scaled_own[:, b, :], own[:, b, :], k["selfs"][:, bass.ds(t.n, 1)]).then_inc(own_scaled, 1)

        with nc.Block() as block:
            @block.sync
            def _(sp):
                sp.wait_ge(cleared, B + 1)

                def load_own(t):
                    b = t.slot(B)
                    if t.reused(B):
                        sp.wait_ge(own_scaled, t.plus(1 - B).n)
                    sp.dma_start(own[:, b, :], tile_rows(k["table"], t)).then_inc(own_in[b], 16)

                def load_x(t):
                    b, n = t.slot(B), t.rows(LAST)
                    if t.reused(B):
                        sp.wait_ge(y_done, t.plus(1 - B).n)
                    sp.dma_start(xres[0:n, b, :], tile_rows(k["x"], t, n)).then_inc(x_in[b], 16)

                def store_y(t):
                    b = t.slot(B)
                    sp.wait_ge(y_done, t.n + 1)
                    sp.dma_start(tile_rows(k["x2_dram"] if fused else k["after"], t), y[:, b, :]).then_inc(y_out[b], 16)

                def store_w(t):
                    b = t.slot(B)
                    sp.wait_ge(w_done, t.n + 1)
                    sp.dma_start(tile_rows(k["w_dram"], t), w[:, b, :]).then_inc(w_out[b], 16)

                if fused:
                    for t in steps(sp, -6, NT + 1, B, end=NT, behind=1, ahead=6):
                        at(t, 6, load_own)
                        at(t, -1, store_w)
                        at(t, 2, store_y)
                        at(t, 6, load_x)
                    for b in range(B):
                        sp.wait_ge(w_out[b], 16 * (-(-(NT - b) // B)))
                else:
                    for t in steps(sp, -5, NT, B, end=NT, ahead=5):
                        at(t, 5, load_own)
                        at(t, 0, store_y)
                for b in range(B):
                    sp.wait_ge(y_out[b], 16 * (-(-(NT - b) // B)))

            @block.gpsimd
            def _(pool):
                over = flagged(pool, k["overflow_i"])
                for i in range(B):
                    nc.gpsimd.memset(others[i][:], 0.0).then_inc(cleared, 1)
                if fused:
                    nc.gpsimd.memset(xres[:], 0.0).then_inc(cleared, 1)
                    nc.gpsimd.memset(k["weight_sum"][:], 0.0).then_inc(wsum_done, 1)
                else:
                    nc.gpsimd.memset(y[:], 0.0).then_inc(cleared, 1)
                pool.wait_ge(cleared, B + 1)

                def deviation(t):
                    b = t.slot(2)
                    pool.wait_ge(var_done, t.n + 1)
                    nc.gpsimd.tensor_tensor(ve[:, b, :], mv[:, b, 1:2], k["eps"][:], ALU.add).then_inc(eps_added, 1)
                    pool.wait_ge(eps_added, t.n + 1)
                    nc.gpsimd.tensor_tensor(rstd[:, b, :], ve[:, b, :], k["minus_half"][:, 0:1],
                                            ALU.pow).then_inc(rstd_done, 1)

                def add_weights(t):
                    pool.wait_ge(w_done, t.n + 1)
                    pool.wait_ge(wsum_done, t.n + 1)
                    n, ws = t.rows(LAST), k["weight_sum"]
                    nc.gpsimd.tensor_tensor(ws[0:n, :], ws[0:n, :], w[0:n, t.slot(B), :], ALU.add).then_inc(wsum_done, 1)

                def program(source):
                    def gather(t):
                        b = t.slot(B)
                        if t.reused(B):
                            wait_apart(pool, sums, t.plus(1 - B).n, c.passed)
                        nc.gpsimd.tensor_copy(row[:, b:b + 1], k["slot_row"][:, bass.ds(t.n, 1)]).then_inc(row_made, 1)
                        wait_apart(pool, row_made, t.n + 1, c.passed)
                        nc.gpsimd.indirect_dma_start(
                            out=others[b][:], out_offset=None, in_=source[0:NT * P, :],
                            in_offset=bass.IndirectOffsetOnAxis(ap=row[:, b:b + 1], axis=0),
                            bounds_check=NT * P - 1, oob_is_err=False).then_inc(others_in[b], 16)
                    if fused:
                        for t in steps(pool, -4, NT + 1, B, end=NT, behind=1, ahead=4):
                            at(t, 4, gather)
                            at(t, -1, add_weights)
                            at(t, 2, deviation)
                    else:
                        for t in steps(pool, 0, NT, B):
                            gather(t)

                with pool.If(over > 0):
                    program(k["node_sums"])
                with pool.If(over < 1):
                    program(k["table"])

            @block.tensor
            def _(pe):
                def aggregate(t):
                    b, q = t.slot(2), t.slot(B)
                    pe.wait_ge(own_scaled, t.n + 1)
                    pe.wait_ge(picks, t.n + 1)
                    if t.reused(2):
                        pe.wait_ge(sums_copied, t.plus(-1).n)
                    for f in range(FC):
                        part = slice(f * P, (f + 1) * P)
                        nc.tensor.matmul(ps_sum[b][:, part], scaled_own[:, q, part], ident[:], is_transpose=True,
                                         start=True, stop=False)
                        if f == 0:
                            pe.wait_ge(others_in[q], t.uses(B) * 16 + 16)
                        last = nc.tensor.matmul(ps_sum[b][:, part], others[q][:, part], pick[:, q, :],
                                                start=False, stop=True)
                    last.then_inc(sums, 1)

                def project(t):
                    b = t.slot(2)
                    pe.wait_ge(sums_copied, t.n + 1)
                    if t.reused(2):
                        pe.wait_ge(z_done, t.plus(-1).n)
                    for f in range(FC):
                        last = nc.tensor.matmul(ps_out[b], sumT[:, b, f * P:(f + 1) * P], k["w"][:, f, :],
                                                start=(f == 0), stop=(f == FC - 1))
                    last.then_inc(outs_done, 1)

                def turn(t):
                    pe.wait_ge(xn_done, t.n + 1)
                    if t.reused(1):
                        pe.wait_ge(turned_copied, t.n)
                    for f in range(FC):
                        last = nc.tensor.transpose(ps_T[:, f * P:(f + 1) * P], xn[:, t.slot(B), f * P:(f + 1) * P], ident[:])
                    last.then_inc(turned, 1)

                def logits(t):
                    pe.wait_ge(turned_copied, t.n + 1)
                    if t.reused(1):
                        pe.wait_ge(biased, t.n)
                    for f in range(FC):
                        last = nc.tensor.matmul(ps_log[:], xnT[:, t.slot(2), f * P:(f + 1) * P], k["wlog"][:, f, :],
                                                start=(f == 0), stop=(f == FC - 1))
                    last.then_inc(logits_done, 1)

                def tokens(t):
                    n, final = t.rows(LAST), t.g is None and t.at == NT - 1
                    first = t.g is None and t.at == 0
                    pe.wait_ge(w_done, t.n + 1)
                    for i in range(IC):
                        last = nc.tensor.matmul(ps_tok[i // 2][:, i % 2, :], w[0:n, t.slot(B), i * P:(i + 1) * P],
                                                xn[0:n, t.slot(B), :], start=first and i % 2 == 0,
                                                stop=final and i % 2 == 1, skip_group_check=True)
                    last.then_inc(tokens_done, 1)

                if fused:
                    for t in steps(pe, -2, NT + 1, B, end=NT, behind=1, ahead=2):
                        at(t, 2, aggregate)
                        at(t, 1, turn)
                        at(t, 2, project)
                        at(t, 1, logits)
                        at(t, -1, tokens)
                else:
                    for t in steps(pe, -1, NT, B, end=NT, ahead=1):
                        at(t, 1, aggregate)
                        at(t, 0, project)

            @block.vector
            def _(dve):
                V = nc.vector

                def pick_others(t):
                    b = t.slot(B)
                    if t.reused(B):
                        dve.wait_ge(sums, t.plus(1 - B).n)
                    V.tensor_scalar(pick[:, b, :], iota[:, :P], k["slot_node"][:, bass.ds(t.n, 1)], None,
                                    ALU.is_equal).then_inc(picks, 1)

                def with_bias(t):
                    b = t.slot(2)
                    dve.wait_ge(outs_done, t.n + 1)
                    if t.reused(2) and not fused:
                        dve.wait_ge(y_done, t.plus(-1).n)
                    V.scalar_tensor_tensor(z[:, b, :], ps_out[b], dinv[:, bass.ds(t.n, 1)], k["b"], ALU.mult,
                                           ALU.add).then_inc(z_done, 1)

                def heads(ap):
                    return ap.rearrange("p (h c) -> p h c", c=C)

                def statistics(t):
                    with_bias(t)
                    b, q = t.slot(2), t.slot(B)
                    dve.wait_ge(z_done, t.n + 1)
                    dve.wait_ge(x_in[q], t.uses(B) * 16 + 16)
                    if t.reused(B):
                        dve.wait_ge(y_out[q], t.uses(B) * 16)
                    V.scalar_tensor_tensor(y[:, q, :], z[:, b, :], 0.0, xres[:, q, :], ALU.max,
                                           ALU.add).then_inc(y_done, 1)
                    dve.wait_ge(y_done, t.n + 1)
                    V.bn_stats(stats[:, b, :], y[:, q, :]).then_inc(stats_done, 1)
                    wait_apart(dve, stats_done, t.n + 1, c.passed)
                    V.bn_aggr(mv[:, b, :], stats[:, b, :]).then_inc(var_done, 1)

                def normalise(t):
                    b, q = t.slot(2), t.slot(B)
                    dve.wait_ge(rstd_done, t.n + 1)
                    if t.reused(B):
                        dve.wait_ge(tokens_done, t.plus(1 - B).n)
                    V.tensor_scalar(xn[:, q, :], y[:, q, :], mv[:, b, 0:1], rstd[:, b, :], ALU.subtract,
                                    ALU.mult).then_inc(xn_done, 1)

                def bias_and_max(t):
                    b = t.slot(2)
                    dve.wait_ge(logits_done, t.n + 1)
                    if t.reused(2):
                        dve.wait_ge(exp_done, t.plus(-1).n * H)
                    V.tensor_tensor(lg[:, b, :], ps_log[:], k["blog"][:], ALU.add).then_inc(biased, 1)
                    dve.wait_ge(biased, t.n + 1)
                    V.tensor_reduce(nmx[:, b, :], heads(lg[:, b, :]), AX.X, ALU.max, negate=True).then_inc(max_done, 1)

                def divide(t):
                    b, q = t.slot(2), t.slot(B)
                    dve.wait_ge(exp_done, (t.n + 1) * H)
                    V.reciprocal(rtot[:, b, :], tot[:, b, :]).then_inc(recip_done, 1)
                    dve.wait_ge(recip_done, t.n + 1)
                    if t.reused(B):
                        dve.wait_ge(w_out[q], t.uses(B) * 16)
                        dve.wait_ge(wsum_done, t.plus(1 - B).n + 1)
                        dve.wait_ge(tokens_done, t.plus(1 - B).n)
                    V.tensor_tensor(heads(w[:, q, :]), heads(ex[:, b, :]),
                                    rtot[:, b, :].unsqueeze(2).to_broadcast([P, H, C]), ALU.mult).then_inc(w_done, 1)

                if fused:
                    for t in steps(dve, -3, NT, B, end=NT, ahead=3):
                        at(t, 3, pick_others)
                        at(t, 2, statistics)
                        at(t, 1, bias_and_max)
                        at(t, 2, normalise)
                        at(t, 0, divide)
                    dve.wait_ge(tokens_done, NT)
                    for i in range(IC // 2):
                        last = V.tensor_copy(k["token_sum"][:, 2 * i:2 * i + 2, :], ps_tok[i])
                    last.then_inc(saved, 1)
                    dve.wait_ge(saved, 1)
                else:
                    for t in steps(dve, -2, NT, B, end=NT, ahead=2):
                        at(t, 2, pick_others)
                        at(t, 2, lambda u: scale_own(dve, V.tensor_scalar_mul, u))
                        at(t, 0, with_bias)

            @block.scalar
            def _(act):
                def copy_sums(t):
                    b = t.slot(2)
                    act.wait_ge(sums, t.n + 1)
                    if t.reused(2):
                        act.wait_ge(outs_done, t.plus(-1).n)
                    nc.scalar.activation(sumT[:, b, :], ps_sum[b], ACT.Copy).then_inc(sums_copied, 1)

                def relu(t):
                    b, q = t.slot(2), t.slot(B)
                    act.wait_ge(z_done, t.n + 1)
                    if t.reused(B):
                        act.wait_ge(y_out[q], t.uses(B) * 16)
                    nc.scalar.activation(y[:, q, :], z[:, b, :], ACT.Relu,
                                         scale=k["cinv"][:, bass.ds(t.n, 1)]).then_inc(y_done, 1)

                def copy_turned(t):
                    b = t.slot(2)
                    act.wait_ge(turned, t.n + 1)
                    if t.reused(2):
                        act.wait_ge(logits_done, t.plus(-1).n)
                    nc.scalar.activation(xnT[:, b, :], ps_T[:], ACT.Copy).then_inc(turned_copied, 1)

                def exponentials(t):
                    b = t.slot(2)
                    act.wait_ge(max_done, t.n + 1)
                    if t.reused(2):
                        act.wait_ge(w_done, t.plus(-1).n)
                    for h in range(H):
                        part = slice(h * C, (h + 1) * C)
                        nc.scalar.activation(ex[:, b, part], lg[:, b, part], ACT.Exp, bias=nmx[:, b, h:h + 1],
                                             accum_out=tot[:, b, h:h + 1]).then_inc(exp_done, 1)

                def scale(to, frm, by):
                    return nc.scalar.activation(to, frm, ACT.Copy, scale=by)

                act.wait_ge(cleared, B + 1)
                if fused:
                    for t in steps(act, -3, NT, B, end=NT, ahead=3):
                        at(t, 3, lambda u: scale_own(act, scale, u))
                        at(t, 2, copy_sums)
                        at(t, 1, copy_turned)
                        at(t, 0, exponentials)
                else:
                    for t in steps(act, -1, NT, B, end=NT, ahead=1):
                        at(t, 1, copy_sums)
                        at(t, 0, relu)


def slices(nc, k, sb, ps, sem):
    D, FC, H, C, IC, INNER = (k[n] for n in ("D", "FC", "H", "C", "IC", "INNER"))
    ident, ones, token_sum = k["ident"], k["ones"], k["token_sum"]
    with Phase(nc) as c:
        norm = sb("s_norm", [P, IC], c=c)
        rnorm = sb("s_rnorm", [P, IC], c=c)
        norm_row = sb("s_norm_row", [1, INNER], c=c)
        ratio_row = sb("s_ratio_row", [1, INNER], c=c)
        sumsT = sb("s_sumsT", [P, FC, INNER], c=c)
        tokT = sb("s_tokT", [C, INNER], c=c)
        qT = sb("s_qT", [C, INNER], c=c)
        kT = sb("s_kT", [C, INNER], c=c)
        v = sb("s_v", [C, INNER], c=c)
        score = sb("s_score", [C, INNER], c=c)
        big = sb("s_big", [C, H], c=c)
        total = sb("s_total", [C, H], c=c)
        attnT = sb("s_attnT", [C, INNER], c=c)
        oT = sb("s_oT", [C, INNER], c=c)
        pa = ps("s_pa", [P, INNER], c=c)
        pb = ps("s_pb", [P, INNER], c=c)
        pc = ps("s_pc", [P, INNER], c=c)
        pe_done = sem("s_pe", c)
        v_done = sem("s_v_done", c)
        a_done = sem("s_a_done", c)

        def head(ap, h):
            return ap[:, h * C:(h + 1) * C]
        with nc.Block() as block:
            @block.tensor
            def _(pe):
                T = nc.tensor
                for i in range(IC):
                    last = T.matmul(pa[:, i:i + 1], k["weight_sum"][:, i * P:(i + 1) * P], ones[:, 0:1],
                                    start=True, stop=True)
                last.then_inc(pe_done, 1)
                T.matmul(pb[0:1, :], ones[:, 0:1], k["weight_sum"][:], start=True, stop=True).then_inc(pe_done, 1)
                pe.wait_ge(v_done, 7)
                for f in range(FC):
                    if f:
                        pe.wait_ge(v_done, 7 + f)
                    for i in range(IC):
                        last = T.transpose(pc[:, i * P:(i + 1) * P], token_sum[:, i, f * P:(f + 1) * P], ident[:])
                    last.then_inc(pe_done, 1)
                pe.wait_ge(v_done, 7 + FC)
                for h in range(H):
                    part = slice(h * C, (h + 1) * C)
                    for f in range(FC):
                        T.matmul(pa[0:C, part], k["wfx_sb"][:, f, part], sumsT[:, f, part], start=(f == 0), stop=False)
                    last = T.matmul(pa[0:C, part], k["bfx_sb"][:, part], ratio_row[:, part], start=False, stop=True)
                last.then_inc(pe_done, 1)
                pe.wait_ge(v_done, 8 + FC)
                T.matmul(pb[0:C, :], k["wqkv_sb"][:, 0, :], tokT[:], start=True, stop=True).then_inc(pe_done, 1)
                T.matmul(pc[0:C, :], k["wqkv_sb"][:, 1, :], tokT[:], start=True, stop=True).then_inc(pe_done, 1)
                for h in range(H):
                    last = T.matmul(head(pa[0:C, :], h), head(tokT, h), k["wqkv_sb"][:, 2, :], start=True, stop=True)
                last.then_inc(pe_done, 1)
                pe.wait_ge(v_done, 11 + FC)
                for h in range(H):
                    last = T.matmul(head(pb[0:C, :], h), head(qT, h), head(kT, h), start=True, stop=True)
                last.then_inc(pe_done, 1)
                pe.wait_ge(v_done, 16 + FC)
                for h in range(H):
                    last = T.transpose(head(pc[0:C, :], h), head(score, h), ident[0:C, 0:C])
                last.then_inc(pe_done, 1)
                pe.wait_ge(v_done, 17 + FC)
                for h in range(H):
                    last = T.matmul(head(pa[0:C, :], h), head(v, h), head(attnT, h), start=True, stop=True)
                last.then_inc(pe_done, 1)
                pe.wait_ge(v_done, 18 + FC)
                for i in range(IC):
                    if i:
                        pe.wait_ge(v_done, 18 + FC + i)
                    for j in range(2):
                        h = 2 * i + j
                        last = T.matmul(pb[j * C:(j + 1) * C, 0:D], head(oT, h), k["wout_sb"][:, h, :],
                                        start=True, stop=True)
                    last.then_inc(pe_done, 1)

            @block.vector
            def _(dve):
                V = nc.vector
                ch = Chain(dve, v_done)
                dve.wait_ge(pe_done, 2)
                ch.mark(V.tensor_copy(norm_row[:], pb[0:1, :]))
                ch.link(V.tensor_scalar(norm[:], pa[:, 0:IC], EPS, None, ALU.add))
                ch.mark(V.reciprocal(rnorm[:], norm[:]))
                ch.link(V.tensor_scalar(ratio_row[:], norm_row[:], EPS, None, ALU.add))
                ch.link(V.reciprocal(ratio_row[:], ratio_row[:]))
                ch.link(V.tensor_tensor(ratio_row[:], ratio_row[:], norm_row[:], ALU.mult))
                ch.link(V.tensor_tensor(token_sum[:], token_sum[:], rnorm[:].unsqueeze(2).to_broadcast([P, IC, D]), ALU.mult))
                for f in range(FC):
                    dve.wait_ge(pe_done, 3 + f)
                    ch.link(V.tensor_copy(sumsT[:, f, :], pc[:]))
                dve.wait_ge(pe_done, 3 + FC)
                ch.link(V.tensor_copy(tokT[:], pa[0:C, :]))
                dve.wait_ge(pe_done, 6 + FC)
                ch.mark(V.tensor_copy(qT[:], pb[0:C, :]))
                ch.mark(V.tensor_copy(kT[:], pc[0:C, :]))
                ch.link(V.tensor_copy(v[:], pa[0:C, :]))
                dve.wait_ge(pe_done, 7 + FC)

                def heads(ap):
                    return ap.rearrange("p (h c) -> p h c", c=C)

                def wide(ap):
                    return ap[:].unsqueeze(2).to_broadcast([C, H, C])
                ch.link(V.tensor_reduce(big[:], heads(pb[0:C, :]), AX.X, ALU.max))
                ch.link(V.tensor_tensor(heads(score[:]), heads(pb[0:C, :]), wide(big), ALU.subtract))
                dve.wait_ge(a_done, 1)
                ch.link(V.tensor_reduce(total[:], heads(score[:]), AX.X, ALU.add))
                ch.link(V.reciprocal(total[:], total[:]))
                ch.link(V.tensor_tensor(heads(score[:]), heads(score[:]), wide(total), ALU.mult))
                dve.wait_ge(pe_done, 8 + FC)
                ch.link(V.tensor_copy(attnT[:], pc[0:C, :]))
                dve.wait_ge(pe_done, 9 + FC)
                ch.link(V.tensor_copy(oT[:], pa[0:C, :]))
                for i in range(IC):
                    dve.wait_ge(pe_done, 10 + FC + i)
                    ch.link(V.tensor_copy(k["mix"][:, i, :], pb[:, 0:D]))

            @block.scalar
            def _(act):
                act.wait_ge(v_done, 13 + FC)
                nc.scalar.activation(score[:], score[:], ACT.Exp, scale=k["SCALE"]).then_inc(a_done, 1)


def spread_back(nc, k, sb, ps, sem):
    NT, D, IC, INNER, LAST = (k[n] for n in ("NT", "D", "IC", "INNER", "LAST"))
    with Phase(nc) as c:
        w = sb("o_w", [P, 4, INNER], c=c)
        x2 = sb("o_x2", [P, 4, D], c=c)
        wT = sb("o_wT", [P, 2, INNER], c=c)
        xb = sb("o_xb", [P, 2, D], c=c)
        o = sb("o_o", [P, 4, D], c=c)
        ps_T = [ps(f"o_psT{i}", [P, INNER], c=c) for i in range(2)]
        ps_o = [ps(f"o_ps{i}", [P, D], c=c) for i in range(2)]
        w_in = [sem(f"o_w_in{i}", c) for i in range(4)]
        x_in = [sem(f"o_x_in{i}", c) for i in range(4)]
        o_out = [sem(f"o_out{i}", c) for i in range(4)]
        turned = sem("o_turned", c)
        copied = sem("o_copied", c)
        mixed = sem("o_mixed", c)
        biased = sem("o_biased", c)
        o_done = sem("o_done", c)
        U = 4
        with nc.Block() as block:
            @block.sync
            def _(sp):
                for t in steps(sp, 0, NT, U):
                    b = t.slot(4)
                    if t.reused(4):
                        sp.wait_ge(turned, t.plus(-3).n)
                        sp.wait_ge(biased, t.plus(-3).n)
                    sp.dma_start(w[:, b, :], tile_rows(k["w_dram"], t)).then_inc(w_in[b], 16)
                    sp.dma_start(x2[:, b, :], tile_rows(k["x2_dram"], t)).then_inc(x_in[b], 16)

            @block.tensor
            def _(pe):
                def turn(t):
                    b = t.slot(2)
                    pe.wait_ge(w_in[t.slot(4)], t.uses(4) * 16 + 16)
                    if t.reused(2):
                        pe.wait_ge(copied, t.plus(-1).n)
                    for i in range(IC):
                        part = slice(i * P, (i + 1) * P)
                        last = nc.tensor.transpose(ps_T[b][:, part], w[:, t.slot(4), part], k["ident"][:])
                    last.then_inc(turned, 1)

                def mixing(t):
                    b = t.slot(2)
                    pe.wait_ge(copied, t.n + 1)
                    if t.reused(2):
                        pe.wait_ge(o_done, t.plus(-1).n)
                    for i in range(IC):
                        last = nc.tensor.matmul(ps_o[b][:], wT[:, b, i * P:(i + 1) * P], k["mix"][:, i, :],
                                                start=(i == 0), stop=(i == IC - 1))
                    last.then_inc(mixed, 1)
                turn(Turn(None, 0, U, NT))
                for t in steps(pe, 0, NT - 1, U):
                    turn(t.plus(1))
                    mixing(t)
                mixing(Turn(None, NT - 1, U, NT))

            @block.scalar
            def _(act):
                def copy(t):
                    b = t.slot(2)
                    act.wait_ge(turned, t.n + 1)
                    if t.reused(2):
                        act.wait_ge(mixed, t.plus(-1).n)
                    nc.scalar.activation(wT[:, b, :], ps_T[b][:], ACT.Copy).then_inc(copied, 1)

                def store(t, n=P):
                    b = t.slot(4)
                    act.wait_ge(o_done, t.n + 1)
                    act.dma_start(tile_rows(k["out"], t, n), o[0:n, b, :]).then_inc(o_out[b], 16)
                copy(Turn(None, 0, U, NT))
                for t in steps(act, 0, NT - 1, U):
                    copy(t.plus(1))
                    store(t)
                store(Turn(None, NT - 1, U, NT), LAST)
                for b in range(4):
                    act.wait_ge(o_out[b], 16 * (-(-(NT - b) // 4)))

            @block.vector
            def _(dve):
                def bias(t):
                    dve.wait_ge(x_in[t.slot(4)], t.uses(4) * 16 + 16)
                    if t.reused(2):
                        dve.wait_ge(o_done, t.plus(-1).n)
                    nc.vector.tensor_tensor(xb[:, t.slot(2), :], x2[:, t.slot(4), :], k["bout_sb"][:],
                                            ALU.add).then_inc(biased, 1)

                def add(t):
                    dve.wait_ge(mixed, t.n + 1)
                    dve.wait_ge(biased, t.n + 1)
                    if t.reused(4):
                        dve.wait_ge(o_out[t.slot(4)], t.uses(4) * 16)
                    nc.vector.tensor_tensor(o[:, t.slot(4), :], ps_o[t.slot(2)][:], xb[:, t.slot(2), :],
                                            ALU.add).then_inc(o_done, 1)
                for t in steps(dve, 0, NT, U):
                    bias(t)
                    add(t)


_INS = ["x", "src", "dst", "L0_gnn_W0", "L0_gnn_b0", "L0_gnn_W1", "L0_gnn_b1", "L0_gnn_W2", "L0_gnn_b2",
        "L0_ffn_W_fx", "L0_ffn_b_fx", "L0_ffn_W_x", "L0_ffn_b_x", "L0_ffn_W_slice", "L0_ffn_b_slice",
        "L0_ffn_W_q", "L0_ffn_W_k", "L0_ffn_W_v", "L0_ffn_W_out", "L0_ffn_b_out", "L0_ffn_temperature"]


def _program(nc, shapes):
    a = {n: nc.dram_tensor(f"in_{n}", s, d, kind="ExternalInput").ap() for n, (s, d) in shapes.items()}
    out = nc.dram_tensor("out_0", shapes["x"][0], FP32, kind="ExternalOutput").ap()
    f = lambda n: a["L0_ffn_" + n]
    gnn_ffn(nc, a["x"], a["src"], a["dst"], [a[f"L0_gnn_W{l}"] for l in range(3)],
            [a[f"L0_gnn_b{l}"] for l in range(3)], f("W_fx"), f("b_fx"), f("W_x"), f("b_x"), f("W_slice"),
            f("b_slice"), f("W_q"), f("W_k"), f("W_v"), f("W_out"), f("b_out"), f("temperature"), out)


def kernel(**inputs):
    import numpy as _np
    import concourse.bacc as _bacc
    from concourse import mybir as _mybir
    from concourse.bass_utils import run_bass_kernel_spmd as _run

    nc = _bacc.Bacc("TRN2", target_bir_lowering=False, num_devices=1)
    arrays = {n: _np.ascontiguousarray(inputs[n]) for n in _INS}
    _program(nc, {n: (v.shape, _mybir.dt.from_np(v.dtype)) for n, v in arrays.items()})
    r = _run(nc, [{f"in_{n}": v for n, v in arrays.items()}], core_ids=[0])
    return r.results[0]["out_0"]
```

```python
import concourse.bass as bass
from concourse import mybir
from contextlib import ExitStack

P = 128
FP32 = mybir.dt.float32
FP32R = mybir.dt.float32r
FP16 = mybir.dt.float16
I32 = mybir.dt.int32
ALU = mybir.AluOpType
ACT = mybir.ActivationFunctionType
AX = mybir.AxisListType
BANK = 512
PAD = 1 << 16
EPS = 1e-5


class Turn:

    def __init__(self, g, at, unroll, end):
        self.g, self.at, self.unroll, self.end = g, at, unroll, end
        self.n = at if g is None else g * unroll + at

    def plus(self, d):
        return Turn(self.g, self.at + d, self.unroll, self.end)

    def slot(self, buffers):
        return self.at % buffers

    def uses(self, buffers):
        before = self.at // buffers
        return before if self.g is None else self.g * (self.unroll // buffers) + before

    def reused(self, buffers):
        return self.at >= buffers

    def exists(self):
        return self.g is not None or 0 <= self.at < self.end

    def rows(self, last):
        return last if self.g is None and self.at == self.end - 1 else P


BUFFERS = 4


def steps(eng, lo, hi, unroll, end=None, behind=0, ahead=0, buffers=BUFFERS):
    end = hi if end is None else end
    first = min(max(lo, buffers + behind), hi)
    rounds = max(min(hi, end - 1 - ahead) - first, 0) // unroll
    rounds = rounds if rounds > 1 else 0
    for n in range(lo, first):
        yield Turn(None, n, unroll, end)
    if rounds:
        with eng.Fori(0, rounds) as g:
            for u in range(unroll):
                yield Turn(g, first + u, unroll, end)
    for n in range(first + rounds * unroll, hi):
        yield Turn(None, n, unroll, end)


def at(t, d, op):
    if t.plus(d).exists():
        op(t.plus(d))


class Chain:

    def __init__(self, eng, sem):
        self.eng, self.sem, self.base, self.count = eng, sem, 0, 0

    def at(self, base):
        self.base, self.count = base, 0

    def link(self, ins):
        self.mark(ins)
        self.wait()

    def mark(self, ins):
        self.count += 1
        ins.then_inc(self.sem, 1)

    def wait(self):
        self.eng.wait_ge(self.sem, self.base + self.count)


class Phase(ExitStack):

    count = 0

    def __init__(self, nc):
        super().__init__()
        self.nc, self.semaphores = nc, []
        Phase.count += 1
        self.number = Phase.count
        self.passed = nc.alloc_semaphore(f"passed_{self.number}")
        self.semaphores.append(self.passed)

    def __exit__(self, *error):
        done = super().__exit__(*error)
        if error[0] is None:
            self.nc.clear_and_free_semaphores(self.semaphores)
            self.nc.all_engine_barrier()
        return done


def wait_apart(eng, sem, value, passed):
    eng.wait_ge(sem, value)
    eng.sem_inc(passed, 1)


def spread(ap, shape_ap):
    return bass.AP(ap.tensor, ap.offset, [[0, P]] + list(shape_ap))


def gnn_ffn(nc, x, src, dst, gw, gb, W_fx, b_fx, W_x, b_x, W_slice, b_slice, W_q, W_k, W_v,
            W_out, b_out, temperature, out):
    Phase.count = 0
    N, D = x.shape
    E = src.shape[0]
    NT = -(-N // P)
    NP = NT * P
    LAST = N - (NT - 1) * P
    FC = D // P
    INNER = W_fx.shape[1]
    H = temperature.shape[1]
    C = INNER // H
    IC = INNER // P
    KE = -(-E // P)
    KE += -KE % 4
    EFULL, EREST = E // KE, E % KE
    LAYERS = len(gw)
    SCALE = float(C) ** -0.5
    assert D == 256 and C == 64 and INNER == 512 and NT <= 391 + 120 and NT > 12
    assert N < NP

    tables = [nc.dram_tensor(f"features_{l}", (NP, D), FP32).ap() for l in range(LAYERS)]
    node_sums = nc.dram_tensor("node_sums", (NP + P, D), FP32).ap()
    x2_dram = nc.dram_tensor("x2_rows", (NP, D), FP32).ap()
    w_dram = nc.dram_tensor("slice_weights", (NP, INNER), FP32).ap()
    dinv_dram = nc.dram_tensor("dinv_rows", (NP, 1), FP32).ap()

    def rows(ap, t, count=P):
        return ap[bass.ds(t.n * P, count), :]

    ctx = ExitStack()
    with ctx:
        def sb(name, shape, dt=FP32, c=ctx):
            name = f"{name}_{c.number}" if c is not ctx else name
            return c.enter_context(nc.sbuf_tensor(name, shape, dt))

        def ps(name, shape, c):
            bank = c.enter_context(nc.psum_tensor(f"{name}_{c.number}", [P, BANK], FP32))
            if len(shape) == 3:
                return bank[:, :shape[1] * shape[2]].rearrange("p (a b) -> p a b", b=shape[2])
            return bank[:shape[0], :shape[1]]

        def sem(name, phase):
            handle = nc.alloc_semaphore(f"{name}_{phase.number}")
            phase.semaphores.append(handle)
            return handle

        ident = sb("ident", [P, P])
        W = max(NT, P)
        iota_i = sb("iota_i", [P, W], I32)
        iota = sb("iota", [P, W])
        iota_h = sb("iota_h", [P, W], FP16)
        before_h = sb("before_h", [P, P], FP16)
        not_before_h = sb("not_before_h", [P, P], FP16)
        ones_h = sb("ones_h", [P, P], FP16)
        zero_h = sb("zero_h", [P, P], FP16)
        ones = sb("ones", [P, P])
        earlier = sb("earlier", [P, P])
        minus_half = sb("minus_half", [P, NT])
        eps = sb("eps", [P, 1])
        lane = sb("lane", [P, 1])
        lane_i = sb("lane_i", [P, 1], I32)

        gw_sb = sb("gw_sb", [P, LAYERS, FC, D])
        gw_last = [sb(f"gw_last_{part}", [P, FC, D], FP32R) for part in ("high", "low")]
        gb_sb = sb("gb_sb", [P, LAYERS, D])
        wfx_sb = sb("wfx_sb", [P, FC, INNER])
        bfx_sb = sb("bfx_sb", [1, INNER])
        wx_sb = sb("wx_sb", [P, FC, INNER])
        bx_sb = sb("bx_sb", [C, H])
        wslice_sb = sb("wslice_sb", [C, C])
        bslice_sb = sb("bslice_sb", [P, C])
        wqkv_sb = sb("wqkv_sb", [C, 3, C])
        wout_sb = sb("wout_sb", [C, H, D])
        bout_sb = sb("bout_sb", [P, D])
        temp_sb = sb("temp_sb", [P, H])
        rtemp = sb("rtemp", [P, H])
        wlog = [sb(f"wlog_{part}", [P, FC, INNER], FP32R) for part in ("high", "low")]
        mix = [sb(f"mix_{part}", [P, IC, D], FP32R) for part in ("high", "low")]
        blog = sb("blog", [P, INNER])
        wxT = sb("wxT", [C, FC, H, P])
        bxw = sb("bxw", [C, H, P])

        dinv = sb("dinv", [P, NT])
        cinv = sb("cinv", [P, NT])
        selfs = sb("selfs", [P, NT])
        slot_row = sb("slot_row", [P, NT], I32)
        slot_node = sb("slot_node", [P, NT])
        slot_tile = sb("slot_tile", [P, NT])
        slot_lane = sb("slot_lane", [P, NT])
        src_i = sb("src_i", [P, KE], I32)
        dst_i = sb("dst_i", [P, KE], I32)
        src_f = sb("src_f", [P, KE])
        dst_f = sb("dst_f", [P, KE])
        other = sb("other", [P, KE])
        overflow_i = sb("overflow_i", [P, 1], I32)
        token_sum = sb("token_sum", [P, IC, D])
        weight_sum = sb("weight_sum", [P, INNER])

        with Phase(nc) as c:
            loaded = sem("weights_loaded", c)
            made = sem("constants_made", c)
            xT_done = sem("wx_transposed", c)
            xT_copied = sem("wx_transposes_copied", c)
            log_done = sem("slice_products", c)
            v_ch = sem("vector_chain_w", c)
            psT = [ps(f"psT{i}", [C, P], c=c) for i in range(2)]
            psW = ps("psW", [P, INNER], c=c)
            psB = ps("psB", [P, INNER], c=c)
            product = sb("slice_product", [P, FC, INNER], c=c)
            LOADS = 0
            with nc.Block() as block:
                pairs = []
                for l in range(LAYERS):
                    pairs.append((gw_sb[:, l, :, :], gw[l].rearrange("(f p) n -> p f n", p=P)))
                    pairs.append((gb_sb[:, l, :], spread(gb[l], [[1, D]])))
                pairs += [
                    (wfx_sb[:], W_fx.rearrange("(f p) n -> p f n", p=P)),
                    (bfx_sb[:], b_fx.rearrange("(a n) -> a n", a=1)),
                    (wx_sb[:], W_x.rearrange("(f p) n -> p f n", p=P)),
                    (wslice_sb[:], W_slice), (bslice_sb[:], spread(b_slice, [[1, C]])),
                    (wqkv_sb[:, 0, :], W_q), (wqkv_sb[:, 1, :], W_k), (wqkv_sb[:, 2, :], W_v),
                    (wout_sb[:], W_out.rearrange("(h c) n -> c h n", c=C)),
                    (bout_sb[:], spread(b_out, [[1, D]])),
                    (temp_sb[:], spread(temperature, [[1, H]])),
                ]
                LOADS = 16 * (len(pairs) + 1)

                @block.sync
                def _(sp):
                    for to, frm in pairs:
                        sp.dma_start(to, frm).then_inc(loaded, 16)
                    with nc.allow_non_contiguous_dma("one small vector, once"):
                        sp.dma_start(bx_sb[:], b_x.rearrange("(h c) -> c h", c=C)).then_inc(loaded, 16)
                    sp.wait_ge(loaded, LOADS)

                @block.gpsimd
                def _(pool):
                    ch = Chain(pool, made)
                    ch.mark(nc.gpsimd.iota(iota_i[:], pattern=[[1, W]], base=0, channel_multiplier=0))
                    ch.mark(nc.gpsimd.iota(lane_i[:], pattern=[[0, 1]], base=0, channel_multiplier=1))
                    for t, v in ((ident, 0.0), (ones_h, 1.0), (zero_h, 0.0), (ones, 1.0), (earlier, 1.0),
                                 (before_h, 1.0), (not_before_h, 1.0), (minus_half, -0.5), (eps, EPS)):
                        ch.mark(nc.gpsimd.memset(t[:], v))
                    ch.wait()
                    ch.mark(nc.gpsimd.tensor_copy(iota[:], iota_i[:]))
                    ch.mark(nc.gpsimd.tensor_copy(iota_h[:], iota_i[:]))
                    ch.mark(nc.gpsimd.tensor_copy(lane[:], lane_i[:]))
                    ch.mark(nc.gpsimd.affine_select(out=ident[:], in_=ident[:], compare_op=ALU.not_equal,
                                                    fill=1.0, base=0, pattern=[[-1, P]], channel_multiplier=1))
                    ch.mark(nc.gpsimd.affine_select(out=before_h[:], in_=before_h[:], compare_op=ALU.is_gt,
                                                    fill=0.0, base=0, pattern=[[1, P]], channel_multiplier=-1))
                    ch.mark(nc.gpsimd.affine_select(out=not_before_h[:], in_=not_before_h[:],
                                                    compare_op=ALU.is_ge, fill=0.0, base=0,
                                                    pattern=[[-1, P]], channel_multiplier=1))
                    ch.mark(nc.gpsimd.affine_select(out=earlier[:], in_=earlier[:], compare_op=ALU.is_gt,
                                                    fill=0.0, base=0, pattern=[[-1, P]], channel_multiplier=1))
                    ch.wait()

                MADE = 18

                @block.tensor
                def _(pe):
                    pe.wait_ge(loaded, LOADS)
                    pe.wait_ge(made, MADE)
                    n = 0
                    for f in range(FC):
                        for h in range(H):
                            if n >= 2:
                                pe.wait_ge(xT_copied, n)
                            nc.tensor.transpose(psT[n % 2][:], wx_sb[:, f, h * C:(h + 1) * C],
                                                ident[:]).then_inc(xT_done, 1)
                            n += 1
                    pe.wait_ge(xT_copied, FC * H + 1)
                    for h in range(H):
                        nc.tensor.matmul(psB[:, h * C:(h + 1) * C], bxw[:, h, :], wslice_sb[:],
                                         start=True, stop=True).then_inc(log_done, 1)
                    for f in range(FC):
                        if f:
                            pe.wait_ge(v_ch, 3 + f)
                        for h in range(H):
                            nc.tensor.matmul(psW[:, h * C:(h + 1) * C], wxT[:, f, h, :], wslice_sb[:],
                                             start=True, stop=True).then_inc(log_done, 1)

                @block.vector
                def _(dve):
                    dve.wait_ge(loaded, LOADS)
                    dve.wait_ge(made, MADE)
                    nc.vector.tensor_copy(bxw[:], bx_sb[:].unsqueeze(2).to_broadcast([C, H, P])).then_inc(xT_copied, 1)
                    n = 0
                    for f in range(FC):
                        for h in range(H):
                            dve.wait_ge(xT_done, n + 1)
                            nc.vector.tensor_copy(wxT[:, f, h, :], psT[n % 2][:]).then_inc(xT_copied, 1)
                            n += 1
                    ch = Chain(dve, v_ch)
                    ch.link(nc.vector.tensor_scalar(rtemp[:], temp_sb[:], 0.1, 5.0, ALU.max, ALU.min))
                    ch.link(nc.vector.reciprocal(rtemp[:], rtemp[:]))
                    scale = rtemp[:].unsqueeze(2).to_broadcast([P, H, C])

                    def heads(ap):
                        return ap.rearrange("p (h c) -> p h c", c=C)
                    dve.wait_ge(log_done, H)
                    ch.link(nc.vector.tensor_tensor(heads(blog[:]), heads(psB[:]),
                                                    bslice_sb[:].unsqueeze(1).to_broadcast([P, H, C]), ALU.add))
                    for f in range(FC):
                        dve.wait_ge(log_done, H + (f + 1) * H)
                        ch.link(nc.vector.tensor_tensor(heads(product[:, f, :]), heads(psW[:]), scale, ALU.mult))
                    ch.link(nc.vector.tensor_tensor(heads(blog[:]), heads(blog[:]), scale, ALU.mult))
                    ch.link(nc.vector.tensor_copy(gw_last[0][:], gw_sb[:, LAYERS - 1, :, :]))
                    ch.link(nc.vector.tensor_tensor(gw_last[1][:], gw_sb[:, LAYERS - 1, :, :], gw_last[0][:],
                                                    ALU.subtract))
                    ch.link(nc.vector.tensor_copy(wlog[0][:], product[:]))
                    ch.link(nc.vector.tensor_tensor(wlog[1][:], product[:], wlog[0][:], ALU.subtract))

        with Phase(nc) as c:
            slot_keys = [sb(f"slot_keys{i}", [P, NT], c=c) for i in range(2)]
            deg = sb("deg", [P, NT], c=c)
            src_tile = sb("src_tile", [P, KE], c=c)
            src_lane = sb("src_lane", [P, KE], c=c)
            own_edge = sb("own_edge", [P, KE], c=c)
            key1 = sb("key1", [P, KE], c=c)
            key2 = sb("key2", [P, KE], c=c)
            scratch_i = sb("scratch_i", [P, KE], I32, c)
            scratch_f = sb("scratch_f", [P, KE], c=c)
            tile_hot = sb("tile_hot", [P, 4, NT], FP16, c)
            lane_hot = sb("lane_hot", [P, 4, P], FP16, c)
            self_hot = sb("self_hot", [P, 4, P], FP16, c)
            other_hot = sb("other_hot", [P, 4, NT], FP16, c)
            lane_col = sb("lane_col", [P, 4], c=c)
            rank = sb("rank", [P, 2], c=c)
            picked = sb("picked", [P, 2, NT], c=c)
            rank_key1 = sb("rank_key1", [P, 2, P], FP16, c)
            rank_key2 = sb("rank_key2", [P, 2, P], FP16, c)
            counts = sb("counts", [P, NT], c=c)
            most = sb("most", [P, 1], c=c)
            over = sb("over", [P, 1], c=c)
            dec = [sb(f"dec{i}", [P, NT], I32, c) for i in range(3)]
            valid = sb("valid", [P, NT], c=c)
            fa = sb("fa", [P, NT], c=c)
            fb = sb("fb", [P, NT], c=c)
            ps_rank = [ps(f"ps_rank{i}", [P, NT], c=c) for i in range(2)]
            ps_deg = ps("ps_deg", [P, NT], c=c)
            ps_self = ps("ps_self", [P, NT], c=c)
            ps_key = [ps(f"ps_key{i}", [P, NT], c=c) for i in range(2)]

            cleared = sem("edges_cleared", c)
            edges_in = sem("edges_in", c)
            split = sem("edges_split", c)
            tile_hot_made = sem("tile_hot_made", c)
            lane_hot_made = sem("lane_hot_made", c)
            lane_col_made = sem("lane_col_made", c)
            self_hot_made = sem("self_hot_made", c)
            other_hot_made = sem("other_hot_made", c)
            ranked = sem("prefix_in_psum", c)
            rank_read = sem("rank_read", c)
            keys_made = sem("rank_keys_made", c)
            counted = sem("column_counted", c)
            swept = sem("sweep_done", c)
            v_ch = sem("vector_chain_e", c)

            with nc.Block() as block:
                @block.gpsimd
                def _(pool):
                    nc.gpsimd.memset(src_i[:], PAD).then_inc(cleared, 1)
                    nc.gpsimd.memset(dst_i[:], PAD).then_inc(cleared, 1)
                    pool.wait_ge(split, 1)
                    for t in steps(pool, 0, KE, 4):
                        b = t.slot(4)
                        if t.reused(4):
                            wait_apart(pool, counted, t.plus(-3).n, c.passed)
                        nc.gpsimd.tensor_copy(lane_col[:, b:b + 1], src_lane[:, bass.ds(t.n, 1)]).then_inc(lane_col_made, 1)
                        wait_apart(pool, lane_col_made, t.n + 1, c.passed)
                        nc.gpsimd.tensor_scalar(lane_hot[:, b, :], iota[:, :P], lane_col[:, b:b + 1], None,
                                                ALU.is_equal).then_inc(lane_hot_made, 1)

                @block.sync
                def _(sp):
                    sp.wait_ge(cleared, 2)
                    for to, frm in ((src_i, src), (dst_i, dst)):
                        sp.dma_start(to[0:EFULL, :], frm[0:EFULL * KE].rearrange("(p k) -> p k", k=KE)).then_inc(edges_in, 16)
                        if EREST:
                            sp.dma_start(to[EFULL:EFULL + 1, 0:EREST],
                                         frm[EFULL * KE:E].rearrange("(a k) -> a k", a=1)).then_inc(edges_in, 16)
                    sp.wait_ge(edges_in, 64 if EREST else 32)

                @block.scalar
                def _(act):
                    act.wait_ge(split, 1)
                    for t in steps(act, 0, KE, 4):
                        b = t.slot(4)
                        if t.reused(4):
                            act.wait_ge(counted, t.plus(-3).n)
                        act.wait_ge(tile_hot_made, t.n + 1)
                        nc.scalar.activation(other_hot[:, b, :], tile_hot[:, b, :], ACT.Copy,
                                             scale=other[:, bass.ds(t.n, 1)]).then_inc(other_hot_made, 1)
                        act.wait_ge(lane_hot_made, t.n + 1)
                        nc.scalar.activation(self_hot[:, b, :], lane_hot[:, b, :], ACT.Copy,
                                             scale=own_edge[:, bass.ds(t.n, 1)]).then_inc(self_hot_made, 1)

                @block.tensor
                def _(pe):
                    pe.wait_ge(split, 1)
                    for bank in (*ps_rank, ps_deg, ps_self, *ps_key):
                        nc.tensor.matmul(bank[:], zero_h[:], iota_h[:, :NT], start=True, stop=False,
                                         skip_group_check=True)

                    def add(bank, lhs, rhs):
                        return nc.tensor.matmul(bank[:], lhs, rhs, start=False, stop=False, skip_group_check=True)

                    def count(t):
                        q, hot = t.slot(4), tile_hot[:, t.slot(4), :]
                        pe.wait_ge(other_hot_made, t.n + 1)
                        add(ps_rank[t.slot(2)], before_h[:], other_hot[:, q, :]).then_inc(ranked, 1)
                        pe.wait_ge(tile_hot_made, t.n + 1)
                        pe.wait_ge(lane_hot_made, t.n + 1)
                        add(ps_deg, lane_hot[:, q, :], hot)
                        pe.wait_ge(self_hot_made, t.n + 1)
                        add(ps_self, self_hot[:, q, :], hot)

                    def finish(t):
                        b, q = t.slot(2), t.slot(4)
                        pe.wait_ge(rank_read, t.n + 1)
                        add(ps_rank[b], not_before_h[:], other_hot[:, q, :])
                        if t.plus(1).exists():
                            q1 = t.plus(1).slot(4)
                            add(ps_rank[b], ones_h[:], other_hot[:, q1, :])
                        pe.wait_ge(keys_made, (t.n + 1) * 2)
                        add(ps_key[0], rank_key1[:, b, :], tile_hot[:, q, :])
                        add(ps_key[1], rank_key2[:, b, :], tile_hot[:, q, :]).then_inc(counted, 1)

                    for t in steps(pe, 0, KE + 1, 4, end=KE, behind=1):
                        at(t, 0, count)
                        if t.g is None and t.at == 0:
                            add(ps_rank[1], ones_h[:], other_hot[:, 0, :])
                        at(t, -1, finish)
                    for bank in (*ps_rank, ps_deg, ps_self, *ps_key):
                        last = nc.tensor.matmul(bank[:], zero_h[:], iota_h[:, :NT], start=False, stop=True,
                                                skip_group_check=True)
                    last.then_inc(swept, 1)

                @block.vector
                def _(dve):
                    ch = Chain(dve, v_ch)
                    dve.wait_ge(edges_in, 64 if EREST else 32)
                    V = nc.vector

                    def part(to, frm, op0, a, op1=None, b=None):
                        ch.link(V.tensor_scalar(scratch_i[:], frm[:], a, b, op0, *((op1,) if op1 else ())))
                        ch.link(V.tensor_copy(to[:], scratch_i[:]))
                    ch.link(V.tensor_copy(src_f[:], src_i[:]))
                    ch.link(V.tensor_copy(dst_f[:], dst_i[:]))
                    ch.link(V.tensor_tensor(other[:], src_f[:], dst_f[:], ALU.not_equal))
                    part(src_tile, src_i, ALU.logical_shift_right, 7)
                    part(src_lane, src_i, ALU.bitwise_and, P - 1)
                    ch.link(V.tensor_scalar(own_edge[:], other[:], -1.0, 1.0, ALU.mult, ALU.add))
                    part(key1, dst_i, ALU.logical_shift_right, 7)
                    part(key2, src_i, ALU.logical_shift_right, 5, ALU.bitwise_and, 3)
                    ch.link(V.scalar_tensor_tensor(key1[:], key1[:], 4.0, key2[:], ALU.mult, ALU.add))
                    ch.link(V.scalar_tensor_tensor(key1[:], key1[:], 1.0, other[:], ALU.add, ALU.mult))
                    part(key2, dst_i, ALU.bitwise_and, P - 1)
                    part(scratch_f, src_i, ALU.bitwise_and, 31)
                    ch.link(V.scalar_tensor_tensor(key2[:], key2[:], 32.0, scratch_f[:], ALU.mult, ALU.add))
                    ch.link(V.scalar_tensor_tensor(key2[:], key2[:], -2048.0, other[:], ALU.add, ALU.mult))
                    V.tensor_scalar_min(src_f[:], src_f[:], float(NP - 1)).then_inc(v_ch, 1)
                    V.tensor_scalar_min(dst_f[:], dst_f[:], float(NP - 1)).then_inc(v_ch, 1)
                    ch.count += 2
                    ch.wait()
                    ch.link(V.tensor_copy(src_i[:], src_f[:]))
                    V.tensor_copy(dst_i[:], dst_f[:]).then_inc(split, 1)
                    base = ch.count

                    def hots(t):
                        q = t.slot(4)
                        if t.reused(4):
                            dve.wait_ge(counted, t.plus(-3).n)
                        V.tensor_scalar(tile_hot[:, q, :], iota_h[:, :NT], src_tile[:, bass.ds(t.n, 1)], None,
                                        ALU.is_equal).then_inc(tile_hot_made, 1)

                    def ranks(t):
                        b = t.slot(2)
                        dve.wait_ge(tile_hot_made, t.n + 1)
                        dve.wait_ge(ranked, t.n + 1)
                        V.tensor_tensor_reduce(out=picked[:, b, :], in0=ps_rank[b][:], in1=tile_hot[:, t.slot(4), :],
                                               scale=1.0, scalar=0.0, op0=ALU.mult, op1=ALU.add,
                                               accum_out=rank[:, b:b + 1]).then_inc(rank_read, 1)

                    def slot_keys_of(t):
                        b = t.slot(2)
                        dve.wait_ge(rank_read, t.n + 1)
                        if t.reused(2):
                            dve.wait_ge(counted, t.plus(-1).n)
                        V.tensor_scalar(rank_key1[:, b, :], iota_h[:, :P], rank[:, b:b + 1],
                                        key1[:, bass.ds(t.n, 1)], ALU.is_equal, ALU.mult).then_inc(keys_made, 1)
                        V.tensor_scalar(rank_key2[:, b, :], iota_h[:, :P], rank[:, b:b + 1],
                                        key2[:, bass.ds(t.n, 1)], ALU.is_equal, ALU.mult).then_inc(keys_made, 1)

                    for t in steps(dve, -2, KE, 4, end=KE, ahead=2):
                        at(t, 0, ranks)
                        at(t, 2, hots)
                        at(t, 0, slot_keys_of)
                    dve.wait_ge(swept, 1)
                    ch.at(base)
                    for to, bank in ((deg, ps_deg), (selfs, ps_self), (slot_keys[0], ps_key[0]),
                                     (slot_keys[1], ps_key[1]), (counts, ps_rank[0])):
                        ch.mark(V.tensor_copy(to[:], bank[:]))
                    ch.wait()
                    ch.link(V.tensor_reduce(most[:], counts[:], AX.X, ALU.max))
                    ch.link(V.tensor_scalar(over[:], most[:], float(P), None, ALU.is_gt))
                    ch.link(V.tensor_copy(overflow_i[:], over[:]))
                    ch.link(V.tensor_scalar(valid[:], slot_keys[0][:], 0.0, None, ALU.is_gt))
                    ch.link(V.tensor_scalar(fa[:], slot_keys[0][:], -1.0, 0.0, ALU.add, ALU.max))
                    ch.link(V.tensor_copy(dec[0][:], fa[:]))
                    ch.link(V.tensor_scalar(fb[:], slot_keys[1][:], 2048.0, None, ALU.add))
                    ch.link(V.tensor_copy(dec[1][:], fb[:]))
                    ch.link(V.tensor_scalar(dec[2][:], dec[0][:], 2, None, ALU.logical_shift_right))
                    ch.link(V.tensor_copy(slot_tile[:], dec[2][:]))
                    ch.link(V.tensor_scalar(dec[2][:], dec[1][:], 5, None, ALU.logical_shift_right))
                    ch.link(V.tensor_copy(slot_lane[:], dec[2][:]))
                    ch.link(V.scalar_tensor_tensor(fa[:], slot_tile[:], float(P), slot_lane[:], ALU.mult,
                                                   ALU.add))
                    ch.link(V.scalar_tensor_tensor(fa[:], fa[:], -float(PAD * 8), valid[:], ALU.add, ALU.mult))
                    ch.link(V.tensor_scalar(fa[:], fa[:], float(PAD * 8), None, ALU.add))
                    ch.link(V.tensor_scalar(dec[0][:], dec[0][:], 3, None, ALU.bitwise_and))
                    ch.link(V.tensor_scalar(dec[1][:], dec[1][:], 31, None, ALU.bitwise_and))
                    ch.link(V.tensor_copy(slot_node[:], dec[0][:]))
                    ch.link(V.tensor_copy(fb[:], dec[1][:]))
                    ch.link(V.scalar_tensor_tensor(slot_node[:], slot_node[:], 32.0, fb[:], ALU.mult, ALU.add))
                    ch.link(V.scalar_tensor_tensor(slot_node[:], slot_node[:], 1.0, valid[:], ALU.add, ALU.mult))
                    ch.link(V.tensor_scalar_add(slot_node[:], slot_node[:], -1.0))
                    ch.link(V.tensor_scalar(fb[:], iota[:, :NT], float(P), lane[:], ALU.mult, ALU.add))
                    ch.link(V.tensor_tensor(fb[:], fb[:], fa[:], ALU.subtract))
                    ch.link(V.scalar_tensor_tensor(fa[:], fb[:], over[:], fa[:], ALU.mult, ALU.add))
                    ch.link(V.tensor_copy(slot_row[:], fa[:]))
                    ch.link(V.tensor_scalar(fb[:], slot_node[:], -1.0, lane[:], ALU.mult, ALU.add))
                    ch.link(V.scalar_tensor_tensor(slot_node[:], fb[:], over[:], slot_node[:], ALU.mult, ALU.add))
                    ch.link(V.tensor_scalar(fa[:], deg[:], 0.0, None, ALU.is_gt))
                    ch.link(V.tensor_scalar(fb[:], deg[:], 1.0, None, ALU.max))
                    ch.link(V.tensor_copy(deg[:], fa[:]))
                    ch.link(V.tensor_copy(dinv[:], fb[:]))
                    ch.link(V.tensor_copy(cinv[:], deg[:]))

        with Phase(nc) as c:
            G = 4
            NG = -(-NT // G)
            dst_tile = sb("dst_tile", [P, KE], c=c)
            dst_lane = sb("dst_lane", [P, KE], c=c)
            scratch_i = sb("scratch_i2", [P, KE], I32, c)
            column = sb("column", [P, 4], I32, c)
            value = [sb(f"value{i}", [P, 1], c=c) for i in range(4)]
            hot_tile = sb("hot_tile32", [P, 4, NT], c=c)
            hot_lane = sb("hot_lane32", [P, 4, P], c=c)
            lane_hot = sb("slot_lane_hot", [P, 4, P], c=c)
            lane_col = sb("slot_lane_col", [P, 4], c=c)
            zero = sb("zero32", [P, P], c=c)
            root = sb("root", [P, NT], c=c)
            raised = sb("raised", [P, NT], c=c)
            scratch = sb("scratch32", [P, NT], c=c)
            mask = sb("mask", [P, NT], c=c)
            by_tile = sb("by_tile", [P, -(-NT // P), P], c=c)
            near = sb("near", [P, 4, G * P], c=c)
            picked = sb("picked_dinv", [P, 2, G, P], c=c)
            slot_value = sb("slot_value", [P, 2, G], c=c)
            ps_sum = ps("ps_sum", [P, NT], c=c)
            ps_t = ps("ps_t", [P, P], c=c)

            ready = sem("edges_ready", c)
            rooted = sem("rooted", c)
            masked = sem("masked", c)
            turned = sem("turned", c)
            copied = sem("turned_copied", c)
            written = sem("dinv_written", c)
            col_ready = sem("column_copied", c)
            got = [sem(f"value_in{i}", c) for i in range(4)]
            hots = sem("hot32_made", c)
            lane_col_made = sem("slot_lane_col_made", c)
            lane_hot_made = sem("slot_lane_hot_made", c)
            lane_scaled = sem("slot_lane_scaled", c)
            summed = sem("column_summed", c)
            cdone = sem("cdeg_done", c)
            near_in = [sem(f"near_in{i}", c) for i in range(4)]
            value_made = sem("value_made", c)
            closed = sem("sums_closed", c)
            maskd = sem("sums_masked", c)
            sums = sb("sums", [P, NT], c=c)
            v_ch = sem("vector_chain_c", c)
            CH = [(k, min(P, NT - k)) for k in range(0, NT, P)]

            def tiles(g):
                return G if g.g is not None or g.at < NG - 1 else NT - (NG - 1) * G

            with nc.Block() as block:
                @block.gpsimd
                def _(pool):
                    pool.wait_ge(written, 16 * len(CH))
                    with pool.If(flagged(pool, overflow_i) > 0):
                        for t in steps(pool, 0, KE, 4):
                            b = t.slot(4)
                            if t.reused(4):
                                wait_apart(pool, hots, t.plus(-3).n * 2, c.passed)
                            nc.gpsimd.tensor_copy(column[:, b:b + 1], src_i[:, bass.ds(t.n, 1)]).then_inc(col_ready, 1)
                            wait_apart(pool, col_ready, t.n + 1, c.passed)
                            nc.gpsimd.indirect_dma_start(
                                out=value[b][:], out_offset=None, in_=dinv_dram[:, :],
                                in_offset=bass.IndirectOffsetOnAxis(ap=column[:, b:b + 1], axis=0)).then_inc(got[b], 16)
                    with pool.If(flagged(pool, overflow_i) < 1):
                        for t in steps(pool, 0, NT, 4):
                            b = t.slot(4)
                            if t.reused(4):
                                wait_apart(pool, lane_scaled, t.plus(-3).n, c.passed)
                            nc.gpsimd.tensor_copy(lane_col[:, b:b + 1],
                                                  slot_lane[:, bass.ds(t.n, 1)]).then_inc(lane_col_made, 1)
                            wait_apart(pool, lane_col_made, t.n + 1, c.passed)
                            nc.gpsimd.tensor_scalar(lane_hot[:, b, :], iota[:, :P], lane_col[:, b:b + 1], None,
                                                    ALU.is_equal).then_inc(lane_hot_made, 1)

                @block.scalar
                def _(act):
                    nc.scalar.activation(root[:], dinv[:], ACT.Sqrt).then_inc(rooted, 1)
                    with act.If(flagged(act, overflow_i) < 1):
                        for g in steps(act, 0, NG, 4):
                            act.wait_ge(value_made, g.n + 1)
                            for j in range(tiles(g)):
                                n = g.n * G + j
                                act.wait_ge(lane_hot_made, n + 1)
                                if g.reused(1):
                                    act.wait_ge(summed, n - 3)
                                nc.scalar.activation(hot_lane[:, j, :], lane_hot[:, j, :], ACT.Copy,
                                                     scale=slot_value[:, g.slot(2), j:j + 1]).then_inc(lane_scaled, 1)
                    act.wait_ge(maskd, 2)
                    nc.scalar.activation(root[:], cinv[:], ACT.Sqrt).then_inc(rooted, 1)

                @block.tensor
                def _(pe):
                    def turn(frm, base):
                        for k, (lo, w) in enumerate(CH):
                            if base + k:
                                pe.wait_ge(copied, base + k)
                            nc.tensor.transpose(ps_t[0:w, :], frm[:, lo:lo + w], ident[:]).then_inc(turned, 1)
                    pe.wait_ge(masked, 1)
                    turn(dinv, 0)
                    pe.wait_ge(ready, 1)
                    nc.tensor.matmul(ps_sum[:], zero[:], iota[:, :NT], start=True, stop=False, skip_group_check=True)

                    def add_column(b):
                        nc.tensor.matmul(ps_sum[:], hot_lane[:, b, :], hot_tile[:, b, :], start=False, stop=False,
                                         skip_group_check=True).then_inc(summed, 1)
                    over = flagged(pe, overflow_i)
                    with pe.If(over > 0):
                        for t in steps(pe, 0, KE, 2):
                            pe.wait_ge(hots, (t.n + 1) * 2)
                            add_column(t.slot(2))
                    with pe.If(over < 1):
                        for t in steps(pe, 0, NT, 4):
                            pe.wait_ge(hots, t.n + 1)
                            pe.wait_ge(lane_scaled, t.n + 1)
                            add_column(t.slot(4))
                    nc.tensor.matmul(ps_sum[:], zero[:], iota[:, :NT], start=False, stop=True,
                                     skip_group_check=True).then_inc(closed, 1)

                @block.vector
                def _(dve):
                    V = nc.vector
                    ch = Chain(dve, v_ch)

                    def inverse_root(of):
                        ch.link(V.reciprocal(raised[:], root[:]))
                        ch.link(V.tensor_tensor(scratch[:], raised[:], raised[:], ALU.mult))
                        ch.link(V.tensor_tensor(scratch[:], scratch[:], of[:], ALU.mult))
                        ch.link(V.tensor_scalar(scratch[:], scratch[:], -0.5, 1.5, ALU.mult, ALU.add))
                        ch.link(V.tensor_tensor(raised[:], raised[:], scratch[:], ALU.mult))
                    dve.wait_ge(rooted, 1)
                    inverse_root(dinv)
                    V.tensor_tensor(dinv[:], raised[:], cinv[:], ALU.mult).then_inc(masked, 1)
                    for k, (lo, w) in enumerate(CH):
                        dve.wait_ge(turned, k + 1)
                        V.tensor_copy(by_tile[0:w, k, :], ps_t[0:w, :]).then_inc(copied, 1)
                    ch.link(V.memset(zero[:], 0.0))
                    ch.link(V.tensor_scalar(scratch_i[:], dst_i[:], 7, None, ALU.logical_shift_right))
                    ch.link(V.tensor_copy(dst_tile[:], scratch_i[:]))
                    ch.link(V.tensor_scalar(scratch_i[:], dst_i[:], P - 1, None, ALU.bitwise_and))
                    V.tensor_copy(dst_lane[:], scratch_i[:]).then_inc(ready, 1)
                    dve.wait_ge(ready, 1)

                    def hot_matrices(t):
                        b = t.slot(2)
                        if t.reused(2):
                            dve.wait_ge(summed, t.plus(-1).n)
                        V.tensor_scalar(hot_tile[:, b, :], iota[:, :NT], dst_tile[:, bass.ds(t.n, 1)], None,
                                        ALU.is_equal).then_inc(hots, 1)
                        V.tensor_scalar(hot_lane[:, b, :], iota[:, :P], dst_lane[:, bass.ds(t.n, 1)],
                                        value[t.slot(4)][:], ALU.is_equal, ALU.mult).then_inc(hots, 1)

                    def slot_dinv(g):
                        b, q = g.slot(2), g.slot(4)
                        dve.wait_ge(near_in[q], g.uses(4) * 16 + 16)
                        if g.reused(2):
                            dve.wait_ge(lane_scaled, g.plus(-1).n * G)
                        for j in range(tiles(g)):
                            last = V.scalar_tensor_tensor(
                                out=picked[:, b, j, :], in0=iota[:, :P], scalar=slot_node[:, bass.ds(g.n * G + j, 1)],
                                in1=near[:, q, j * P:(j + 1) * P], op0=ALU.is_equal, op1=ALU.mult,
                                accum_out=slot_value[:, b, j:j + 1])
                        last.then_inc(value_made, 1)

                    over, linked = flagged(dve, overflow_i), ch.count
                    with dve.If(over > 0):
                        for t in steps(dve, 0, KE, 4):
                            dve.wait_ge(got[t.slot(4)], t.uses(4) * 16 + 16)
                            hot_matrices(t)
                        dve.wait_ge(closed, 1)
                        ch.link(V.tensor_copy(sums[:], ps_sum[:]))
                    with dve.If(over < 1):
                        ch.at(linked)
                        for g in steps(dve, -1, NG, 4, end=NG, ahead=1):
                            at(g, 1, slot_dinv)
                            for j in range(tiles(g) if g.exists() else 0):
                                if g.reused(1):
                                    dve.wait_ge(summed, g.n * G + j - 3)
                                V.tensor_scalar(hot_tile[:, j, :], iota[:, :NT],
                                                slot_tile[:, bass.ds(g.n * G + j, 1)], None,
                                                ALU.is_equal).then_inc(hots, 1)
                        ch.link(V.tensor_tensor(sums[:], selfs[:], dinv[:], ALU.mult))
                        dve.wait_ge(closed, 1)
                        V.tensor_tensor(sums[:], sums[:], ps_sum[:], ALU.add).then_inc(cdone, 1)
                        dve.wait_ge(cdone, 1)
                    ends = ch.count + ch.base
                    V.tensor_scalar(mask[:], sums[:], 0.0, None, ALU.is_gt).then_inc(maskd, 1)
                    V.tensor_scalar(cinv[:], sums[:], 1e-30, None, ALU.max).then_inc(maskd, 1)
                    dve.wait_ge(rooted, 2)
                    ch.at(ends)
                    inverse_root(cinv)
                    V.tensor_tensor(cinv[:], raised[:], mask[:], ALU.mult).then_inc(masked, 1)
                    dve.wait_ge(masked, 2)

                @block.sync
                def _(sp):
                    view = dinv_dram.rearrange("(t p) a -> t (p a)", p=P)
                    for k, (lo, w) in enumerate(CH):
                        sp.wait_ge(copied, k + 1)
                        sp.dma_start(view[lo:lo + w, :], by_tile[0:w, k, :]).then_inc(written, 16)
                    sp.wait_ge(written, 16 * len(CH))
                    with sp.If(flagged(sp, overflow_i) < 1):
                        flat = dinv_dram.rearrange("n a -> (n a)")
                        for g in steps(sp, 0, NG, 4):
                            q, size = g.slot(4), tiles(g) * P
                            if g.reused(4):
                                sp.wait_ge(value_made, g.plus(-3).n)
                            sp.dma_start(near[:, q, 0:size],
                                         flat[bass.ds(g.n * (G * P), size)].partition_broadcast(P)).then_inc(near_in[q], 16)

        layer_norm_pass(nc, x, tables[0], NT, LAST, D, minus_half, eps, cinv, sb, sem)

        for l in range(LAYERS):
            general_pass(nc, l, tables[l], dict(
                KE=KE, NP=NP, D=D, node_sums=node_sums, src_i=src_i, dst_i=dst_i, src_f=src_f,
                other=other, ident=ident, earlier=earlier, lane=lane,
                overflow_i=overflow_i), sb, ps, sem)
            layer(nc, l, l == LAYERS - 1, dict(
                NT=NT, D=D, FC=FC, H=H, C=C, IC=IC, INNER=INNER, LAST=LAST, N=N, table=tables[l],
                after=tables[l + 1] if l + 1 < LAYERS else None, x=x, x2_dram=x2_dram, w_dram=w_dram,
                ident=ident, iota=iota, minus_half=minus_half, eps=eps, slot_row=slot_row,
                slot_node=slot_node, selfs=selfs, dinv=dinv, cinv=cinv,
                w=gw_sb[:, l, :, :], w_parts=gw_last, b=gb_sb[:, l, :], wlog=wlog, blog=blog, token_sum=token_sum,
                weight_sum=weight_sum, node_sums=node_sums, overflow_i=overflow_i), sb, ps, sem)

        slices(nc, dict(D=D, FC=FC, H=H, C=C, IC=IC, INNER=INNER, SCALE=SCALE, ident=ident, ones=ones,
                        token_sum=token_sum, weight_sum=weight_sum, mix=mix, wfx_sb=wfx_sb, bfx_sb=bfx_sb,
                        wqkv_sb=wqkv_sb, wout_sb=wout_sb), sb, ps, sem)

        spread_back(nc, dict(NT=NT, D=D, IC=IC, INNER=INNER, LAST=LAST, N=N, x2_dram=x2_dram, w_dram=w_dram,
                             out=out, ident=ident, mix=mix, bout_sb=bout_sb), sb, ps, sem)


def flagged(eng, overflow_i):
    return eng.value_load(overflow_i[0:1, 0:1], min_val=0, max_val=1)


def tile_rows(ap, t, count=P):
    return ap[bass.ds(t.n * P, count), :]


def layer_norm_pass(nc, x, to, NT, LAST, D, minus_half, eps, cinv, sb, sem):
    B, T = 4, 4
    NG = -(-NT // T)
    with Phase(nc) as c:
        xin = sb("ln_x", [P, B, T, D], c=c)
        y = sb("ln_y", [P, B, T, D], c=c)
        stats = sb("ln_stats", [P, B, T, 6], c=c)
        mv = sb("ln_mv", [P, B, T, 2], c=c)
        scale = sb("ln_scale", [P, B, T], c=c)
        eps_t = sb("ln_eps", [P, T], c=c)
        cleared = sem("ln_cleared", c)
        x_in = [sem(f"ln_x_in{i}", c) for i in range(B)]
        y_out = [sem(f"ln_y_out{i}", c) for i in range(B)]
        stats_done = sem("ln_stats_done", c)
        var_done = sem("ln_var_done", c)
        pool_step = sem("ln_pool_step", c)
        scale_done = sem("ln_scale_done", c)
        y_done = sem("ln_y_done", c)

        def group(ap, t):
            return ap[bass.ds(t.n * (T * P), T * P), :].rearrange("(j p) n -> p j n", p=P)

        def tiles(t):
            return T if t.g is not None or t.at < NG - 1 else NT - (NG - 1) * T
        with nc.Block() as block:
            @block.sync
            def _(sp):
                sp.wait_ge(cleared, 1)
                for t in steps(sp, 0, NG, B, ahead=0):
                    b = t.slot(B)
                    if t.reused(B):
                        sp.wait_ge(y_done, t.plus(1 - B).n)
                    if t.g is not None or t.at < NG - 1:
                        sp.dma_start(xin[:, b, :, :], group(x, t)).then_inc(x_in[b], 16)
                    else:
                        for j in range(tiles(t)):
                            n, r0 = (P if t.at * T + j < NT - 1 else LAST), (t.at * T + j) * P
                            sp.dma_start(xin[0:n, b, j, :], x[r0:r0 + n, :]).then_inc(x_in[b], 16)

            @block.gpsimd
            def _(pool):
                nc.gpsimd.memset(xin[:], 0.0).then_inc(cleared, 1)
                nc.gpsimd.memset(eps_t[:], EPS).then_inc(cleared, 1)
                pool.wait_ge(cleared, 2)
                for t in steps(pool, 0, NG, B):
                    b, k = t.slot(B), tiles(t)
                    pool.wait_ge(var_done, t.n + 1)
                    s, m = scale[:, b, 0:k], mv[:, b, 0:k, :]
                    nc.gpsimd.tensor_tensor(s, m[:, :, 1], eps_t[:, 0:k], ALU.add).then_inc(pool_step, 1)
                    pool.wait_ge(pool_step, t.n * 2 + 1)
                    nc.gpsimd.tensor_tensor(s, s, minus_half[:, 0:k], ALU.pow).then_inc(pool_step, 1)
                    pool.wait_ge(pool_step, t.n * 2 + 2)
                    nc.gpsimd.tensor_tensor(s, s, cinv[:, bass.ds(t.n * T, k)], ALU.mult).then_inc(scale_done, 1)

            @block.vector
            def _(dve):
                def statistics(t):
                    b = t.slot(B)
                    dve.wait_ge(x_in[b], t.uses(B) * 16 + 16 * (1 if tiles(t) == T or t.g is not None else tiles(t)))
                    for j in range(tiles(t)):
                        last = nc.vector.bn_stats(stats[:, b, j, :], xin[:, b, j, :])
                    last.then_inc(stats_done, 1)

                def aggregate(t):
                    b = t.slot(B)
                    wait_apart(dve, stats_done, t.n + 1, c.passed)
                    for j in range(tiles(t)):
                        last = nc.vector.bn_aggr(mv[:, b, j, :], stats[:, b, j, :])
                    last.then_inc(var_done, 1)

                def normalise(t):
                    b = t.slot(B)
                    dve.wait_ge(scale_done, t.n + 1)
                    if t.reused(B):
                        dve.wait_ge(y_out[b], t.uses(B) * 16)
                    for j in range(tiles(t)):
                        last = nc.vector.tensor_scalar(y[:, b, j, :], xin[:, b, j, :], mv[:, b, j, 0:1],
                                                       scale[:, b, j:j + 1], ALU.subtract, ALU.mult)
                    last.then_inc(y_done, 1)
                for t in steps(dve, -1, NG + 1, B, end=NG, behind=1, ahead=1):
                    at(t, 1, statistics)
                    at(t, 1, aggregate)
                    at(t, 0, normalise)

            @block.scalar
            def _(act):
                for t in steps(act, 0, NG, B):
                    b = t.slot(B)
                    act.wait_ge(y_done, t.n + 1)
                    if t.g is not None or t.at < NG - 1:
                        act.dma_start(group(to, t), y[:, b, :, :]).then_inc(y_out[b], 16)
                    else:
                        r0, k = t.at * T * P, tiles(t)
                        act.dma_start(to[r0:r0 + k * P, :].rearrange("(j p) n -> p j n", p=P),
                                      y[:, b, 0:k, :]).then_inc(y_out[b], 16)
                for b in range(B):
                    act.wait_ge(y_out[b], 16 * (-(-(NG - b) // B)))


def split_product(nc, out, left, right, start, stop):
    high, low = left
    nc.tensor.matmul(out, high, right[0], start=start, stop=False)
    nc.tensor.matmul(out, high, right[1], start=False, stop=False)
    return nc.tensor.matmul(out, low, right[0], start=False, stop=stop)


def general_pass(nc, l, table, k, sb, ps, sem):
    KE, NP, D, node_sums = k["KE"], k["NP"], k["D"], k["node_sums"]
    src_i, dst_i, src_f, other, ident = k["src_i"], k["dst_i"], k["src_f"], k["other"], k["ident"]
    with Phase(nc) as c:
        zero = sb(f"g_zero{l}", [P, D], c=c)
        col = sb(f"g_col{l}", [P, 3], I32, c)
        row_f = sb(f"g_row_f{l}", [P, 2], c=c)
        feat = sb(f"g_feat{l}", [P, D], c=c)
        have = sb(f"g_have{l}", [P, D], c=c)
        new = sb(f"g_new{l}", [P, D], c=c)
        wide = sb(f"g_wide{l}", [P, P], c=c)
        same = sb(f"g_same{l}", [P, P], c=c)
        dups = sb(f"g_dups{l}", [P, P], c=c)
        dup = sb(f"g_dup{l}", [P, 1], c=c)
        srow = sb(f"g_srow{l}", [P, 1], c=c)
        ps_wide = ps(f"g_ps_wide{l}", [P, P], c=c)
        ps_comb = ps(f"g_ps_comb{l}", [P, D], c=c)
        zeroed = sem(f"g_zeroed{l}", c)
        clear = sem(f"g_clear{l}", c)
        index = sem(f"g_index{l}", c)
        in_feat = sem(f"g_in_feat{l}", c)
        in_have = sem(f"g_in_have{l}", c)
        scattered = sem(f"g_scattered{l}", c)
        wide_made = sem(f"g_wide_made{l}", c)
        turned = sem(f"g_turned{l}", c)
        scaled = sem(f"g_scaled{l}", c)
        combined = sem(f"g_combined{l}", c)
        v_ch = sem(f"g_chain{l}", c)
        row_made = sem(f"g_row_made{l}", c)
        sums_made = sem(f"g_sums_made{l}", c)

        with nc.Block() as block:
            @block.sync
            def _(sp):
                with sp.If(flagged(sp, k["overflow_i"]) > 0):
                    sp.wait_ge(zeroed, 1)
                    with sp.Fori(0, NP // P + 1) as i:
                        sp.dma_start(node_sums[bass.ds(i * P, P), :], zero[:]).then_inc(clear, 16)
                    sp.wait_ge(clear, (NP // P + 1) * 16)

            @block.gpsimd
            def _(pool):
                with pool.If(flagged(pool, k["overflow_i"]) > 0):
                    pool.wait_ge(clear, (NP // P + 1) * 16)
                    with pool.Fori(0, KE) as n:
                        wait_apart(pool, row_made, n * 2 + 1, c.passed)
                        nc.gpsimd.tensor_copy(col[:, 0:1], dst_i[:, bass.ds(n, 1)]).then_inc(index, 1)
                        nc.gpsimd.tensor_copy(col[:, 1:2], row_f[:, 0:1]).then_inc(index, 1)
                        wait_apart(pool, index, n * 3 + 2, c.passed)
                        for to, frm, i, s in ((feat, table, 0, in_feat), (have, node_sums, 1, in_have)):
                            nc.gpsimd.indirect_dma_start(
                                out=to[:], out_offset=None, in_=frm[:, :],
                                in_offset=bass.IndirectOffsetOnAxis(ap=col[:, i:i + 1], axis=0)).then_inc(s, 16)
                        wait_apart(pool, row_made, n * 2 + 2, c.passed)
                        nc.gpsimd.tensor_copy(col[:, 2:3], row_f[:, 1:2]).then_inc(index, 1)
                        wait_apart(pool, index, n * 3 + 3, c.passed)
                        wait_apart(pool, sums_made, n + 1, c.passed)
                        nc.gpsimd.indirect_dma_start(
                            out=node_sums[:, :], out_offset=bass.IndirectOffsetOnAxis(ap=col[:, 2:3], axis=0),
                            in_=new[:], in_offset=None).then_inc(scattered, 16)
                        pool.wait_ge(scattered, n * 16 + 16)

            @block.vector
            def _(dve):
                V = nc.vector
                with dve.If(flagged(dve, k["overflow_i"]) > 0):
                    V.memset(zero[:], 0.0).then_inc(zeroed, 1)
                    with dve.Fori(0, KE) as n:
                        ch = Chain(dve, v_ch)
                        ch.at(n * 7)
                        V.tensor_copy(row_f[:, 0:1], src_f[:, bass.ds(n, 1)]).then_inc(row_made, 1)
                        ch.link(V.tensor_copy(srow[:], src_f[:, bass.ds(n, 1)]))
                        V.tensor_copy(wide[:], srow[:].to_broadcast([P, P])).then_inc(wide_made, 1)
                        dve.wait_ge(turned, n + 1)
                        ch.link(V.tensor_scalar(same[:], ps_wide[:], srow[:], None, ALU.is_equal))
                        ch.link(V.tensor_tensor_reduce(out=dups[:], in0=same[:], in1=k["earlier"][:], scale=1.0,
                                                       scalar=0.0, op0=ALU.mult, op1=ALU.add, accum_out=dup[:]))
                        ch.link(V.tensor_scalar(dup[:], dup[:], 0.0, None, ALU.is_gt))
                        dve.wait_ge(row_made, n * 2 + 1)
                        ch.link(V.tensor_scalar(row_f[:, 1:2], row_f[:, 0:1], -1.0, float(NP), ALU.mult, ALU.add))
                        ch.link(V.tensor_scalar(row_f[:, 1:2], row_f[:, 1:2], k["lane"][:], None, ALU.add))
                        ch.link(V.tensor_tensor(row_f[:, 1:2], row_f[:, 1:2], dup[:], ALU.mult))
                        V.tensor_tensor(row_f[:, 1:2], row_f[:, 1:2], row_f[:, 0:1], ALU.add).then_inc(row_made, 1)
                        dve.wait_ge(in_feat, n * 16 + 16)
                        V.tensor_scalar(feat[:], feat[:], other[:, bass.ds(n, 1)], None, ALU.mult).then_inc(scaled, 1)
                        dve.wait_ge(in_have, n * 16 + 16)
                        dve.wait_ge(combined, n + 1)
                        V.tensor_tensor(new[:], ps_comb[:], have[:], ALU.add).then_inc(sums_made, 1)
                        dve.wait_ge(scattered, n * 16 + 16)

            @block.tensor
            def _(pe):
                with pe.If(flagged(pe, k["overflow_i"]) > 0):
                    with pe.Fori(0, KE) as n:
                        pe.wait_ge(wide_made, n + 1)
                        nc.tensor.transpose(ps_wide[:], wide[:], ident[:]).then_inc(turned, 1)
                        pe.wait_ge(scaled, n + 1)
                        nc.tensor.matmul(ps_comb[:], same[:], feat[:], start=True, stop=True).then_inc(combined, 1)


def layer(nc, l, fused, k, sb, ps, sem):
    NT, D, FC, H, C, IC, INNER, LAST = (k[n] for n in ("NT", "D", "FC", "H", "C", "IC", "INNER", "LAST"))
    ident, iota, dinv = k["ident"], k["iota"], k["dinv"]
    B = BUFFERS
    with Phase(nc) as c:
        own = sb("own", [P, B, D], c=c)
        scaled_own = sb("scaled_own", [P, B, D], c=c)
        others = [sb(f"others{i}", [P, D], c=c) for i in range(B)]
        row = sb("row", [P, B], I32, c)
        pick = sb("pick", [P, B, P], c=c)
        sumT = [sb(f"sumT_{part}", [P, 2, D], FP32R if fused else FP32, c)
                for part in (("high", "low") if fused else ("all",))]
        z = sb("z", [P, 2, D], c=c)
        y = sb("y", [P, B, D], c=c)
        ps_sum = [ps(f"ps_sum{l}_{i}", [P, D], c=c) for i in range(2)]
        ps_out = [ps(f"ps_out{l}_{i}", [P, D], c=c) for i in range(2)]

        cleared = sem("cleared", c)
        own_in = [sem(f"own_in{i}", c) for i in range(B)]
        others_in = [sem(f"others_in{i}", c) for i in range(B)]
        row_made = sem("row_made", c)
        own_scaled = sem("own_scaled", c)
        picks = sem("picks_made", c)
        sums = sem("sums_done", c)
        sums_copied = sem("sums_copied", c)
        sums_rest = sem("sums_rest", c) if fused else sums_copied
        outs_done = sem("outs_done", c)
        z_done = sem("z_done", c)
        y_done = sem("y_done", c)
        y_out = [sem(f"y_out{i}", c) for i in range(B)]
        if fused:
            xres = sb("xres", [P, B, D], c=c)
            xn = sb("xn", [P, B, D], c=c)
            stats = sb("stats", [P, 2, 6], c=c)
            mv = sb("mv", [P, 2, 2], c=c)
            ve = sb("ve", [P, 2, 1], c=c)
            rstd = sb("rstd", [P, 2, 1], c=c)
            xnT = [sb(f"xnT_{part}", [P, 2, D], FP32R, c) for part in ("high", "low")]
            lg = sb("lg", [P, 2, INNER], c=c)
            nmx = sb("nmx", [P, 2, H], c=c)
            ex = sb("ex", [P, 2, INNER], c=c)
            tot = sb("tot", [P, 2, H], c=c)
            rtot = sb("rtot", [P, 2, H], c=c)
            w = sb("w", [P, B, INNER], c=c)
            ps_T = ps("ps_T", [P, D], c=c)
            ps_log = ps("ps_log", [P, INNER], c=c)
            ps_tok = [ps(f"ps_tok{i}", [P, 2, D], c=c) for i in range(IC // 2)]
            x_in = [sem(f"x_in{i}", c) for i in range(B)]
            stats_done = sem("stats_done", c)
            var_done = sem("var_done", c)
            eps_added = sem("eps_added", c)
            rstd_done = sem("rstd_done", c)
            xn_done = sem("xn_done", c)
            turned = sem("xn_turned", c)
            turned_copied = sem("xn_turned_copied", c)
            turned_rest = sem("xn_turned_rest", c)
            logits_done = sem("logits_done", c)
            biased = sem("biased", c)
            max_done = sem("max_done", c)
            exp_done = sem("exp_done", c)
            recip_done = sem("recip_done", c)
            w_done = sem("w_done", c)
            w_out = [sem(f"w_out{i}", c) for i in range(B)]
            tokens_done = sem("tokens_done", c)
            wsum_done = sem("wsum_done", c)
            saved = sem("tokens_saved", c)
        LOADS = B

        def scale_own(eng, make, t):
            b = t.slot(B)
            eng.wait_ge(own_in[b], t.uses(B) * 16 + 16)
            if t.reused(B):
                eng.wait_ge(sums, t.plus(1 - B).n)
            make(scaled_own[:, b, :], own[:, b, :], k["selfs"][:, bass.ds(t.n, 1)]).then_inc(own_scaled, 1)

        with nc.Block() as block:
            @block.sync
            def _(sp):
                sp.wait_ge(cleared, B + 1)

                def load_own(t):
                    b = t.slot(B)
                    if t.reused(B):
                        sp.wait_ge(own_scaled, t.plus(1 - B).n)
                    sp.dma_start(own[:, b, :], tile_rows(k["table"], t)).then_inc(own_in[b], 16)

                def load_x(t):
                    b, n = t.slot(B), t.rows(LAST)
                    if t.reused(B):
                        sp.wait_ge(y_done, t.plus(1 - B).n)
                    sp.dma_start(xres[0:n, b, :], tile_rows(k["x"], t, n)).then_inc(x_in[b], 16)

                def store_y(t):
                    b = t.slot(B)
                    sp.wait_ge(y_done, t.n + 1)
                    sp.dma_start(tile_rows(k["x2_dram"] if fused else k["after"], t), y[:, b, :]).then_inc(y_out[b], 16)

                def store_w(t):
                    b = t.slot(B)
                    sp.wait_ge(w_done, t.n + 1)
                    sp.dma_start(tile_rows(k["w_dram"], t), w[:, b, :]).then_inc(w_out[b], 16)

                if fused:
                    for t in steps(sp, -7, NT + 1, B, end=NT, behind=1, ahead=7):
                        at(t, 7, load_own)
                        at(t, -1, store_w)
                        at(t, 2, store_y)
                        at(t, 6, load_x)
                    for b in range(B):
                        sp.wait_ge(w_out[b], 16 * (-(-(NT - b) // B)))
                else:
                    for t in steps(sp, -5, NT, B, end=NT, ahead=5):
                        at(t, 5, load_own)
                        at(t, 0, store_y)
                for b in range(B):
                    sp.wait_ge(y_out[b], 16 * (-(-(NT - b) // B)))

            @block.gpsimd
            def _(pool):
                over = flagged(pool, k["overflow_i"])
                for i in range(B):
                    nc.gpsimd.memset(others[i][:], 0.0).then_inc(cleared, 1)
                if fused:
                    nc.gpsimd.memset(xres[:], 0.0).then_inc(cleared, 1)
                    nc.gpsimd.memset(k["weight_sum"][:], 0.0).then_inc(wsum_done, 1)
                else:
                    nc.gpsimd.memset(y[:], 0.0).then_inc(cleared, 1)
                pool.wait_ge(cleared, B + 1)

                def deviation(t):
                    b = t.slot(2)
                    pool.wait_ge(var_done, t.n + 1)
                    nc.gpsimd.tensor_tensor(ve[:, b, :], mv[:, b, 1:2], k["eps"][:], ALU.add).then_inc(eps_added, 1)
                    pool.wait_ge(eps_added, t.n + 1)
                    nc.gpsimd.tensor_tensor(rstd[:, b, :], ve[:, b, :], k["minus_half"][:, 0:1],
                                            ALU.pow).then_inc(rstd_done, 1)

                def add_weights(t):
                    pool.wait_ge(w_done, t.n + 1)
                    pool.wait_ge(wsum_done, t.n + 1)
                    n, ws = t.rows(LAST), k["weight_sum"]
                    nc.gpsimd.tensor_tensor(ws[0:n, :], ws[0:n, :], w[0:n, t.slot(B), :], ALU.add).then_inc(wsum_done, 1)

                def program(source):
                    def gather(t):
                        b = t.slot(B)
                        if t.reused(B):
                            wait_apart(pool, sums, t.plus(1 - B).n, c.passed)
                        nc.gpsimd.tensor_copy(row[:, b:b + 1], k["slot_row"][:, bass.ds(t.n, 1)]).then_inc(row_made, 1)
                        wait_apart(pool, row_made, t.n + 1, c.passed)
                        nc.gpsimd.indirect_dma_start(
                            out=others[b][:], out_offset=None, in_=source[0:NT * P, :],
                            in_offset=bass.IndirectOffsetOnAxis(ap=row[:, b:b + 1], axis=0),
                            bounds_check=NT * P - 1, oob_is_err=False).then_inc(others_in[b], 16)
                    if fused:
                        for t in steps(pool, -6, NT + 1, B, end=NT, behind=1, ahead=6):
                            at(t, 6, gather)
                            at(t, 2, deviation)
                            at(t, -1, add_weights)
                    else:
                        for t in steps(pool, 0, NT, B):
                            gather(t)

                with pool.If(over > 0):
                    program(k["node_sums"])
                with pool.If(over < 1):
                    program(k["table"])

            @block.tensor
            def _(pe):
                def aggregate(t):
                    b, q = t.slot(2), t.slot(B)
                    pe.wait_ge(own_scaled, t.n + 1)
                    pe.wait_ge(picks, t.n + 1)
                    if t.reused(2):
                        pe.wait_ge(sums_rest, t.plus(-1).n)
                    for f in range(FC):
                        part = slice(f * P, (f + 1) * P)
                        nc.tensor.matmul(ps_sum[b][:, part], scaled_own[:, q, part], ident[:], is_transpose=True,
                                         start=True, stop=False)
                        if f == 0:
                            pe.wait_ge(others_in[q], t.uses(B) * 16 + 16)
                        last = nc.tensor.matmul(ps_sum[b][:, part], others[q][:, part], pick[:, q, :],
                                                start=False, stop=True)
                    last.then_inc(sums, 1)

                def project(t):
                    b = t.slot(2)
                    pe.wait_ge(sums_rest, t.n + 1)
                    if t.reused(2):
                        pe.wait_ge(z_done, t.plus(-1).n)
                    for f in range(FC):
                        turned_sums, first, final = [part[:, b, f * P:(f + 1) * P] for part in sumT], f == 0, f == FC - 1
                        if fused:
                            last = split_product(nc, ps_out[b], turned_sums, [part[:, f, :] for part in k["w_parts"]],
                                                 first, final)
                        else:
                            last = nc.tensor.matmul(ps_out[b], turned_sums[0], k["w"][:, f, :], start=first, stop=final)
                    last.then_inc(outs_done, 1)

                def turn(t):
                    pe.wait_ge(xn_done, t.n + 1)
                    if t.reused(1):
                        pe.wait_ge(turned_rest, t.n)
                    for f in range(FC):
                        last = nc.tensor.transpose(ps_T[:, f * P:(f + 1) * P], xn[:, t.slot(B), f * P:(f + 1) * P], ident[:])
                    last.then_inc(turned, 1)

                def logits(t):
                    pe.wait_ge(turned_rest, t.n + 1)
                    if t.reused(1):
                        pe.wait_ge(biased, t.n)
                    for f in range(FC):
                        last = split_product(nc, ps_log[:], [part[:, t.slot(2), f * P:(f + 1) * P] for part in xnT],
                                             [part[:, f, :] for part in k["wlog"]], f == 0, f == FC - 1)
                    last.then_inc(logits_done, 1)

                def tokens(t):
                    n, final = t.rows(LAST), t.g is None and t.at == NT - 1
                    first = t.g is None and t.at == 0
                    pe.wait_ge(w_done, t.n + 1)
                    for i in range(IC):
                        last = nc.tensor.matmul(ps_tok[i // 2][:, i % 2, :], w[0:n, t.slot(B), i * P:(i + 1) * P],
                                                xn[0:n, t.slot(B), :], start=first and i % 2 == 0,
                                                stop=final and i % 2 == 1, skip_group_check=True)
                    last.then_inc(tokens_done, 1)

                if fused:
                    for t in steps(pe, -4, NT + 1, B, end=NT, behind=1, ahead=4):
                        at(t, 1, turn)
                        at(t, 4, aggregate)
                        at(t, 3, project)
                        at(t, 1, logits)
                        at(t, -1, tokens)
                else:
                    for t in steps(pe, -1, NT, B, end=NT, ahead=1):
                        at(t, 1, aggregate)
                        at(t, 0, project)

            @block.vector
            def _(dve):
                V = nc.vector

                def pick_others(t):
                    b = t.slot(B)
                    if t.reused(B):
                        dve.wait_ge(sums, t.plus(1 - B).n)
                    V.tensor_scalar(pick[:, b, :], iota[:, :P], k["slot_node"][:, bass.ds(t.n, 1)], None,
                                    ALU.is_equal).then_inc(picks, 1)

                def with_bias(t):
                    b = t.slot(2)
                    dve.wait_ge(outs_done, t.n + 1)
                    if t.reused(2) and not fused:
                        dve.wait_ge(y_done, t.plus(-1).n)
                    V.scalar_tensor_tensor(z[:, b, :], ps_out[b], dinv[:, bass.ds(t.n, 1)], k["b"], ALU.mult,
                                           ALU.add).then_inc(z_done, 1)

                def heads(ap):
                    return ap.rearrange("p (h c) -> p h c", c=C)

                def residual(t):
                    b, q = t.slot(2), t.slot(B)
                    dve.wait_ge(z_done, t.n + 1)
                    dve.wait_ge(x_in[q], t.uses(B) * 16 + 16)
                    if t.reused(B):
                        dve.wait_ge(y_out[q], t.uses(B) * 16)
                    V.scalar_tensor_tensor(y[:, q, :], z[:, b, :], 0.0, xres[:, q, :], ALU.max,
                                           ALU.add).then_inc(y_done, 1)

                def statistics(t):
                    dve.wait_ge(y_done, t.n + 1)
                    V.bn_stats(stats[:, t.slot(2), :], y[:, t.slot(B), :]).then_inc(stats_done, 1)

                def mean_and_variance(t):
                    wait_apart(dve, stats_done, t.n + 1, c.passed)
                    V.bn_aggr(mv[:, t.slot(2), :], stats[:, t.slot(2), :]).then_inc(var_done, 1)

                def normalise(t):
                    b, q = t.slot(2), t.slot(B)
                    dve.wait_ge(rstd_done, t.n + 1)
                    if t.reused(B):
                        dve.wait_ge(tokens_done, t.plus(1 - B).n)
                    V.tensor_scalar(xn[:, q, :], y[:, q, :], mv[:, b, 0:1], rstd[:, b, :], ALU.subtract,
                                    ALU.mult).then_inc(xn_done, 1)

                def sums_low(t):
                    b = t.slot(2)
                    dve.wait_ge(sums_copied, t.n + 1)
                    if t.reused(2):
                        dve.wait_ge(outs_done, t.plus(-1).n)
                    V.tensor_tensor(sumT[1][:, b, :], ps_sum[b], sumT[0][:, b, :], ALU.subtract).then_inc(sums_rest, 1)

                def turned_low(t):
                    b = t.slot(2)
                    dve.wait_ge(turned_copied, t.n + 1)
                    if t.reused(2):
                        dve.wait_ge(logits_done, t.plus(-1).n)
                    V.tensor_tensor(xnT[1][:, b, :], ps_T[:], xnT[0][:, b, :], ALU.subtract).then_inc(turned_rest, 1)

                def add_bias(t):
                    b = t.slot(2)
                    dve.wait_ge(logits_done, t.n + 1)
                    if t.reused(2):
                        dve.wait_ge(exp_done, t.plus(-1).n * H)
                    V.tensor_tensor(lg[:, b, :], ps_log[:], k["blog"][:], ALU.add).then_inc(biased, 1)

                def maximum(t):
                    b = t.slot(2)
                    dve.wait_ge(biased, t.n + 1)
                    V.tensor_reduce(nmx[:, b, :], heads(lg[:, b, :]), AX.X, ALU.max, negate=True).then_inc(max_done, 1)

                def invert_sums(t):
                    b = t.slot(2)
                    dve.wait_ge(exp_done, (t.n + 1) * H)
                    V.reciprocal(rtot[:, b, :], tot[:, b, :]).then_inc(recip_done, 1)

                def divide(t):
                    b, q = t.slot(2), t.slot(B)
                    dve.wait_ge(recip_done, t.n + 1)
                    if t.reused(B):
                        dve.wait_ge(w_out[q], t.uses(B) * 16)
                        dve.wait_ge(wsum_done, t.plus(1 - B).n + 1)
                        dve.wait_ge(tokens_done, t.plus(1 - B).n)
                    V.tensor_tensor(heads(w[:, q, :]), heads(ex[:, b, :]),
                                    rtot[:, b, :].unsqueeze(2).to_broadcast([P, H, C]), ALU.mult).then_inc(w_done, 1)

                if fused:
                    for t in steps(dve, -5, NT + 1, B, end=NT, behind=1, ahead=5):
                        at(t, 2, with_bias)
                        at(t, 0, add_bias)
                        at(t, 0, maximum)
                        at(t, 2, residual)
                        at(t, 2, statistics)
                        at(t, 1, turned_low)
                        at(t, 2, mean_and_variance)
                        at(t, -1, invert_sums)
                        at(t, 5, pick_others)
                        at(t, 4, sums_low)
                        at(t, -1, divide)
                        at(t, 2, normalise)
                    dve.wait_ge(tokens_done, NT)
                    for i in range(IC // 2):
                        last = V.tensor_copy(k["token_sum"][:, 2 * i:2 * i + 2, :], ps_tok[i])
                    last.then_inc(saved, 1)
                    dve.wait_ge(saved, 1)
                else:
                    for t in steps(dve, -2, NT, B, end=NT, ahead=2):
                        at(t, 2, pick_others)
                        at(t, 2, lambda u: scale_own(dve, V.tensor_scalar_mul, u))
                        at(t, 0, with_bias)

            @block.scalar
            def _(act):
                def copy_sums(t):
                    b = t.slot(2)
                    act.wait_ge(sums, t.n + 1)
                    if t.reused(2):
                        act.wait_ge(outs_done, t.plus(-1).n)
                    nc.scalar.activation(sumT[0][:, b, :], ps_sum[b], ACT.Copy).then_inc(sums_copied, 1)

                def relu(t):
                    b, q = t.slot(2), t.slot(B)
                    act.wait_ge(z_done, t.n + 1)
                    if t.reused(B):
                        act.wait_ge(y_out[q], t.uses(B) * 16)
                    nc.scalar.activation(y[:, q, :], z[:, b, :], ACT.Relu,
                                         scale=k["cinv"][:, bass.ds(t.n, 1)]).then_inc(y_done, 1)

                def copy_turned(t):
                    b = t.slot(2)
                    act.wait_ge(turned, t.n + 1)
                    if t.reused(2):
                        act.wait_ge(logits_done, t.plus(-1).n)
                    nc.scalar.activation(xnT[0][:, b, :], ps_T[:], ACT.Copy).then_inc(turned_copied, 1)

                def exponentials(t):
                    b = t.slot(2)
                    act.wait_ge(max_done, t.n + 1)
                    if t.reused(2):
                        act.wait_ge(w_done, t.plus(-1).n)
                    for h in range(H):
                        part = slice(h * C, (h + 1) * C)
                        nc.scalar.activation(ex[:, b, part], lg[:, b, part], ACT.Exp, bias=nmx[:, b, h:h + 1],
                                             accum_out=tot[:, b, h:h + 1]).then_inc(exp_done, 1)

                def scale(to, frm, by):
                    return nc.scalar.activation(to, frm, ACT.Copy, scale=by)

                act.wait_ge(cleared, B + 1)
                if fused:
                    for t in steps(act, -5, NT, B, end=NT, ahead=5):
                        at(t, 1, copy_turned)
                        at(t, 4, copy_sums)
                        at(t, 5, lambda u: scale_own(act, scale, u))
                        at(t, 0, exponentials)
                else:
                    for t in steps(act, -1, NT, B, end=NT, ahead=1):
                        at(t, 1, copy_sums)
                        at(t, 0, relu)


def slices(nc, k, sb, ps, sem):
    D, FC, H, C, IC, INNER = (k[n] for n in ("D", "FC", "H", "C", "IC", "INNER"))
    ident, ones, token_sum = k["ident"], k["ones"], k["token_sum"]
    with Phase(nc) as c:
        norm = sb("s_norm", [P, IC], c=c)
        rnorm = sb("s_rnorm", [P, IC], c=c)
        norm_row = sb("s_norm_row", [1, INNER], c=c)
        ratio_row = sb("s_ratio_row", [1, INNER], c=c)
        sumsT = sb("s_sumsT", [P, FC, INNER], c=c)
        tokT = sb("s_tokT", [C, INNER], c=c)
        qT = sb("s_qT", [C, INNER], c=c)
        kT = sb("s_kT", [C, INNER], c=c)
        v = sb("s_v", [C, INNER], c=c)
        score = sb("s_score", [C, INNER], c=c)
        big = sb("s_big", [C, H], c=c)
        total = sb("s_total", [C, H], c=c)
        attnT = sb("s_attnT", [C, INNER], c=c)
        oT = sb("s_oT", [C, INNER], c=c)
        pa = ps("s_pa", [P, INNER], c=c)
        pb = ps("s_pb", [P, INNER], c=c)
        pc = ps("s_pc", [P, INNER], c=c)
        pe_done = sem("s_pe", c)
        v_done = sem("s_v_done", c)
        a_done = sem("s_a_done", c)

        def head(ap, h):
            return ap[:, h * C:(h + 1) * C]
        with nc.Block() as block:
            @block.tensor
            def _(pe):
                T = nc.tensor
                for i in range(IC):
                    last = T.matmul(pa[:, i:i + 1], k["weight_sum"][:, i * P:(i + 1) * P], ones[:, 0:1],
                                    start=True, stop=True)
                last.then_inc(pe_done, 1)
                T.matmul(pb[0:1, :], ones[:, 0:1], k["weight_sum"][:], start=True, stop=True).then_inc(pe_done, 1)
                pe.wait_ge(v_done, 7)
                for f in range(FC):
                    if f:
                        pe.wait_ge(v_done, 7 + f)
                    for i in range(IC):
                        last = T.transpose(pc[:, i * P:(i + 1) * P], token_sum[:, i, f * P:(f + 1) * P], ident[:])
                    last.then_inc(pe_done, 1)
                pe.wait_ge(v_done, 7 + FC)
                for h in range(H):
                    part = slice(h * C, (h + 1) * C)
                    for f in range(FC):
                        T.matmul(pa[0:C, part], k["wfx_sb"][:, f, part], sumsT[:, f, part], start=(f == 0), stop=False)
                    last = T.matmul(pa[0:C, part], k["bfx_sb"][:, part], ratio_row[:, part], start=False, stop=True)
                last.then_inc(pe_done, 1)
                pe.wait_ge(v_done, 8 + FC)
                T.matmul(pb[0:C, :], k["wqkv_sb"][:, 0, :], tokT[:], start=True, stop=True).then_inc(pe_done, 1)
                T.matmul(pc[0:C, :], k["wqkv_sb"][:, 1, :], tokT[:], start=True, stop=True).then_inc(pe_done, 1)
                for h in range(H):
                    last = T.matmul(head(pa[0:C, :], h), head(tokT, h), k["wqkv_sb"][:, 2, :], start=True, stop=True)
                last.then_inc(pe_done, 1)
                pe.wait_ge(v_done, 11 + FC)
                for h in range(H):
                    last = T.matmul(head(pb[0:C, :], h), head(qT, h), head(kT, h), start=True, stop=True)
                last.then_inc(pe_done, 1)
                pe.wait_ge(v_done, 16 + FC)
                for h in range(H):
                    last = T.transpose(head(pc[0:C, :], h), head(score, h), ident[0:C, 0:C])
                last.then_inc(pe_done, 1)
                pe.wait_ge(v_done, 17 + FC)
                for h in range(H):
                    last = T.matmul(head(pa[0:C, :], h), head(v, h), head(attnT, h), start=True, stop=True)
                last.then_inc(pe_done, 1)
                pe.wait_ge(v_done, 18 + FC)
                for i in range(IC):
                    if i:
                        pe.wait_ge(v_done, 18 + FC + 2 * i)
                    for j in range(2):
                        h = 2 * i + j
                        last = T.matmul(pb[j * C:(j + 1) * C, 0:D], head(oT, h), k["wout_sb"][:, h, :],
                                        start=True, stop=True)
                    last.then_inc(pe_done, 1)

            @block.vector
            def _(dve):
                V = nc.vector
                ch = Chain(dve, v_done)
                dve.wait_ge(pe_done, 2)
                ch.mark(V.tensor_copy(norm_row[:], pb[0:1, :]))
                ch.link(V.tensor_scalar(norm[:], pa[:, 0:IC], EPS, None, ALU.add))
                ch.mark(V.reciprocal(rnorm[:], norm[:]))
                ch.link(V.tensor_scalar(ratio_row[:], norm_row[:], EPS, None, ALU.add))
                ch.link(V.reciprocal(ratio_row[:], ratio_row[:]))
                ch.link(V.tensor_tensor(ratio_row[:], ratio_row[:], norm_row[:], ALU.mult))
                ch.link(V.tensor_tensor(token_sum[:], token_sum[:], rnorm[:].unsqueeze(2).to_broadcast([P, IC, D]), ALU.mult))
                for f in range(FC):
                    dve.wait_ge(pe_done, 3 + f)
                    ch.link(V.tensor_copy(sumsT[:, f, :], pc[:]))
                dve.wait_ge(pe_done, 3 + FC)
                ch.link(V.tensor_copy(tokT[:], pa[0:C, :]))
                dve.wait_ge(pe_done, 6 + FC)
                ch.mark(V.tensor_copy(qT[:], pb[0:C, :]))
                ch.mark(V.tensor_copy(kT[:], pc[0:C, :]))
                ch.link(V.tensor_copy(v[:], pa[0:C, :]))
                dve.wait_ge(pe_done, 7 + FC)

                def heads(ap):
                    return ap.rearrange("p (h c) -> p h c", c=C)

                def wide(ap):
                    return ap[:].unsqueeze(2).to_broadcast([C, H, C])
                ch.link(V.tensor_reduce(big[:], heads(pb[0:C, :]), AX.X, ALU.max))
                ch.link(V.tensor_tensor(heads(score[:]), heads(pb[0:C, :]), wide(big), ALU.subtract))
                dve.wait_ge(a_done, 1)
                ch.link(V.tensor_reduce(total[:], heads(score[:]), AX.X, ALU.add))
                ch.link(V.reciprocal(total[:], total[:]))
                ch.link(V.tensor_tensor(heads(score[:]), heads(score[:]), wide(total), ALU.mult))
                dve.wait_ge(pe_done, 8 + FC)
                ch.link(V.tensor_copy(attnT[:], pc[0:C, :]))
                dve.wait_ge(pe_done, 9 + FC)
                ch.link(V.tensor_copy(oT[:], pa[0:C, :]))
                for i in range(IC):
                    dve.wait_ge(pe_done, 10 + FC + i)
                    high, low = (part[:, i, :] for part in k["mix"])
                    ch.link(V.tensor_copy(high, pb[:, 0:D]))
                    ch.link(V.tensor_tensor(low, pb[:, 0:D], high, ALU.subtract))

            @block.scalar
            def _(act):
                act.wait_ge(v_done, 13 + FC)
                nc.scalar.activation(score[:], score[:], ACT.Exp, scale=k["SCALE"]).then_inc(a_done, 1)


def spread_back(nc, k, sb, ps, sem):
    NT, D, IC, INNER, LAST = (k[n] for n in ("NT", "D", "IC", "INNER", "LAST"))
    PAIR, B, U = 2, 4, 8
    NG = -(-NT // PAIR)
    m_last = NT - (NG - 1) * PAIR
    with Phase(nc) as c:
        w = sb("o_w", [P, B, PAIR, INNER], c=c)
        x2 = sb("o_x2", [P, B, PAIR, D], c=c)
        wT = [sb(f"o_wT_{part}", [P, 4, INNER], FP32R, c) for part in ("high", "low")]
        xb = sb("o_xb", [P, 4, D], c=c)
        o = sb("o_o", [P, B, PAIR, D], c=c)
        ps_T = [ps(f"o_psT{i}", [P, INNER], c=c) for i in range(4)]
        ps_o = [ps(f"o_ps{i}", [P, D], c=c) for i in range(4)]
        w_in = [sem(f"o_w_in{i}", c) for i in range(B)]
        x_in = [sem(f"o_x_in{i}", c) for i in range(B)]
        o_out = [sem(f"o_out{i}", c) for i in range(B)]
        turned = sem("o_turned", c)
        copied = sem("o_copied", c)
        rest_copied = sem("o_rest_copied", c)
        mixed = sem("o_mixed", c)
        biased = sem("o_biased", c)
        o_done = sem("o_done", c)

        def tiles(g):
            return PAIR if g.g is not None or g.at < NG - 1 else NT - (NG - 1) * PAIR

        def pair(ap, n, count):
            return ap[bass.ds(n * P, count * P), :].rearrange("(j p) n -> p j n", p=P)

        def place(t):
            return t.slot(U) // PAIR, t.slot(PAIR), t.uses(U)
        with nc.Block() as block:
            @block.sync
            def _(sp):
                def load(g):
                    b, m = g.slot(B), tiles(g)
                    if g.reused(B):
                        sp.wait_ge(turned, g.plus(1 - B).n * PAIR)
                        sp.wait_ge(biased, g.plus(1 - B).n * PAIR)
                    sp.dma_start(w[:, b, 0:m, :], pair(k["w_dram"], g.n * PAIR, m)).then_inc(w_in[b], 16)
                    sp.dma_start(x2[:, b, 0:m, :], pair(k["x2_dram"], g.n * PAIR, m)).then_inc(x_in[b], 16)

                def store(g):
                    b, m = g.slot(B), tiles(g)
                    if g.g is not None or g.at < NG - 1:
                        sp.wait_ge(o_done, (g.n + 1) * PAIR)
                        sp.dma_start(pair(k["out"], g.n * PAIR, m), o[:, b, 0:m, :]).then_inc(o_out[b], 16)
                    else:
                        sp.wait_ge(o_done, NT)
                        for j in range(m):
                            n, r0 = (LAST if j == m - 1 else P), (g.at * PAIR + j) * P
                            sp.dma_start(k["out"][r0:r0 + n, :], o[0:n, b, j, :]).then_inc(o_out[b], 16)
                for g in steps(sp, 1 - B, NG, B, end=NG, ahead=B - 1):
                    at(g, B - 1, load)
                    at(g, 0, store)
                for b in range(B):
                    stores = -(-(NG - b) // B) + (m_last - 1 if (NG - 1) % B == b else 0)
                    sp.wait_ge(o_out[b], 16 * stores)

            @block.tensor
            def _(pe):
                def turn(t):
                    b, (q, j, uses) = t.slot(4), place(t)
                    pe.wait_ge(w_in[q], uses * 16 + 16)
                    if t.reused(4):
                        pe.wait_ge(rest_copied, t.plus(-3).n)
                    for i in range(IC):
                        part = slice(i * P, (i + 1) * P)
                        last = nc.tensor.transpose(ps_T[b][:, part], w[:, q, j, part], k["ident"][:])
                    last.then_inc(turned, 1)

                def mixing(t):
                    q = t.slot(4)
                    pe.wait_ge(rest_copied, t.n + 1)
                    if t.reused(4):
                        pe.wait_ge(o_done, t.plus(-3).n)
                    for i in range(IC):
                        last = split_product(nc, ps_o[q][:], [part[:, q, i * P:(i + 1) * P] for part in wT],
                                             [part[:, i, :] for part in k["mix"]], i == 0, i == IC - 1)
                    last.then_inc(mixed, 1)
                for t in steps(pe, -2, NT, U, end=NT, ahead=2, buffers=U):
                    at(t, 2, turn)
                    at(t, 0, mixing)

            @block.scalar
            def _(act):
                def copy(t):
                    q = t.slot(4)
                    act.wait_ge(turned, t.n + 1)
                    if t.reused(4):
                        act.wait_ge(mixed, t.plus(-3).n)
                    nc.scalar.activation(wT[0][:, q, :], ps_T[q][:], ACT.Copy).then_inc(copied, 1)

                for t in steps(act, 0, NT, U, buffers=U):
                    copy(t)

            @block.vector
            def _(dve):
                def rest(t):
                    q = t.slot(4)
                    dve.wait_ge(copied, t.n + 1)
                    if t.reused(4):
                        dve.wait_ge(mixed, t.plus(-3).n)
                    nc.vector.tensor_tensor(wT[1][:, q, :], ps_T[q][:], wT[0][:, q, :],
                                            ALU.subtract).then_inc(rest_copied, 1)

                def bias(t):
                    q, j, uses = place(t)
                    dve.wait_ge(x_in[q], uses * 16 + 16)
                    if t.reused(4):
                        dve.wait_ge(o_done, t.plus(-3).n)
                    nc.vector.tensor_tensor(xb[:, t.slot(4), :], x2[:, q, j, :], k["bout_sb"][:],
                                            ALU.add).then_inc(biased, 1)

                def add(t):
                    q, j, uses = place(t)
                    dve.wait_ge(mixed, t.n + 1)
                    dve.wait_ge(biased, t.n + 1)
                    if t.reused(U):
                        dve.wait_ge(o_out[q], uses * 16)
                    nc.vector.tensor_tensor(o[:, q, j, :], ps_o[t.slot(4)][:], xb[:, t.slot(4), :],
                                            ALU.add).then_inc(o_done, 1)
                for t in steps(dve, -2, NT, U, end=NT, ahead=2, buffers=U):
                    at(t, 2, rest)
                    at(t, 1, bias)
                    at(t, 0, add)


_INS = ["x", "src", "dst", "L0_gnn_W0", "L0_gnn_b0", "L0_gnn_W1", "L0_gnn_b1", "L0_gnn_W2", "L0_gnn_b2",
        "L0_ffn_W_fx", "L0_ffn_b_fx", "L0_ffn_W_x", "L0_ffn_b_x", "L0_ffn_W_slice", "L0_ffn_b_slice",
        "L0_ffn_W_q", "L0_ffn_W_k", "L0_ffn_W_v", "L0_ffn_W_out", "L0_ffn_b_out", "L0_ffn_temperature"]


def _program(nc, shapes):
    a = {n: nc.dram_tensor(f"in_{n}", s, d, kind="ExternalInput").ap() for n, (s, d) in shapes.items()}
    out = nc.dram_tensor("out_0", shapes["x"][0], FP32, kind="ExternalOutput").ap()
    f = lambda n: a["L0_ffn_" + n]
    gnn_ffn(nc, a["x"], a["src"], a["dst"], [a[f"L0_gnn_W{l}"] for l in range(3)],
            [a[f"L0_gnn_b{l}"] for l in range(3)], f("W_fx"), f("b_fx"), f("W_x"), f("b_x"), f("W_slice"),
            f("b_slice"), f("W_q"), f("W_k"), f("W_v"), f("W_out"), f("b_out"), f("temperature"), out)


def kernel(**inputs):
    import numpy as _np
    import concourse.bacc as _bacc
    from concourse import mybir as _mybir
    from concourse.bass_utils import run_bass_kernel_spmd as _run

    nc = _bacc.Bacc("TRN2", target_bir_lowering=False, num_devices=1)
    arrays = {n: _np.ascontiguousarray(inputs[n]) for n in _INS}
    _program(nc, {n: (v.shape, _mybir.dt.from_np(v.dtype)) for n, v in arrays.items()})
    r = _run(nc, [{f"in_{n}": v for n, v in arrays.items()}], core_ids=[0])
    return r.results[0]["out_0"]
```
